# Optimizing a Trainium2 kernel written in Bass

```python
import numpy as np
import jax
import jax.numpy as jnp

def _softmax(x, axis=-1):
    return jax.nn.softmax(x, axis=axis)

def _gelu(x):
    return jax.nn.gelu(x, approximate=True)

def _silu(x):
    return jax.nn.silu(x)

def _sigmoid(x):
    return jax.nn.sigmoid(x)

def _layernorm(x, axis=-1, eps=1e-05):
    m = jnp.mean(x, axis=axis, keepdims=True)
    v = jnp.var(x, axis=axis, keepdims=True)
    return (x - m) / jnp.sqrt(v + eps)

def _scatter_add(tgt, idx, src, axis=0):
    return tgt.at[idx].add(src)

def _segment_sum(src, seg, n):
    return jax.ops.segment_sum(src, seg, n)
kernel_name = 'mk_decoder_postln_d1_seqx_r8_b430a5'

def setup_inputs(seed: int=0):
    np.random.seed(seed)
    _w = jnp.asarray

    def _rec_inputs():
        import jax
        import jax.numpy as jnp
        _rk = jax.random.key(seed)
        x = -0.0003929 + 0.9999 * jax.random.normal(jax.random.fold_in(_rk, 1), (16, 64, 512), jnp.float32)
        _lenS = 64 - jax.random.randint(jax.random.fold_in(_rk, 7), (16,), 0, max(1, 64 // 4) + 1, jnp.int32)
        _lenS2 = 64 - jax.random.randint(jax.random.fold_in(_rk, 8), (16,), 0, max(1, 64 // 4) + 1, jnp.int32)
        _ctx_4096P = jax.random.normal(jax.random.fold_in(_rk, 11), (16, 16, 512), jnp.float32)
        _ctx_4096c = jax.random.dirichlet(jax.random.fold_in(_rk, 511), 0.3 * jnp.ones((16,), jnp.float32), (16, 64))
        _ctx_4096t = jnp.einsum('bsk,bkd->bsd', _ctx_4096c, _ctx_4096P)
        _ctx_4096t = _ctx_4096t * jax.lax.rsqrt(jnp.mean(jnp.square(_ctx_4096t)) + 1e-12) * 0.953939
        ctx_4096 = 2.81802e-05 + 1.00001 * (_ctx_4096t + 0.3 * jax.random.normal(jax.random.fold_in(_rk, 611), (16, 64, 512), jnp.float32))
        return (x, ctx_4096)
    x, ctx_4096 = _rec_inputs()

    def _L0_attn_setup():
        import jax, jax.numpy as jnp
        import numpy as np
        import math
        B, S, H = (1, 256, 512)
        NH, NKV, HD = (32, 8, 128)
        GS = 128
        WBITS = 4
        ZERO = float(2 ** (WBITS - 1))
        THETA = 10000.0

        def _dequant_matmul(x, qw, scales):
            w = (qw.astype(jnp.float32) - ZERO) * jnp.repeat(scales, GS, axis=0)
            return x @ w

        def _rope_tables(seq_len, dtype):
            inv_freq = 1.0 / THETA ** (jnp.arange(0, HD, 2, dtype=jnp.float32) / HD)
            freqs = jnp.arange(seq_len, dtype=jnp.float32)[:, None] * inv_freq
            emb = jnp.concatenate([freqs, freqs], axis=-1)
            return (jnp.cos(emb).astype(dtype), jnp.sin(emb).astype(dtype))

        def _rotate_half(x):
            x1, x2 = jnp.split(x, 2, axis=-1)
            return jnp.concatenate([-x2, x1], axis=-1)

        def _apply_rope(x, cos, sin):
            return x * cos[None, None] + _rotate_half(x) * sin[None, None]
        key = jax.random.key(seed)
        ks = jax.random.split(key, 9)
        small = lambda k, shp: jax.random.uniform(k, shp, jnp.float32) * 0.01 + 0.001
        return {'hidden_states': jax.random.normal(ks[0], (B, S, H), jnp.float32), 'scales_q': small(ks[1], (H // GS, NH * HD)), 'scales_k': small(ks[2], (H // GS, NKV * HD)), 'scales_v': small(ks[3], (H // GS, NKV * HD)), 'scales_o': small(ks[4], (NH * HD // GS, H)), 'qw_q': jax.random.randint(ks[5], (H, NH * HD), 0, 2 ** WBITS, jnp.int32), 'qw_k': jax.random.randint(ks[6], (H, NKV * HD), 0, 2 ** WBITS, jnp.int32), 'qw_v': jax.random.randint(ks[7], (H, NKV * HD), 0, 2 ** WBITS, jnp.int32), 'qw_o': jax.random.randint(ks[8], (NH * HD, H), 0, 2 ** WBITS, jnp.int32)}
    _L0_attn_all = _L0_attn_setup()
    _L0_attn_in = {k: v for k, v in _L0_attn_all.items() if k in ('scales_q', 'scales_k', 'scales_v', 'scales_o', 'qw_q', 'qw_k', 'qw_v', 'qw_o')}
    del _L0_attn_all

    def _L0_xattn_setup():
        import jax, jax.numpy as jnp
        import numpy as np
        DIM = 64
        HEADS = 8
        DIM_HEAD = 64
        HIDDEN = HEADS * DIM_HEAD
        SCALE = DIM_HEAD ** (-0.5)
        key = jax.random.key(seed)
        ks = jax.random.split(key, 9)
        b, n = (8, 512)
        std = 1.0 / np.sqrt(DIM)
        return {'q': jax.random.normal(ks[0], (b, DIM, n), jnp.float32), 'k': jax.random.normal(ks[1], (b, DIM, n), jnp.float32), 'v': jax.random.normal(ks[2], (b, DIM, n), jnp.float32), 'Wq': jax.random.normal(ks[3], (HIDDEN, DIM), jnp.float32) * std, 'Wk': jax.random.normal(ks[4], (HIDDEN, DIM), jnp.float32) * std, 'Wv': jax.random.normal(ks[5], (HIDDEN, DIM), jnp.float32) * std, 'Wo': jax.random.normal(ks[6], (DIM, HIDDEN), jnp.float32) * (1.0 / np.sqrt(HIDDEN)), 'bo': jax.random.normal(ks[7], (DIM,), jnp.float32) * 0.01, 'g': jnp.ones((1, DIM, 1), jnp.float32)}
    _L0_xattn_all = _L0_xattn_setup()
    _L0_xattn_in = {k: v for k, v in _L0_xattn_all.items() if k in ('Wq', 'Wk', 'Wv', 'Wo', 'bo', 'g')}
    del _L0_xattn_all

    def _L0_ffn_setup():
        import jax, jax.numpy as jnp
        import numpy as np
        THRESH_FACTOR = 0.7

        def _bitlinear(x, w, scale):
            w_abs = jnp.abs(w)
            thr = jnp.mean(w_abs) * THRESH_FACTOR
            wq = jnp.sign(w) * (w_abs > thr).astype(w.dtype)
            w_scaled = wq * scale
            return jnp.einsum('bsd,od->bso', x, w_scaled)
        key = jax.random.key(seed)
        k1, k2, k3, k4 = jax.random.split(key, 4)
        dim, hidden = (512, 2048)
        x = jax.random.normal(k1, (2, 256, dim), dtype=jnp.float32)
        gate_w = jax.random.normal(k2, (hidden, dim), dtype=jnp.float32) / np.sqrt(dim)
        up_w = jax.random.normal(k3, (hidden, dim), dtype=jnp.float32) / np.sqrt(dim)
        down_w = jax.random.normal(k4, (dim, hidden), dtype=jnp.float32) / np.sqrt(hidden)
        return {'x': x, 'gate_w': gate_w, 'gate_scale': jnp.ones((hidden, 1), jnp.float32), 'up_w': up_w, 'up_scale': jnp.ones((hidden, 1), jnp.float32), 'down_w': down_w, 'down_scale': jnp.ones((dim, 1), jnp.float32)}
    _L0_ffn_all = _L0_ffn_setup()
    _L0_ffn_in = {k: v for k, v in _L0_ffn_all.items() if k in ('gate_w', 'gate_scale', 'up_w', 'up_scale', 'down_w', 'down_scale')}
    del _L0_ffn_all
    return {'x': x, 'ctx_4096': ctx_4096, 'L0_attn_scales_q': _L0_attn_in['scales_q'], 'L0_attn_scales_k': _L0_attn_in['scales_k'], 'L0_attn_scales_v': _L0_attn_in['scales_v'], 'L0_attn_scales_o': _L0_attn_in['scales_o'], 'L0_attn_qw_q': _L0_attn_in['qw_q'], 'L0_attn_qw_k': _L0_attn_in['qw_k'], 'L0_attn_qw_v': _L0_attn_in['qw_v'], 'L0_attn_qw_o': _L0_attn_in['qw_o'], 'L0_xattn_Wq': _L0_xattn_in['Wq'], 'L0_xattn_Wk': _L0_xattn_in['Wk'], 'L0_xattn_Wv': _L0_xattn_in['Wv'], 'L0_xattn_Wo': _L0_xattn_in['Wo'], 'L0_xattn_bo': _L0_xattn_in['bo'], 'L0_xattn_g': _L0_xattn_in['g'], 'L0_ffn_gate_w': _L0_ffn_in['gate_w'], 'L0_ffn_gate_scale': _L0_ffn_in['gate_scale'], 'L0_ffn_up_w': _L0_ffn_in['up_w'], 'L0_ffn_up_scale': _L0_ffn_in['up_scale'], 'L0_ffn_down_w': _L0_ffn_in['down_w'], 'L0_ffn_down_scale': _L0_ffn_in['down_scale']}

def reference(x, ctx_4096, L0_attn_scales_q, L0_attn_scales_k, L0_attn_scales_v, L0_attn_scales_o, L0_attn_qw_q, L0_attn_qw_k, L0_attn_qw_v, L0_attn_qw_o, L0_xattn_Wq, L0_xattn_Wk, L0_xattn_Wv, L0_xattn_Wo, L0_xattn_bo, L0_xattn_g, L0_ffn_gate_w, L0_ffn_gate_scale, L0_ffn_up_w, L0_ffn_up_scale, L0_ffn_down_w, L0_ffn_down_scale):
    import jax
    import jax.numpy as jnp

    def _L0_attn_ref(hidden_states, scales_q, scales_k, scales_v, scales_o, qw_q, qw_k, qw_v, qw_o):
        import jax, jax.numpy as jnp
        import numpy as np
        import math
        B, S, H = (1, 256, 512)
        NH, NKV, HD = (32, 8, 128)
        GS = 128
        WBITS = 4
        ZERO = float(2 ** (WBITS - 1))
        THETA = 10000.0

        def _dequant_matmul(x, qw, scales):
            w = (qw.astype(jnp.float32) - ZERO) * jnp.repeat(scales, GS, axis=0)
            return x @ w

        def _rope_tables(seq_len, dtype):
            inv_freq = 1.0 / THETA ** (jnp.arange(0, HD, 2, dtype=jnp.float32) / HD)
            freqs = jnp.arange(seq_len, dtype=jnp.float32)[:, None] * inv_freq
            emb = jnp.concatenate([freqs, freqs], axis=-1)
            return (jnp.cos(emb).astype(dtype), jnp.sin(emb).astype(dtype))

        def _rotate_half(x):
            x1, x2 = jnp.split(x, 2, axis=-1)
            return jnp.concatenate([-x2, x1], axis=-1)

        def _apply_rope(x, cos, sin):
            return x * cos[None, None] + _rotate_half(x) * sin[None, None]
        b, s, _ = hidden_states.shape
        q = _dequant_matmul(hidden_states, qw_q, scales_q).reshape(b, s, NH, HD).transpose(0, 2, 1, 3)
        k = _dequant_matmul(hidden_states, qw_k, scales_k).reshape(b, s, NKV, HD).transpose(0, 2, 1, 3)
        v = _dequant_matmul(hidden_states, qw_v, scales_v).reshape(b, s, NKV, HD).transpose(0, 2, 1, 3)
        cos, sin = _rope_tables(s, hidden_states.dtype)
        q = _apply_rope(q, cos, sin)
        k = _apply_rope(k, cos, sin)
        rep = NH // NKV
        k = jnp.repeat(k, rep, axis=1)
        v = jnp.repeat(v, rep, axis=1)
        scores = jnp.einsum('bhqd,bhkd->bhqk', q, k) / math.sqrt(HD)
        causal = jnp.tril(jnp.ones((s, s), dtype=bool))
        scores = jnp.where(causal[None, None], scores, jnp.finfo(scores.dtype).min)
        attn = jax.nn.softmax(scores.astype(jnp.float32), axis=-1).astype(q.dtype)
        ctx = jnp.einsum('bhqk,bhkd->bhqd', attn, v)
        ctx = ctx.transpose(0, 2, 1, 3).reshape(b, s, NH * HD)
        return _dequant_matmul(ctx, qw_o, scales_o)

    def _L0_xattn_ref(q, k, v, Wq, Wk, Wv, Wo, bo, g):
        import jax, jax.numpy as jnp
        import numpy as np
        DIM = 64
        HEADS = 8
        DIM_HEAD = 64
        HIDDEN = HEADS * DIM_HEAD
        SCALE = DIM_HEAD ** (-0.5)
        b = q.shape[0]
        qh = jnp.einsum('bcn,oc->bon', q, Wq).reshape(b, HEADS, DIM_HEAD, -1)
        kh = jnp.einsum('bcn,oc->bon', k, Wk).reshape(b, HEADS, DIM_HEAD, -1)
        vh = jnp.einsum('bcn,oc->bon', v, Wv).reshape(b, HEADS, DIM_HEAD, -1)
        qh = jax.nn.softmax(qh, axis=-2) * SCALE
        kh = jax.nn.softmax(kh, axis=-1)
        context = jnp.einsum('bhdn,bhen->bhde', kh, vh)
        out = jnp.einsum('bhde,bhdn->bhen', context, qh)
        out = out.reshape(b, HIDDEN, -1)
        out = jnp.einsum('bcn,oc->bon', out, Wo) + bo[None, :, None]
        norm = jnp.maximum(jnp.sqrt(jnp.sum(out * out, axis=1, keepdims=True)), 1e-12)
        return out / norm * g * np.sqrt(DIM)

    def _L0_ffn_ref(x, gate_w, gate_scale, up_w, up_scale, down_w, down_scale):
        import jax, jax.numpy as jnp
        import numpy as np
        THRESH_FACTOR = 0.7

        def _bitlinear(x, w, scale):
            w_abs = jnp.abs(w)
            thr = jnp.mean(w_abs) * THRESH_FACTOR
            wq = jnp.sign(w) * (w_abs > thr).astype(w.dtype)
            w_scaled = wq * scale
            return jnp.einsum('bsd,od->bso', x, w_scaled)
        gate = _bitlinear(x, gate_w, gate_scale)
        up = _bitlinear(x, up_w, up_scale)
        hidden = jax.nn.silu(gate) * up
        out = _bitlinear(hidden, down_w, down_scale)
        return out
    x = _layernorm(x + _L0_attn_ref(x, L0_attn_scales_q, L0_attn_scales_k, L0_attn_scales_v, L0_attn_scales_o, L0_attn_qw_q, L0_attn_qw_k, L0_attn_qw_v, L0_attn_qw_o), axis=-1)
    x = _layernorm(x + _L0_xattn_ref(x, ctx_4096, ctx_4096, L0_xattn_Wq, L0_xattn_Wk, L0_xattn_Wv, L0_xattn_Wo, L0_xattn_bo, L0_xattn_g), axis=-1)
    x = _layernorm(x + _L0_ffn_ref(x, L0_ffn_gate_w, L0_ffn_gate_scale, L0_ffn_up_w, L0_ffn_up_scale, L0_ffn_down_w, L0_ffn_down_scale), axis=-1)
    return x

_drawn_inputs = setup_inputs


def setup_inputs(seed=0):
    import zlib

    import numpy as np

    out = dict(_drawn_inputs(seed))
    spreads = {'L0_xattn_g': (1.0, 0.2),
     'L0_ffn_gate_scale': (1.0, 0.2),
     'L0_ffn_up_scale': (1.0, 0.2),
     'L0_ffn_down_scale': (1.0, 0.2)}
    factors = {}
    for name, (base, spread) in spreads.items():
        noise = np.random.default_rng([zlib.crc32(name.encode()), seed]).standard_normal(out[name].shape)
        drawn = base * np.exp(spread * noise) if base else spread * noise
        out[name] = jnp.asarray(drawn.astype(out[name].dtype))
    for name, factor in factors.items():
        out[name] = (out[name] * factor).astype(out[name].dtype)
    return out
```

```python
from contextlib import ExitStack

import numpy as np
import concourse.bass as bass
from concourse import mybir

F32, F16, BF16, I32 = mybir.dt.float32, mybir.dt.float16, mybir.dt.bfloat16, mybir.dt.int32
ALU = mybir.AluOpType
ACT = mybir.ActivationFunctionType
AX = mybir.AxisListType
RMAX = bass.bass_isa.ReduceOp.absmax
RADD = bass.bass_isa.ReduceOp.add

P = 128
B, S, D = 16, 64, 512
TOK = B * S
TILES = TOK // P
KT = D // P
HD = 128
HEADS, KV = 32, 8
GROUPS = KV
GH = HEADS // KV
QC = GH * HD
QK = QC + HD
PC = QC + 2 * HD
WC = PC + D
STEPS = TILES * GROUPS
XH, XD = 8, 64
HID = 2048
HT = HID // P
FC = HID // D
EXP_BITS = 0x7F800000
TINY = 1e-30
EPS = 1e-5


def reached(eng, sem, count):
    if not isinstance(count, int) or count > 0:
        eng.wait_ge(sem, count)


def live(n, lag, steps):
    return not isinstance(n, int) or 0 <= n - lag < steps


def setup_block(nc, ins, keep):
    x_rows, scales = ins["x_rows"], ins["scales"]
    fac, sc_parts = keep["fac"], keep["sc_parts"]
    with ExitStack() as ctx:
        sb = lambda name, shape, dt: ctx.enter_context(nc.sbuf_tensor(name, shape, dt))
        sem = lambda name: ctx.enter_context(nc.semaphore(name))
        x_all = sb("x_all", [P, TILES * D], F32)
        sc = sb("sc", [P, WC], F32)
        peak = sb("peak", [P, 5], F32)
        gpeak = sb("gpeak", [P, 5], F32)
        x_in, sc_in, const_in = sem("x_in"), sem("sc_in"), sem("const_in")
        cleared, peaked, all_peaked, step_done = sem("cleared"), sem("peaked"), sem("all_peaked"), sem("step_done")
        blocks = [(0, QC), (QC, QK), (QK, PC), (PC, WC)]
        block = ctx.enter_context(nc.Block())

        @block.sync
        def _(sp):
            sp.dma_start(x_all[:].rearrange("p (t d) -> p t d", t=TILES),
                         x_rows.rearrange("(t p) d -> p t d", p=P)).then_inc(x_in, 16)
            sp.wait_ge(cleared, 1)
            sp.dma_start(sc[0:GROUPS * KT, :], scales).then_inc(sc_in, 16)
            sp.dma_start(keep["cos"][:], ins["cos"]).then_inc(const_in, 16)
            sp.dma_start(keep["sin"][:], ins["sin"]).then_inc(const_in, 16)
            sp.dma_start(keep["mask"][:], ins["mask"]).then_inc(const_in, 16)
            sp.dma_start(keep["ident"][:], ins["ident"]).then_inc(const_in, 16)
            sp.wait_ge(const_in, 64)

        @block.gpsimd
        def _(pool):
            pool.wait_ge(peaked, 1)
            nc.gpsimd.partition_all_reduce(gpeak[:], peak[:], P, RMAX).then_inc(all_peaked, 1)

        @block.vector
        def _(dve):
            done = [0]

            def chain(ins_):
                done[0] += 1
                ins_.then_inc(step_done, 1)
                dve.wait_ge(step_done, done[0])

            nc.vector.memset(sc[:], 0.0).then_inc(cleared, 1)
            dve.wait_ge(sc_in, 16)
            for k, (a, b) in enumerate(blocks):
                chain(nc.vector.tensor_reduce(peak[:, k:k + 1], sc[:, a:b], AX.X, ALU.max, apply_absolute_value=True))
            dve.wait_ge(x_in, 16)
            chain(nc.vector.tensor_reduce(peak[:, 4:5], x_all[:], AX.X, ALU.max, apply_absolute_value=True))
            nc.vector.tensor_scalar(peak[:], peak[:], TINY, None, ALU.max).then_inc(peaked, 1)
            dve.wait_ge(all_peaked, 1)
            chain(nc.vector.tensor_scalar(fac[:, 0:5].bitcast(I32), gpeak[:].bitcast(I32), EXP_BITS, None,
                                          ALU.bitwise_and))
            chain(nc.vector.reciprocal(fac[:, 5:10], fac[:, 0:5]))
            chain(nc.vector.tensor_tensor(fac[:, 10:11], fac[:, 0:1], fac[:, 1:2], ALU.mult))
            chain(nc.vector.tensor_tensor(fac[:, 10:11], fac[:, 10:11], fac[:, 4:5], ALU.mult))
            chain(nc.vector.tensor_tensor(fac[:, 10:11], fac[:, 10:11], fac[:, 4:5], ALU.mult))
            chain(nc.vector.tensor_scalar(fac[:, 10:11], fac[:, 10:11], float(HD) ** -0.5, None, ALU.mult))
            chain(nc.vector.tensor_tensor(fac[:, 11:12], fac[:, 2:3], fac[:, 3:4], ALU.mult))
            chain(nc.vector.tensor_tensor(fac[:, 11:12], fac[:, 11:12], fac[:, 4:5], ALU.mult))
            for k, (a, b) in enumerate(blocks):
                chain(nc.vector.tensor_scalar(sc[:, a:b], sc[:, a:b], fac[:, 5 + k:6 + k], None, ALU.mult))
            for k in range(3):
                chain(nc.vector.tensor_copy(sc_parts[:, k, :], sc[:]))
                if k < 2:
                    chain(nc.vector.tensor_tensor(sc[:], sc[:], sc_parts[:, k, :], ALU.subtract))
            dve.wait_ge(const_in, 64)
            chain(nc.vector.tensor_copy(keep["ident_b"][:], keep["ident"][:]))


def dequant_block(nc, ins, keep):
    w_int = ins["w_int"]
    w_hi, w_lo, sc_parts, ident_b = keep["w_hi"], keep["w_lo"], keep["sc_parts"], keep["ident_b"]
    NI, NW = 4, 2
    with ExitStack() as ctx:
        sb = lambda name, shape, dt: ctx.enter_context(nc.sbuf_tensor(name, shape, dt))
        sem = lambda name: ctx.enter_context(nc.semaphore(name))
        wi = sb("wi", [P, NI, WC], I32)
        w32 = sb("w32", [P, NW, WC], F32)
        scale_ps = [ctx.enter_context(nc.psum_tensor(f"scale_ps{k}", [P, 1536], F32)) for k in range(2)]
        w_in = [sem(f"w_in{k}") for k in range(NI)]
        spread, scaled, hi_done, lo_even, lo_odd = (sem(n) for n in ("spread", "scaled", "hi_done", "lo_even",
                                                                    "lo_odd"))
        block = ctx.enter_context(nc.Block())

        @block.sync
        def _(sp):
            for k in range(NI):
                sp.dma_start(wi[:, k, :], w_int[0, k]).then_inc(w_in[k], 16)
            with sp.Fori(1, GROUPS) as g:
                for k in range(NI):
                    sp.wait_ge(scaled, g * KT - KT + k + 1)
                    sp.dma_start(wi[:, k, :], w_int[g, k]).then_inc(w_in[k], 16)

        @block.tensor
        def _(pe):
            def unit(g, k, first):
                if not first:
                    pe.wait_ge(scaled, g * KT + k - 1)
                pick = ident_b[:, bass.ds(g * KT + k, 1)].to_broadcast([P, P])
                for a in range(0, WC, 512):
                    b = min(a + 512, WC)
                    for part in range(3):
                        last = nc.tensor.matmul(scale_ps[k % 2][:, a:b], pick, sc_parts[:, part, a:b],
                                                start=(part == 0), stop=(part == 2))
                last.then_inc(spread, 1)

            for k in range(KT):
                unit(0, k, k < 2)
            with pe.Fori(1, GROUPS) as g:
                for k in range(KT):
                    unit(g, k, False)

        @block.vector
        def _(dve):
            def unit(g, k, first):
                u = g * KT + k
                dve.wait_ge(w_in[k], g * 16 + 16)
                dve.wait_ge(spread, u + 1)
                if not (first and k < NW):
                    dve.wait_ge(hi_done, u - 1)
                    dve.wait_ge(lo_odd if k % 2 else lo_even, g * 2 + k // 2)
                nc.vector.scalar_tensor_tensor(out=w32[:, k % NW, :], in0=wi[:, k, :], scalar=-8.0,
                                               in1=scale_ps[k % 2][:, 0:WC], op0=ALU.add,
                                               op1=ALU.mult).then_inc(scaled, 1)
                if k % 2:
                    dve.wait_ge(hi_done, u + 1)
                    nc.vector.tensor_tensor(w_lo[:, g, k, :], w32[:, k % NW, :], w_hi[:, g, k, :],
                                            ALU.subtract).then_inc(lo_odd, 1)

            for k in range(KT):
                unit(0, k, True)
            with dve.Fori(1, GROUPS) as g:
                for k in range(KT):
                    unit(g, k, False)
            dve.wait_ge(lo_odd, GROUPS * KT // 2)

        @block.scalar
        def _(act):
            with act.Fori(0, GROUPS) as g:
                for k in range(KT):
                    act.wait_ge(scaled, g * KT + k + 1)
                    nc.scalar.activation(w_hi[:, g, k, :], w32[:, k % NW, :], ACT.Copy).then_inc(hi_done, 1)

        @block.gpsimd
        def _(pool):
            with pool.Fori(0, GROUPS) as g:
                for k in range(0, KT, 2):
                    pool.wait_ge(hi_done, g * KT + k + 1)
                    nc.gpsimd.tensor_tensor(w_lo[:, g, k, :], w32[:, k % NW, :], w_hi[:, g, k, :],
                                            ALU.subtract).then_inc(lo_even, 1)


def attention_block(nc, ins, keep, x1_dram):
    w_hi, w_lo, fac = keep["w_hi"], keep["w_lo"], keep["fac"]
    cos, sin, mask, ident = keep["cos"], keep["sin"], keep["mask"], keep["ident"]
    x_t, x_rows, ffn_w = ins["x_t"], ins["x_rows"], ins["ffn_w"]
    alpha, beta, x_inv = fac[:, 10:11], fac[:, 11:12], fac[:, 9:10]
    NV = 4
    HALF = HD // 2
    SUMS = 6
    with ExitStack() as ctx:
        sb = lambda name, shape, dt: ctx.enter_context(nc.sbuf_tensor(name, shape, dt))
        ps = lambda name, shape, dt: ctx.enter_context(nc.psum_tensor(name, shape, dt))
        sem = lambda name: ctx.enter_context(nc.semaphore(name))
        xt32 = sb("xt32", [P, KT * P], F32)
        xt_hi = sb("xt_hi", [P, KT * P], F16)
        xt_lo = sb("xt_lo", [P, KT * P], F16)
        x_res = sb("x_res", [P, D], F32)
        by_cos = sb("by_cos", [P, QK], F32)
        by_sin = sb("by_sin", [P, QK], F32)
        rot = sb("rot", [P, QK], F32)
        qk_t = sb("qk_t", [P, QK], F32)
        v_two = sb("v_two", [P, NV, 2, HD], F32)
        probs = sb("probs", [P, GH * S], F32)
        probs_t = sb("probs_t", [P, 2, P], F32)
        c_hi = sb("c_hi", [P, 2, GH * P], F16)
        c_lo = sb("c_lo", [P, 2, GH * P], F16)
        neg_max = sb("neg_max", [P, GH], F32)
        psum_row = sb("psum_row", [P, GH], F32)
        rcp = sb("rcp", [P, GH], F32)
        z = sb("z", [P, D], F32)
        y = sb("y", [P, D], F32)
        stats = sb("stats", [P, 6], F32)
        mv = sb("mv", [P, 2], F32)
        veps = sb("veps", [P, 1], F32)
        rstd = sb("rstd", [P, 1], F32)
        neg_half = sb("neg_half", [P, 1], F32)
        ffn_in = sb("ffn_in", [P, 2, D], F32)
        pj = ps("pj", [P, 1024], F32)
        tr = ps("tr", [P, 1024], F32)
        sp_ = ps("scores_ps", [P, 512], F32)
        pv = ps("pv", [P, 2, 512], F32)
        oacc = ps("oacc", [P, 512], F32)

        xt_in, xr_in, ffn_sem = sem("xt_in"), sem("xr_in"), [sem("ffn_in0"), sem("ffn_in1")]
        xt_hi_done, xt_split = sem("xt_hi_done"), sem("xt_split")
        projected, turned, scored, p_turned, weighed, o_done = (sem(s) for s in (
            "projected", "turned", "scored", "p_turned", "weighed", "o_done"))
        roped, masked, maxed, inverted, c_lo_done, residual = (sem(s) for s in (
            "roped", "masked", "maxed", "inverted", "c_lo_done", "residual"))
        rotated, normed, rstd_done = sem("rotated"), sem("normed"), sem("rstd_done")
        v_copied, qk_copied, exped, pt_copied, c_hi_done = (sem(s) for s in (
            "v_copied", "qk_copied", "exped", "pt_copied", "c_hi_done"))
        summed, ln_chain, y_done, stored, half_set = (sem(s) for s in (
            "summed", "ln_chain", "y_done", "stored", "half_set"))
        block = ctx.enter_context(nc.Block())

        def schedule(eng, step):
            for g in range(GROUPS):
                step(0, g, g)
            with eng.Fori(1, TILES - 1) as i:
                for g in range(GROUPS):
                    step(i, g, i * GROUPS + g)
            for g in range(GROUPS):
                step(TILES - 1, g, STEPS - GROUPS + g)
            for g in range(4):
                step(TILES, g, STEPS + g)

        @block.sync
        def _(sp):
            def tile(i, first):
                if not first:
                    sp.wait_ge(xt_split, i)
                sp.dma_start(xt32[:], x_t[i]).then_inc(xt_in, 16)
                for g in range(SUMS):
                    if not (first and g < 2):
                        sp.wait_ge(summed, i * SUMS + g - 1)
                    sp.dma_start(ffn_in[:, g % 2, :], ffn_w[g // 2, i, :, (g % 2) * D:(g % 2 + 1) * D]
                                 ).then_inc(ffn_sem[g % 2], 16)
                if not first:
                    sp.wait_ge(residual, i)
                sp.dma_start(x_res[:], x_rows.rearrange("(t p) d -> t p d", p=P)[i]).then_inc(xr_in, 16)

            tile(0, True)
            with sp.Fori(1, TILES) as i:
                tile(i, False)
                sp.wait_ge(y_done, i)
                sp.dma_start(x1_dram.rearrange("(t p) d -> t p d", p=P)[i - 1], y[:]).then_inc(stored, 16)
            sp.wait_ge(y_done, TILES)
            sp.dma_start(x1_dram.rearrange("(t p) d -> t p d", p=P)[TILES - 1], y[:]).then_inc(stored, 16)
            sp.wait_ge(stored, 16 * TILES)

        @block.tensor
        def _(pe):
            def step(i, g, n):
                if live(n, 1, STEPS):
                    pe.wait_ge(rotated, n)
                    reached(pe, qk_copied, n - 1)
                    for h in range(GH + 1):
                        last = nc.tensor.transpose(tr[:, h * P:(h + 1) * P], rot[:, h * P:(h + 1) * P], ident[:])
                    last.then_inc(turned, 1)
                if live(n, 2, STEPS):
                    pe.wait_ge(normed, n - 1)
                    for c in range(2):
                        last = nc.tensor.transpose(sp_[:, c * P:(c + 1) * P], probs[:, c * P:(c + 1) * P], ident[:])
                    last.then_inc(p_turned, 1)
                if live(n, 0, STEPS):
                    if g == 0:
                        pe.wait_ge(xt_split, i + 1)
                    reached(pe, roped, n)
                    reached(pe, v_copied, n)
                    for k in range(KT):
                        for part, (xs, w) in enumerate(((xt_hi, w_hi), (xt_hi, w_lo), (xt_lo, w_hi))):
                            for a, b in ((0, QC), (QC, PC)):
                                last = nc.tensor.matmul(pj[:, a:b], xs[:, k * P:(k + 1) * P], w[:, g, k, a:b],
                                                        start=(k == 0 and part == 0), stop=(k == KT - 1 and part == 2))
                    last.then_inc(projected, 1)
                if live(n, 1, STEPS):
                    pe.wait_ge(qk_copied, n)
                    reached(pe, pt_copied, n - 1)
                    for h in range(GH):
                        last = nc.tensor.matmul(sp_[:, h * P:(h + 1) * P], qk_t[:, h * P:(h + 1) * P],
                                                qk_t[:, QC:QK], start=True, stop=True)
                    last.then_inc(scored, 1)
                if live(n, 2, STEPS):
                    pe.wait_ge(pt_copied, n - 1)
                    reached(pe, c_lo_done, n - 2)
                    gv = (g - 2) % NV
                    for par in range(2):
                        rows = slice(par * S, par * S + S)
                        for b in range(2):
                            last = nc.tensor.matmul(
                                pv[:, par, 0:2 * P].rearrange("p (c b q) -> p c b q", c=2, b=2)[:, :, b, :],
                                v_two[rows, gv, b, :],
                                probs_t[rows, :, b * S:(b + 1) * S], start=(b == 0), stop=True,
                                skip_group_check=True)
                    last.then_inc(weighed, 1)
                if live(n, 3, STEPS):
                    go = (g - 3) % GROUPS
                    pe.wait_ge(c_lo_done, n - 2)
                    if go == 0:
                        reached(pe, residual, i)
                    for h in range(GH):
                        cols = slice(h * P, (h + 1) * P)
                        for part, (cs, w) in enumerate(((c_hi, w_hi), (c_hi, w_lo), (c_lo, w_hi))):
                            last = nc.tensor.matmul(oacc[:], cs[:, (g - 3) % 2, cols], w[:, go, h, PC:WC],
                                                    start=(go == 0 and h == 0 and part == 0),
                                                    stop=(go == GROUPS - 1 and h == GH - 1 and part == 2))
                    last.then_inc(o_done, 1)

            schedule(pe, step)

        @block.vector
        def _(dve):
            nc.vector.memset(neg_half[:], -0.5).then_inc(half_set, 1)

            def split_x(i):
                dve.wait_ge(xt_hi_done, i + 1)
                nc.vector.scalar_tensor_tensor(out=xt_lo[:], in0=xt32[:], scalar=x_inv, in1=xt_hi[:],
                                               op0=ALU.mult, op1=ALU.subtract).then_inc(xt_split, 1)

            def step(i, g, n):
                if live(n, 0, STEPS):
                    dve.wait_ge(projected, n + 1)
                    reached(dve, rotated, n)
                    heads = GH + 1
                    src = pj[:, 0:QK].rearrange("p (h d) -> p h d", h=heads)
                    out = by_sin[:].rearrange("p (h d) -> p h d", h=heads)
                    nc.vector.tensor_tensor(by_cos[:].rearrange("p (h d) -> p h d", h=heads), src,
                                            cos[:, None, :].to_broadcast([P, heads, HD]), ALU.mult)
                    for a, b in ((0, HALF), (HALF, 0)):
                        last = nc.vector.tensor_tensor(out[:, :, a:a + HALF], src[:, :, b:b + HALF],
                                                       sin[:, None, a:a + HALF].to_broadcast([P, heads, HALF]),
                                                       ALU.mult)
                    last.then_inc(roped, 1)
                if live(n, 1, STEPS):
                    dve.wait_ge(scored, n)
                    reached(dve, p_turned, n - 1)
                    for b in range(2):
                        rows = slice(b * S, (b + 1) * S)
                        last = nc.vector.scalar_tensor_tensor(
                            out=probs[rows, :].rearrange("p (h k) -> p h k", h=GH),
                            in0=sp_[rows, :].rearrange("p (h k) -> p h k", h=GH)[:, :, b * S:(b + 1) * S],
                            scalar=alpha[rows, :], in1=mask[rows, None, :].to_broadcast([S, GH, S]),
                            op0=ALU.mult, op1=ALU.add)
                    last.then_inc(masked, 1)
                    dve.wait_ge(masked, n)
                    reached(dve, exped, n - 1)
                    nc.vector.tensor_reduce(neg_max[:], probs[:].rearrange("p (h k) -> p h k", h=GH), AX.X,
                                            ALU.max, negate=True).then_inc(maxed, 1)
                if live(n, 2, STEPS):
                    dve.wait_ge(c_hi_done, n - 1)
                    reached(dve, o_done, n - 3)
                    nc.vector.tensor_tensor(
                        c_lo[:, g % 2, :].rearrange("p (c r q) -> p r c q", c=2, r=2),
                        pv[:, :, 0:2 * P].rearrange("p r (c q) -> p r c q", c=2),
                        c_hi[:, g % 2, :].rearrange("p (c r q) -> p r c q", c=2, r=2),
                        ALU.subtract).then_inc(c_lo_done, 1)
                if live(n, 1, STEPS):
                    dve.wait_ge(exped, n)
                    reached(dve, normed, n - 1)
                    nc.vector.reciprocal(rcp[:], psum_row[:]).then_inc(inverted, 1)
                if g < SUMS and live(n, 0, STEPS):
                    dve.wait_ge(ffn_sem[g % 2], i * 3 * 16 + (g // 2 + 1) * 16)
                    nc.vector.tensor_reduce(keep["abs_sums"][:, g // 2, bass.ds(i * 2 + g % 2, 1)],
                                            ffn_in[:, g % 2, :], AX.X, ALU.add,
                                            apply_absolute_value=True).then_inc(summed, 1)
                if g == GROUPS - 1 and live(n, 0, STEPS - 1):
                    split_x(i + 1)
                if g == 2 and live(n, GROUPS, STEPS):
                    dve.wait_ge(o_done, i * GROUPS)
                    dve.wait_ge(xr_in, i * 16)
                    reached(dve, y_done, i - 1)
                    nc.vector.scalar_tensor_tensor(out=z[:], in0=oacc[:], scalar=beta, in1=x_res[:],
                                                   op0=ALU.mult, op1=ALU.add).then_inc(residual, 1)
                    dve.wait_ge(residual, i)
                    nc.vector.bn_stats(stats[:], z[:]).then_inc(ln_chain, 1)
                    dve.wait_ge(ln_chain, i * 3 - 2)
                    nc.vector.memset(veps[:], EPS)
                    nc.vector.bn_aggr(mv[:], stats[:]).then_inc(ln_chain, 1)
                    dve.wait_ge(ln_chain, i * 3 - 1)
                    nc.vector.tensor_tensor(veps[:], veps[:], mv[:, 1:2], ALU.add).then_inc(ln_chain, 1)
                if g == 3 and live(n, GROUPS, STEPS):
                    dve.wait_ge(rstd_done, i)
                    reached(dve, stored, (i - 1) * 16)
                    nc.vector.tensor_scalar(y[:], z[:], mv[:, 0:1], rstd[:], ALU.subtract,
                                            ALU.mult).then_inc(y_done, 1)

            split_x(0)
            schedule(dve, step)

        @block.scalar
        def _(act):
            def split_x(i):
                act.wait_ge(xt_in, i * 16 + 16)
                reached(act, projected, i * GROUPS)
                nc.scalar.activation(xt_hi[:], xt32[:], ACT.Copy, scale=x_inv).then_inc(xt_hi_done, 1)

            def step(i, g, n):
                if live(n, 1, STEPS):
                    act.wait_ge(turned, n)
                    reached(act, scored, n - 1)
                    nc.scalar.activation(qk_t[:], tr[:, 0:QK], ACT.Copy).then_inc(qk_copied, 1)
                if live(n, 2, STEPS):
                    act.wait_ge(p_turned, n - 1)
                    reached(act, weighed, n - 2)
                    nc.scalar.activation(probs_t[:].rearrange("p c q -> p (c q)"), sp_[:, 0:2 * P],
                                         ACT.Copy).then_inc(pt_copied, 1)
                if live(n, 0, STEPS):
                    act.wait_ge(roped, n + 1)
                    reached(act, weighed, n - NV + 1)
                    for b in range(2):
                        for half in range(2):
                            last = nc.scalar.activation(v_two[half * S:(half + 1) * S, g % NV, b, :],
                                                        pj[b * S:(b + 1) * S, QK:PC], ACT.Copy)
                    last.then_inc(v_copied, 1)
                if live(n, 2, STEPS):
                    act.wait_ge(weighed, n - 1)
                    reached(act, o_done, n - 3)
                    nc.scalar.activation(
                        c_hi[:, g % 2, :].rearrange("p (c r q) -> p r c q", c=2, r=2),
                        pv[:, :, 0:2 * P].rearrange("p r (c q) -> p r c q", c=2), ACT.Copy).then_inc(c_hi_done, 1)
                if live(n, 1, STEPS):
                    act.wait_ge(maxed, n)
                    reached(act, inverted, n - 1)
                    for h in range(GH):
                        cols = slice(h * S, (h + 1) * S)
                        last = nc.scalar.activation(probs[:, cols], probs[:, cols], ACT.Exp,
                                                    bias=neg_max[:, h:h + 1], accum_out=psum_row[:, h:h + 1])
                    last.then_inc(exped, 1)
                if g == GROUPS - 1 and live(n, 0, STEPS - 1):
                    split_x(i + 1)

            split_x(0)
            schedule(act, step)

        @block.gpsimd
        def _(pool):
            pool.wait_ge(half_set, 1)

            def step(i, g, n):
                if live(n, 0, STEPS):
                    pool.wait_ge(roped, n + 1)
                    reached(pool, turned, n)
                    nc.gpsimd.tensor_tensor(rot[:], by_cos[:], by_sin[:], ALU.add).then_inc(rotated, 1)
                if live(n, 1, STEPS):
                    pool.wait_ge(inverted, n)
                    nc.gpsimd.tensor_tensor(probs[:].rearrange("p (h k) -> p h k", h=GH),
                                            probs[:].rearrange("p (h k) -> p h k", h=GH),
                                            rcp[:, :, None].to_broadcast([P, GH, S]), ALU.mult).then_inc(normed, 1)
                if g == 2 and live(n, GROUPS, STEPS):
                    pool.wait_ge(ln_chain, i * 3)
                    reached(pool, y_done, i - 1)
                    nc.gpsimd.tensor_tensor(rstd[:], veps[:], neg_half[:], ALU.pow).then_inc(rstd_done, 1)

            schedule(pool, step)


def cross_setup_block(nc, ins, keep):
    xf = keep["xfac"]
    with ExitStack() as ctx:
        sb = lambda name, shape, dt: ctx.enter_context(nc.sbuf_tensor(name, shape, dt))
        sem = lambda name: ctx.enter_context(nc.semaphore(name))
        ctx_all = sb("ctx_all", [P, TILES * D], F32)
        wqk = sb("wqk", [P, 2, XH * XD], F32)
        wv = sb("wv", [XD, XH * XD], F32)
        wo = sb("wo", [XD, XH * XD], F32)
        peak = sb("peak2", [P, 3], F32)
        gpeak = sb("gpeak2", [P, 3], F32)
        asum = sb("asum", [P, 3], F32)
        gsum = sb("gsum", [P, 3], F32)
        u_ps = ctx.enter_context(nc.psum_tensor("u_ps", [XD, XH * XD], F32))
        c_in, w_in, small_in, table_in = sem("c_in"), sem("wqk_in"), sem("small_in"), sem("table_in")
        peaked, summed, reduced, step_done, folded = (sem(s) for s in (
            "peaked2", "summed2", "reduced2", "step_done2", "folded"))
        block = ctx.enter_context(nc.Block())

        @block.sync
        def _(sp):
            for half in range(2):
                rows = slice(half * XD, (half + 1) * XD)
                sp.dma_start(wqk[rows, 0, :], ins["wq_t"]).then_inc(w_in, 16)
                sp.dma_start(wqk[rows, 1, :], ins["wk_t"]).then_inc(w_in, 16)
                sp.dma_start(keep["bo"][rows, :], ins["bo"]).then_inc(small_in, 16)
                sp.dma_start(keep["g8"][rows, :], ins["g"]).then_inc(small_in, 16)
            sp.dma_start(wv[:], ins["wv"]).then_inc(small_in, 16)
            sp.dma_start(wo[:], ins["wo"]).then_inc(small_in, 16)
            sp.dma_start(keep["half_of"][:], ins["half_of"]).then_inc(small_in, 16)
            sp.dma_start(ctx_all[:].rearrange("p (t d) -> p t d", t=TILES),
                         ins["c_rows"].rearrange("(t p) d -> p t d", p=P)).then_inc(c_in, 16)
            sp.dma_start(keep["gate_s"][:], ins["gate_s"].to_broadcast([P, HID])).then_inc(table_in, 16)
            sp.dma_start(keep["up_s"][:], ins["up_s"].to_broadcast([P, HID])).then_inc(table_in, 16)
            sp.dma_start(keep["down_s"][:], ins["down_s"].to_broadcast([P, D])).then_inc(table_in, 16)
            sp.wait_ge(table_in, 48)

        @block.tensor
        def _(pe):
            pe.wait_ge(small_in, 7 * 16)
            for h in range(XH):
                cols = slice(h * XD, (h + 1) * XD)
                last = nc.tensor.matmul(u_ps[:, cols], wv[:, cols], wo[:, cols], start=True, stop=True)
            last.then_inc(folded, 1)

        @block.gpsimd
        def _(pool):
            pool.wait_ge(summed, 1)
            nc.gpsimd.partition_all_reduce(gsum[:], asum[:], P, RADD)
            pool.wait_ge(peaked, 1)
            nc.gpsimd.partition_all_reduce(gpeak[:], peak[:], P, RMAX).then_inc(reduced, 1)

        @block.vector
        def _(dve):
            done = [0]

            def chain(ins_):
                done[0] += 1
                ins_.then_inc(step_done, 1)
                dve.wait_ge(step_done, done[0])

            nc.vector.tensor_reduce(asum[:], keep["abs_sums"][:], AX.X, ALU.add).then_inc(summed, 1)
            chain(nc.vector.memset(keep["neg_half"][:], -0.5))
            dve.wait_ge(w_in, 64)
            for k in range(2):
                chain(nc.vector.tensor_reduce(peak[:, k:k + 1], wqk[:, k, :], AX.X, ALU.max,
                                              apply_absolute_value=True))
            dve.wait_ge(c_in, 16)
            chain(nc.vector.tensor_reduce(peak[:, 2:3], ctx_all[:], AX.X, ALU.max, apply_absolute_value=True))
            nc.vector.tensor_scalar(peak[:], peak[:], TINY, None, ALU.max).then_inc(peaked, 1)
            dve.wait_ge(small_in, 7 * 16)
            chain(nc.vector.tensor_scalar(keep["g8"][:], keep["g8"][:], float(XD) ** 0.5, None, ALU.mult))
            dve.wait_ge(folded, 1)
            chain(nc.vector.tensor_scalar(keep["u"][:], u_ps[:], float(XD) ** -0.5, None, ALU.mult))
            dve.wait_ge(reduced, 1)
            chain(nc.vector.tensor_scalar(xf[:, 0:3].bitcast(I32), gpeak[:].bitcast(I32), EXP_BITS, None,
                                          ALU.bitwise_and))
            chain(nc.vector.reciprocal(xf[:, 3:6], xf[:, 0:3]))
            chain(nc.vector.tensor_tensor(xf[:, 6:7], xf[:, 1:2], xf[:, 2:3], ALU.mult))
            for k in range(2):
                chain(nc.vector.tensor_scalar(wqk[:, k, :], wqk[:, k, :], xf[:, 3 + k:4 + k], None, ALU.mult))
                chain(nc.vector.tensor_copy(keep["wqk_hi"][:, k, :], wqk[:, k, :]))
                chain(nc.vector.tensor_tensor(keep["wqk_lo"][:, k, :], wqk[:, k, :], keep["wqk_hi"][:, k, :],
                                              ALU.subtract))
            chain(nc.vector.tensor_scalar(keep["thr"][:, 0:3], gsum[:], 1.0 / (HID * D), 0.7, ALU.mult, ALU.mult))
            chain(nc.vector.tensor_scalar(keep["thr"][:, 3:6], keep["thr"][:, 0:3], -1.0, None, ALU.mult))


def cross_block(nc, ins, keep, x1_dram, x2_dram):
    ident, wqk_hi, wqk_lo, xf, thr = (keep[k] for k in ("ident", "wqk_hi", "wqk_lo", "xfac", "thr"))
    ffn_q, u, half_of = keep["ffn_q"], keep["u"], keep["half_of"]
    wq_scale, k_scale, c_inv = xf[:, 0:1], xf[:, 6:7], xf[:, 5:6]
    NT = D // P
    SLOTS = 2 * NT
    ALL = SLOTS * TILES
    QUANT = 6
    with ExitStack() as ctx:
        sb = lambda name, shape, dt: ctx.enter_context(nc.sbuf_tensor(name, shape, dt))
        ps = lambda name, shape, dt: ctx.enter_context(nc.psum_tensor(name, shape, dt))
        sem = lambda name: ctx.enter_context(nc.semaphore(name))
        x_raw = sb("x_raw", [P, D], F32)
        c_raw = sb("c_raw", [P, D], F32)
        x_res = sb("x_res2", [P, D], F32)
        c_t = sb("c_t", [P, NT * P], F32)
        xs = sb("xs", [P, 2, D], F16)
        cs = sb("cs", [P, 2, D], F16)
        e_k = sb("e_k", [P, 2, D], F32)
        p_q = sb("p_q", [P, 2, D], F32)
        e_t = sb("e_t", [P, 2, NT, D], F32)
        p_t = sb("p_t", [P, 2, NT, D], F32)
        k_neg = sb("k_neg", [P, 1], F32)
        k_bias = sb("k_bias", [P, 1], F32)
        z_k = sb("z_k", [P, 2, NT], F32)
        r_k = sb("r_k", [P, NT], F32)
        q_max = sb("q_max", [P, XH], F32)
        q_sum = sb("q_sum", [P, XH], F32)
        q_rcp = sb("q_rcp", [P, XH], F32)
        g_t = sb("g_t", [XD, XH * XD], F32)
        m_sb = sb("m_sb", [P, NT, XD], F32)
        o_sb = sb("o_sb", [P, D], F32)
        sq = sb("sq", [P, D], F32)
        ss = sb("ss", [P, SLOTS], F32)
        rn = sb("rn", [P, SLOTS], F32)
        half8 = sb("half8", [P, SLOTS], F32)
        rn_wide = sb("rn_wide", [P, NT, P], F32)
        y1 = sb("y1", [P, D], F32)
        z = sb("z2", [P, D], F32)
        y = sb("y2", [P, D], F32)
        stats = sb("stats2", [P, 6], F32)
        mv = sb("mv2", [P, 2], F32)
        veps = sb("veps2", [P, 1], F32)
        rstd = sb("rstd2", [P, 1], F32)
        w_raw = sb("w_raw", [P, 2, D], F32)
        below = sb("below", [P, D], F32)
        kl = ps("kl", [P, D], F32)
        ql = ps("ql", [P, 2, D], F32)
        trk = ps("trk", [P, D], F32)
        trp = ps("trp", [P, D], F32)
        gm = ps("gm", [P, D], F32)
        ob = ps("ob", [P, D], F32)
        nb = ps("nb", [P, D], F32)

        names = ("x_in", "c_in", "xr_in", "ct_in", "x_split", "c_split", "x_hi_done", "c_hi_done",
                 "k_logits", "q_logits", "k_turned", "q_turned", "g_done", "m_done", "o_done", "ss_done", "rb_done",
                 "k_maxed", "k_biased", "q_maxed", "q_shifted", "q_summed", "q_inverted", "m_scaled", "r_k_done",
                 "k_exped", "q_exped", "kt_copied", "qt_copied", "g_copied", "squared", "q_normed", "ss_copied",
                 "rn_done", "attended", "residual", "chain", "rstd_done", "y_done", "stored", "below_done",
                 "quantized", "half8_set", "rn_raw")
        m = {name: sem("x_" + name) for name in names}
        w_sem = [sem("x_w_in0"), sem("x_w_in1")]
        block = ctx.enter_context(nc.Block())
        rows_of = lambda a: a.rearrange("(t p) d -> t p d", p=P)

        def schedule(eng, slot):
            for s in range(SLOTS):
                slot(0, s, s)
            with eng.Fori(1, TILES - 1) as i:
                for s in range(SLOTS):
                    slot(i, s, i * SLOTS + s)
            for s in range(SLOTS):
                slot(TILES - 1, s, ALL - SLOTS + s)
            for s in range(SLOTS):
                slot(TILES, s, ALL + s)

        @block.sync
        def _(sp):
            def rows_in(i):
                reached(sp, m["x_split"], 2 * i)
                sp.dma_start(x_raw[:], rows_of(x1_dram)[i]).then_inc(m["x_in"], 16)
                reached(sp, m["c_split"], 2 * i)
                sp.dma_start(c_raw[:], rows_of(ins["c_rows"])[i]).then_inc(m["c_in"], 16)

            def tile(i, first, last):
                for k in range(QUANT):
                    if not (first and k < 2):
                        sp.wait_ge(m["quantized"], i * QUANT + k - 1)
                    sp.dma_start(w_raw[:, k % 2, :], ins["ffn_w"][k // 2, i, :, (k % 2) * D:(k % 2 + 1) * D]
                                 ).then_inc(w_sem[k % 2], 16)
                    if k == 1:
                        if not last:
                            rows_in(i + 1)
                        reached(sp, m["g_done"], 2 * i)
                        sp.dma_start(c_t[:], ins["c_t"][i]).then_inc(m["ct_in"], 16)
                reached(sp, m["residual"], i)
                sp.dma_start(x_res[:], rows_of(x1_dram)[i]).then_inc(m["xr_in"], 16)
                if not first:
                    sp.wait_ge(m["y_done"], i)
                    sp.dma_start(rows_of(x2_dram)[i - 1], y[:]).then_inc(m["stored"], 16)

            rows_in(0)
            tile(0, True, False)
            with sp.Fori(1, TILES - 1) as i:
                tile(i, False, False)
            tile(TILES - 1, False, True)
            sp.wait_ge(m["y_done"], TILES)
            sp.dma_start(rows_of(x2_dram)[TILES - 1], y[:]).then_inc(m["stored"], 16)
            sp.wait_ge(m["stored"], 16 * TILES)

        @block.tensor
        def _(pe):
            def slot(i, s, n):
                b, t = s // NT, s % NT
                bp = 1 - b
                if live(n, 1, ALL):
                    pe.wait_ge(m["k_exped"], n)
                    reached(pe, m["kt_copied"], n - 1)
                    for j in range(NT):
                        last = nc.tensor.transpose(trk[:, j * P:(j + 1) * P],
                                                   e_k[:, (s - 1) % 2, j * P:(j + 1) * P], ident[:])
                    last.then_inc(m["k_turned"], 1)
                if live(n, 2, ALL):
                    pe.wait_ge(m["q_normed"], n - 1)
                    reached(pe, m["qt_copied"], n - 2)
                    for j in range(NT):
                        last = nc.tensor.transpose(trp[:, j * P:(j + 1) * P],
                                                   p_q[:, s % 2, j * P:(j + 1) * P], ident[:])
                    last.then_inc(m["q_turned"], 1)
                if live(n, 0, ALL):
                    pe.wait_ge(m["c_split"], 2 * i + b + 1)
                    reached(pe, m["k_exped"], n)
                    for part, w in enumerate((wqk_hi, wqk_lo)):
                        last = nc.tensor.matmul(kl[:], w[:, 1, t * P:(t + 1) * P], cs[:, b, :],
                                                start=(part == 0), stop=(part == 1))
                    last.then_inc(m["k_logits"], 1)
                    pe.wait_ge(m["x_split"], 2 * i + b + 1)
                    reached(pe, m["q_shifted"], n - 1)
                    for part, w in enumerate((wqk_hi, wqk_lo)):
                        last = nc.tensor.matmul(ql[:, s % 2, :], xs[:, b, t * P:(t + 1) * P], w[:, 0, :],
                                                start=(part == 0), stop=(part == 1))
                    last.then_inc(m["q_logits"], 1)
                if t == 1 and live(n, NT, ALL):
                    seq = 2 * i + b
                    pe.wait_ge(m["kt_copied"], n - 1)
                    if b == 0:
                        pe.wait_ge(m["ct_in"], 16 * i)
                    else:
                        pe.wait_ge(m["ct_in"], 16 * i + 16)
                    reached(pe, m["m_scaled"], seq - 1)
                    for j in range(NT):
                        last = nc.tensor.matmul(gm[0:XD, :], c_t[:, j * P + bp * XD:j * P + (bp + 1) * XD],
                                                e_t[:, bp, j, :], start=(j == 0), stop=(j == NT - 1))
                    last.then_inc(m["g_done"], 1)
                if t == 2 and live(n, NT, ALL):
                    seq = 2 * i + b
                    pe.wait_ge(m["g_copied"], seq)
                    for c in range(NT):
                        last = nc.tensor.matmul(gm[:, c * P:(c + 1) * P], g_t[:, c * P:(c + 1) * P],
                                                u[:, c * P:(c + 1) * P], start=True, stop=True)
                    last.then_inc(m["m_done"], 1)
                if t == 3 and live(n, NT, ALL):
                    seq = 2 * i + b
                    pe.wait_ge(m["m_scaled"], seq)
                    pe.wait_ge(m["qt_copied"], n - 3)
                    if bp == 0:
                        reached(pe, m["squared"], i)
                    for c in range(NT):
                        last = nc.tensor.matmul(ob[bp * XD:(bp + 1) * XD, :], m_sb[:, c, :], p_t[:, bp, c, :],
                                                start=(c == 0), stop=(c == NT - 1))
                    last.then_inc(m["o_done"], 1)
                if s == 4 and live(n, SLOTS, ALL):
                    pe.wait_ge(m["squared"], i)
                    reached(pe, m["attended"], i - 1)
                    for j in range(NT):
                        last = nc.tensor.matmul(nb[:, 2 * j:2 * j + 2], sq[:, j * P:(j + 1) * P], half_of[:],
                                                start=True, stop=True)
                    last.then_inc(m["ss_done"], 1)
                if s == 6 and live(n, SLOTS, ALL):
                    pe.wait_ge(m["rn_done"], i)
                    for j in range(NT):
                        last = nc.tensor.matmul(nb[:, j * P:(j + 1) * P],
                                                rn_wide[:, j, :], ident[:],
                                                start=True, stop=True)
                    last.then_inc(m["rb_done"], 1)

            schedule(pe, slot)

        @block.vector
        def _(dve):
            nc.vector.memset(half8[:], -0.5).then_inc(m["half8_set"], 1)

            def split(i, b):
                rows, other = slice(b * XD, (b + 1) * XD), slice((1 - b) * XD, (2 - b) * XD)
                dve.wait_ge(m["c_hi_done"], 2 * i + b + 1)
                nc.vector.scalar_tensor_tensor(out=cs[other, b, :], in0=c_raw[rows, :], scalar=c_inv[rows, :],
                                               in1=cs[rows, b, :], op0=ALU.mult,
                                               op1=ALU.subtract).then_inc(m["c_split"], 1)
                dve.wait_ge(m["x_hi_done"], 2 * i + b + 1)
                nc.vector.tensor_tensor(xs[other, b, :], x_raw[rows, :], xs[rows, b, :],
                                        ALU.subtract).then_inc(m["x_split"], 1)

            def slot(i, s, n):
                b, t = s // NT, s % NT
                if s == 0 and live(n, 0, ALL):
                    split(i, 1)
                if live(n, 0, ALL):
                    dve.wait_ge(m["k_logits"], n + 1)
                    reached(dve, m["k_biased"], n)
                    nc.vector.tensor_reduce(k_neg[:], kl[:], AX.X, ALU.max, negate=True).then_inc(m["k_maxed"], 1)
                    dve.wait_ge(m["k_maxed"], n + 1)
                    reached(dve, m["k_exped"], n)
                    nc.vector.tensor_scalar(k_bias[:], k_neg[:], k_scale, None, ALU.mult).then_inc(m["k_biased"], 1)
                    dve.wait_ge(m["q_logits"], n + 1)
                    q3 = ql[:, s % 2, :].rearrange("p (h d) -> p h d", h=XH)
                    reached(dve, m["q_shifted"], n)
                    nc.vector.tensor_reduce(q_max[:], q3, AX.X, ALU.max).then_inc(m["q_maxed"], 1)
                    dve.wait_ge(m["q_maxed"], n + 1)
                    reached(dve, m["q_turned"], n - 1)
                    nc.vector.tensor_tensor(p_q[:, s % 2, :].rearrange("p (h d) -> p h d", h=XH), q3,
                                            q_max[:, :, None].to_broadcast([P, XH, XD]),
                                            ALU.subtract).then_inc(m["q_shifted"], 1)
                if live(n, 1, ALL):
                    dve.wait_ge(m["q_exped"], n)
                    reached(dve, m["q_inverted"], n - 1)
                    nc.vector.tensor_reduce(q_sum[:], p_q[:, (s - 1) % 2, :].rearrange("p (h d) -> p h d", h=XH),
                                            AX.X, ALU.add).then_inc(m["q_summed"], 1)
                    dve.wait_ge(m["q_summed"], n)
                    reached(dve, m["q_normed"], n - 1)
                    nc.vector.reciprocal(q_rcp[:], q_sum[:]).then_inc(m["q_inverted"], 1)
                if s < QUANT and live(n, 0, ALL):
                    k, w = s // 2, w_raw[:, s % 2, :]
                    dve.wait_ge(w_sem[s % 2], i * 48 + (s // 2 + 1) * 16)
                    if not (isinstance(n, int) and n == 0):
                        dve.wait_ge(m["quantized"], i * QUANT + s)
                    nc.vector.tensor_scalar(below[:], w, thr[:, 3 + k:4 + k], None, ALU.is_lt
                                            ).then_inc(m["below_done"], 1)
                    dve.wait_ge(m["below_done"], i * QUANT + s + 1)
                    nc.vector.scalar_tensor_tensor(out=ffn_q[:, k, i, (s % 2) * D:(s % 2 + 1) * D], in0=w,
                                                   scalar=thr[:, k:k + 1], in1=below[:], op0=ALU.is_gt,
                                                   op1=ALU.subtract).then_inc(m["quantized"], 1)
                if t == 1 and live(n, NT, ALL):
                    dve.wait_ge(m["k_exped"], n - 1)
                    reached(dve, m["m_scaled"], 2 * i + b - 1)
                    nc.vector.reciprocal(r_k[:], z_k[:, 1 - b, :]).then_inc(m["r_k_done"], 1)
                if t == 2 and live(n, NT, ALL):
                    seq = 2 * i + b
                    dve.wait_ge(m["m_done"], seq)
                    dve.wait_ge(m["r_k_done"], seq)
                    reached(dve, m["o_done"], seq - 1)
                    for h in range(2):
                        rows = slice(h * XD, (h + 1) * XD)
                        last = nc.vector.tensor_tensor(
                            m_sb[rows, :, :],
                            gm[rows, :].rearrange("p (c o) -> p c o", c=NT)[:, :, h * XD:(h + 1) * XD],
                            r_k[rows, :, None].to_broadcast([XD, NT, XD]), ALU.mult)
                    last.then_inc(m["m_scaled"], 1)
                if s == 4 and live(n, SLOTS, ALL):
                    dve.wait_ge(m["ss_done"], i)
                    reached(dve, m["rn_raw"], i - 1)
                    nc.vector.tensor_scalar(ss[:], nb[:, 0:SLOTS], 1e-24, None, ALU.max).then_inc(m["ss_copied"], 1)
                if s == 5 and live(n, SLOTS, ALL):
                    dve.wait_ge(m["rn_raw"], i)
                    reached(dve, m["rb_done"], i - 1)
                    nc.vector.tensor_copy(rn_wide[:].rearrange("p j (b o) -> p (j b) o", b=2),
                                          rn[:, :, None].to_broadcast([P, SLOTS, XD])).then_inc(m["rn_done"], 1)
                if s == 4 and live(n, 0, ALL - SLOTS):
                    split(i + 1, 0)
                if s == 6 and live(n, SLOTS, ALL):
                    dve.wait_ge(m["rb_done"], i)
                    reached(dve, m["residual"], i - 1)
                    nc.vector.scalar_tensor_tensor(out=y1[:], in0=o_sb[:], scalar=keep["g8"][:], in1=nb[:],
                                                   op0=ALU.mult, op1=ALU.mult).then_inc(m["attended"], 1)
                    dve.wait_ge(m["attended"], i)
                    dve.wait_ge(m["xr_in"], 16 * i)
                    reached(dve, m["y_done"], i - 1)
                    nc.vector.tensor_tensor(z[:], y1[:], x_res[:], ALU.add).then_inc(m["residual"], 1)
                    dve.wait_ge(m["residual"], i)
                    nc.vector.bn_stats(stats[:], z[:]).then_inc(m["chain"], 1)
                    dve.wait_ge(m["chain"], 3 * i - 2)
                    nc.vector.memset(veps[:], EPS)
                    nc.vector.bn_aggr(mv[:], stats[:]).then_inc(m["chain"], 1)
                    dve.wait_ge(m["chain"], 3 * i - 1)
                    nc.vector.tensor_tensor(veps[:], veps[:], mv[:, 1:2], ALU.add).then_inc(m["chain"], 1)
                if s == 7 and live(n, SLOTS, ALL):
                    dve.wait_ge(m["rstd_done"], i)
                    reached(dve, m["stored"], 16 * (i - 1))
                    nc.vector.tensor_scalar(y[:], z[:], mv[:, 0:1], rstd[:], ALU.subtract,
                                            ALU.mult).then_inc(m["y_done"], 1)

            split(0, 0)
            schedule(dve, slot)

        @block.scalar
        def _(act):
            def split(i, b):
                rows = slice(b * XD, (b + 1) * XD)
                act.wait_ge(m["c_in"], 16 * i + 16)
                reached(act, m["k_logits"], i * SLOTS - (NT if b == 0 else 0))
                nc.scalar.activation(cs[rows, b, :], c_raw[rows, :], ACT.Copy,
                                     scale=c_inv[rows, :]).then_inc(m["c_hi_done"], 1)
                act.wait_ge(m["x_in"], 16 * i + 16)
                reached(act, m["q_logits"], i * SLOTS - (NT if b == 0 else 0))
                nc.scalar.activation(xs[rows, b, :], x_raw[rows, :], ACT.Copy).then_inc(m["x_hi_done"], 1)

            def slot(i, s, n):
                b, t = s // NT, s % NT
                if s == 0 and live(n, 0, ALL):
                    split(i, 1)
                if live(n, 1, ALL):
                    bk, tk = ((s - 1) % SLOTS) // NT, (s - 1) % NT
                    act.wait_ge(m["k_turned"], n)
                    if tk == 0:
                        reached(act, m["g_done"], 2 * i + b - 1)
                    nc.scalar.activation(e_t[:, bk, :, tk * P:(tk + 1) * P],
                                         trk[:].rearrange("p (j r) -> p j r", j=NT),
                                         ACT.Copy).then_inc(m["kt_copied"], 1)
                if live(n, 2, ALL):
                    bq, tq = ((s - 2) % SLOTS) // NT, (s - 2) % NT
                    act.wait_ge(m["q_turned"], n - 1)
                    if tq == 0:
                        reached(act, m["o_done"], 2 * i + b - 1)
                    nc.scalar.activation(p_t[:, bq, :, tq * P:(tq + 1) * P],
                                         trp[:].rearrange("p (c q) -> p c q", c=NT),
                                         ACT.Copy).then_inc(m["qt_copied"], 1)
                if live(n, 0, ALL):
                    act.wait_ge(m["k_biased"], n + 1)
                    reached(act, m["k_turned"], n - 1)
                    if t == 0:
                        reached(act, m["r_k_done"], 2 * i + b - 1)
                    nc.scalar.activation(e_k[:, s % 2, :], kl[:], ACT.Exp, bias=k_bias[:], scale=k_scale,
                                         accum_out=z_k[:, b, t:t + 1]).then_inc(m["k_exped"], 1)
                    act.wait_ge(m["q_shifted"], n + 1)
                    nc.scalar.activation(p_q[:, s % 2, :], p_q[:, s % 2, :], ACT.Exp,
                                         scale=wq_scale).then_inc(m["q_exped"], 1)
                if t == 1 and live(n, NT, ALL):
                    seq = 2 * i + b
                    act.wait_ge(m["g_done"], seq)
                    reached(act, m["m_done"], seq - 1)
                    nc.scalar.activation(g_t[:], gm[0:XD, :], ACT.Copy).then_inc(m["g_copied"], 1)
                if s == 3 and live(n, SLOTS - 1, ALL):
                    act.wait_ge(m["o_done"], 2 * i)
                    reached(act, m["attended"], i - 1)
                    reached(act, m["ss_done"], i - 1)
                    nc.scalar.activation(o_sb[:], ob[:], ACT.Identity, bias=keep["bo"][:])
                    nc.scalar.activation(sq[:], ob[:], ACT.Square, bias=keep["bo"][:]).then_inc(m["squared"], 1)
                if s == 4 and live(n, 0, ALL - SLOTS):
                    split(i + 1, 0)

            split(0, 0)
            schedule(act, slot)

        @block.gpsimd
        def _(pool):
            pool.wait_ge(m["half8_set"], 1)

            def slot(i, s, n):
                if live(n, 1, ALL):
                    pool.wait_ge(m["q_inverted"], n)
                    p3 = p_q[:, (s - 1) % 2, :].rearrange("p (h d) -> p h d", h=XH)
                    nc.gpsimd.tensor_tensor(p3, p3, q_rcp[:, :, None].to_broadcast([P, XH, XD]),
                                            ALU.mult).then_inc(m["q_normed"], 1)
                if s == 4 and live(n, SLOTS, ALL):
                    pool.wait_ge(m["ss_copied"], i)
                    nc.gpsimd.tensor_tensor(rn[:], ss[:], half8[:], ALU.pow).then_inc(m["rn_raw"], 1)
                if s == 6 and live(n, SLOTS, ALL):
                    pool.wait_ge(m["chain"], 3 * i)
                    reached(pool, m["y_done"], i - 1)
                    nc.gpsimd.tensor_tensor(rstd[:], veps[:], keep["neg_half"][:], ALU.pow
                                            ).then_inc(m["rstd_done"], 1)

            schedule(pool, slot)


def ffn_block(nc, ins, keep, x2_dram, out):
    ident, ffn_q = keep["ident"], keep["ffn_q"]
    gate_s, up_s, down_s = keep["gate_s"], keep["up_s"], keep["down_s"]
    w_gate = ffn_q[:, 0].rearrange("p t c -> p (t c)").rearrange("p (k o) -> p k o", k=KT)
    w_up = ffn_q[:, 1].rearrange("p t c -> p (t c)").rearrange("p (k o) -> p k o", k=KT)
    w_down = ffn_q[:, 2].rearrange("p t c -> p (t c)").rearrange("p (k o) -> p k o", k=HT)
    with ExitStack() as ctx:
        sb = lambda name, shape, dt: ctx.enter_context(nc.sbuf_tensor(name, shape, dt))
        ps = lambda name, shape, dt: ctx.enter_context(nc.psum_tensor(name, shape, dt))
        x_in_sb = sb("fx", [P, D], F32)
        x_res = sb("fx_res", [P, D], F32)
        xt_hi = sb("fxt_hi", [P, D], F16)
        xt_lo = sb("fxt_lo", [P, D], F16)
        gate = sb("gate", [P, 2, D], F32)
        up = sb("up", [P, 2, D], F32)
        silu = sb("silu", [P, 2, D], F32)
        h = sb("h", [P, HID], F32)
        hs = sb("hs", [P, HID], F32)
        ht_hi = sb("ht_hi", [P, 2, D], F16)
        ht_lo = sb("ht_lo", [P, 2, D], F16)
        peaks = sb("peaks", [P, FC], F32)
        peak = sb("fpeak", [P, 1], F32)
        power = sb("power", [P, 1], F32)
        inverse = sb("inverse", [P, 1], F32)
        powered = sb("powered", [P, 1], F32)
        d_sb = sb("d_sb", [P, D], F32)
        z = sb("fz", [P, D], F32)
        y = sb("fy", [P, D], F32)
        stats = sb("fstats", [P, 6], F32)
        mv = sb("fmv", [P, 2], F32)
        veps = sb("fveps", [P, 1], F32)
        rstd = sb("frstd", [P, 1], F32)
        tx = ps("tx", [P, D], F32)
        gp = ps("gp", [P, 2, D], F32)
        up_ps = ps("up_ps", [P, 2, D], F32)
        th = ps("th", [P, 2, D], F32)
        dn = ps("dn", [P, D], F32)
        names = ("x_in", "xr_in", "x_turned", "x_hi", "x_split", "gate_up", "gated", "upped", "silu_done", "h_done",
                 "maxed", "peaked", "clamped", "powered", "inverted", "h_scaled", "h_turned", "ht_hi", "ht_split",
                 "down", "unscaled", "residual", "chain", "rstd_done", "y_done", "stored")
        m = {name: ctx.enter_context(nc.semaphore("f_" + name)) for name in names}
        block = ctx.enter_context(nc.Block())
        rows_of = lambda a: a.rearrange("(t p) d -> t p d", p=P)

        def schedule(eng, tile):
            tile(0, True, False)
            tile(1, False, False)
            with eng.Fori(2, TILES) as i:
                tile(i, False, False)
            tile(TILES, False, True)

        @block.sync
        def _(sp):
            def store(i):
                sp.wait_ge(m["y_done"], i + 1)
                sp.dma_start(rows_of(out)[i], y[:]).then_inc(m["stored"], 16)

            def residual_rows(i):
                reached(sp, m["residual"], i)
                sp.dma_start(x_res[:], rows_of(x2_dram)[i]).then_inc(m["xr_in"], 16)

            def next_rows(i):
                reached(sp, m["x_turned"], i)
                sp.dma_start(x_in_sb[:], rows_of(x2_dram)[i]).then_inc(m["x_in"], 16)

            next_rows(0)
            next_rows(1)
            residual_rows(0)
            with sp.Fori(2, TILES) as i:
                next_rows(i)
                residual_rows(i - 1)
                store(i - 2)
            residual_rows(TILES - 1)
            store(TILES - 2)
            store(TILES - 1)
            sp.wait_ge(m["stored"], 16 * TILES)

        @block.tensor
        def _(pe):
            def tile(i, first, past):
                def gate_and_up(c):
                    n = i * FC + c
                    if not (first and c < 2):
                        pe.wait_ge(m["upped"], n - 1)
                    for w, o in ((w_gate, gp), (w_up, up_ps)):
                        for k in range(KT):
                            for part, xs in enumerate((xt_hi, xt_lo)):
                                last = nc.tensor.matmul(o[:, c % 2, :], xs[:, k * P:(k + 1) * P],
                                                        w[:, k, c * D:(c + 1) * D],
                                                        start=(k == 0 and part == 0), stop=(k == KT - 1 and part == 1))
                    last.then_inc(m["gate_up"], 1)

                def turn_hidden(c):
                    n = (i - 1) * FC + c
                    if c == 0:
                        pe.wait_ge(m["h_scaled"], i)
                    reached(pe, m["ht_split"], n - 1)
                    for k in range(4):
                        last = nc.tensor.transpose(th[:, c % 2, k * P:(k + 1) * P],
                                                   hs[:, (c * 4 + k) * P:(c * 4 + k + 1) * P], ident[:])
                    last.then_inc(m["h_turned"], 1)

                def down(c):
                    n = (i - 1) * FC + c
                    pe.wait_ge(m["ht_split"], n + 1)
                    if c == 0:
                        reached(pe, m["unscaled"], i - 1)
                    for k in range(4):
                        for part, hx in enumerate((ht_hi, ht_lo)):
                            last = nc.tensor.matmul(dn[:], hx[:, c % 2, k * P:(k + 1) * P], w_down[:, c * 4 + k, :],
                                                    start=(c == 0 and k == 0 and part == 0),
                                                    stop=(c == FC - 1 and k == 3 and part == 1))
                    last.then_inc(m["down"], 1)

                if not past:
                    pe.wait_ge(m["x_in"], 16 * i + 16)
                    reached(pe, m["x_split"], i)
                    for k in range(KT):
                        last = nc.tensor.transpose(tx[:, k * P:(k + 1) * P], x_in_sb[:, k * P:(k + 1) * P], ident[:])
                    last.then_inc(m["x_turned"], 1)
                    pe.wait_ge(m["x_split"], i + 1)
                    gate_and_up(0)
                    gate_and_up(1)
                if not first:
                    turn_hidden(0)
                    for c in range(FC):
                        if c + 1 < FC:
                            turn_hidden(c + 1)
                        down(c)
                if not past:
                    gate_and_up(2)
                    gate_and_up(3)

            schedule(pe, tile)

        @block.vector
        def _(dve):
            def tile(i, first, past):
                def scale_chunk(c):
                    n = i * FC + c
                    dve.wait_ge(m["gate_up"], n + 1)
                    if not (first and c < 2):
                        dve.wait_ge(m["h_done"], n - 1)
                    nc.vector.tensor_tensor(gate[:, c % 2, :], gp[:, c % 2, :], gate_s[:, c * D:(c + 1) * D],
                                            ALU.mult).then_inc(m["gated"], 1)
                    nc.vector.tensor_tensor(up[:, c % 2, :], up_ps[:, c % 2, :], up_s[:, c * D:(c + 1) * D],
                                            ALU.mult).then_inc(m["upped"], 1)

                def chunk_peak(c):
                    dve.wait_ge(m["h_done"], i * FC + c + 1)
                    if c == 0:
                        reached(dve, m["peaked"], i)
                    nc.vector.tensor_reduce(peaks[:, c:c + 1], h[:, c * D:(c + 1) * D], AX.X, ALU.max,
                                            apply_absolute_value=True).then_inc(m["maxed"], 1)

                if not past:
                    dve.wait_ge(m["x_hi"], i + 1)
                    nc.vector.tensor_tensor(xt_lo[:], tx[:], xt_hi[:], ALU.subtract).then_inc(m["x_split"], 1)
                    scale_chunk(0)
                    scale_chunk(1)
                    chunk_peak(0)
                if not first:
                    for c in range(FC):
                        n = (i - 1) * FC + c
                        dve.wait_ge(m["ht_hi"], n + 1)
                        nc.vector.tensor_tensor(ht_lo[:, c % 2, :], th[:, c % 2, :], ht_hi[:, c % 2, :],
                                                ALU.subtract).then_inc(m["ht_split"], 1)
                if not past:
                    chunk_peak(1)
                if not first:
                    dve.wait_ge(m["down"], i * FC)
                    nc.vector.scalar_tensor_tensor(out=d_sb[:], in0=dn[:], scalar=powered[:], in1=down_s[:],
                                                   op0=ALU.mult, op1=ALU.mult).then_inc(m["unscaled"], 1)
                    dve.wait_ge(m["unscaled"], i)
                    dve.wait_ge(m["xr_in"], 16 * i)
                    reached(dve, m["y_done"], i - 1)
                    nc.vector.tensor_tensor(z[:], d_sb[:], x_res[:], ALU.add).then_inc(m["residual"], 1)
                    dve.wait_ge(m["residual"], i)
                    nc.vector.bn_stats(stats[:], z[:]).then_inc(m["chain"], 1)
                    dve.wait_ge(m["chain"], 3 * i - 2)
                    nc.vector.memset(veps[:], EPS)
                    nc.vector.bn_aggr(mv[:], stats[:]).then_inc(m["chain"], 1)
                    dve.wait_ge(m["chain"], 3 * i - 1)
                    nc.vector.tensor_tensor(veps[:], veps[:], mv[:, 1:2], ALU.add).then_inc(m["chain"], 1)
                if not past:
                    scale_chunk(2)
                    scale_chunk(3)
                if not first:
                    dve.wait_ge(m["rstd_done"], i)
                    reached(dve, m["stored"], 16 * (i - 1))
                    nc.vector.tensor_scalar(y[:], z[:], mv[:, 0:1], rstd[:], ALU.subtract,
                                            ALU.mult).then_inc(m["y_done"], 1)
                if not past:
                    chunk_peak(2)
                    chunk_peak(3)
                    dve.wait_ge(m["maxed"], i * FC + FC)
                    nc.vector.tensor_reduce(peak[:], peaks[:], AX.X, ALU.max).then_inc(m["peaked"], 1)
                    dve.wait_ge(m["peaked"], i + 1)
                    nc.vector.tensor_scalar(power[:], peak[:], TINY, None, ALU.max).then_inc(m["clamped"], 1)
                    dve.wait_ge(m["clamped"], i + 1)
                    nc.vector.tensor_scalar(powered[:].bitcast(I32), power[:].bitcast(I32), EXP_BITS, None,
                                            ALU.bitwise_and).then_inc(m["powered"], 1)
                    dve.wait_ge(m["powered"], i + 1)
                    nc.vector.reciprocal(inverse[:], powered[:]).then_inc(m["inverted"], 1)

            schedule(dve, tile)

        @block.scalar
        def _(act):
            def tile(i, first, past):
                def silu_chunk(c):
                    n = i * FC + c
                    act.wait_ge(m["gated"], n + 1)
                    nc.scalar.activation(silu[:, c % 2, :], gate[:, c % 2, :], ACT.Silu).then_inc(m["silu_done"], 1)

                if not past:
                    act.wait_ge(m["x_turned"], i + 1)
                    reached(act, m["gate_up"], i * FC)
                    nc.scalar.activation(xt_hi[:], tx[:], ACT.Copy).then_inc(m["x_hi"], 1)
                    silu_chunk(0)
                    silu_chunk(1)
                if not first:
                    for c in range(FC):
                        n = (i - 1) * FC + c
                        act.wait_ge(m["h_turned"], n + 1)
                        reached(act, m["down"], n - 1)
                        nc.scalar.activation(ht_hi[:, c % 2, :], th[:, c % 2, :], ACT.Copy).then_inc(m["ht_hi"], 1)
                if not past:
                    silu_chunk(2)
                    silu_chunk(3)
                    act.wait_ge(m["inverted"], i + 1)
                    reached(act, m["h_turned"], i * FC)
                    nc.scalar.activation(hs[:], h[:], ACT.Copy, scale=inverse[:]).then_inc(m["h_scaled"], 1)

            schedule(act, tile)

        @block.gpsimd
        def _(pool):
            def tile(i, first, past):
                def hidden(c):
                    n = i * FC + c
                    pool.wait_ge(m["silu_done"], n + 1)
                    pool.wait_ge(m["upped"], n + 1)
                    if c == 0:
                        reached(pool, m["h_scaled"], i)
                    nc.gpsimd.tensor_tensor(h[:, c * D:(c + 1) * D], silu[:, c % 2, :], up[:, c % 2, :],
                                            ALU.mult).then_inc(m["h_done"], 1)

                if not past:
                    hidden(0)
                    hidden(1)
                if not first:
                    pool.wait_ge(m["chain"], 3 * i)
                    reached(pool, m["y_done"], i - 1)
                    nc.gpsimd.tensor_tensor(rstd[:], veps[:], keep["neg_half"][:], ALU.pow
                                            ).then_inc(m["rstd_done"], 1)
                if not past:
                    hidden(2)
                    hidden(3)

            schedule(pool, tile)


def decoder_layer(nc, ins, out):
    x1_dram = nc.dram_tensor("x1_scratch", [TOK, D], F32, kind="Internal").ap()
    x2_dram = nc.dram_tensor("x2_scratch", [TOK, D], F32, kind="Internal").ap()
    with ExitStack() as whole:
        keep = {}

        def hold(stack, name, shape, dt):
            keep[name] = stack.enter_context(nc.sbuf_tensor("keep_" + name, shape, dt))

        hold(whole, "ident", [P, P], F32)
        hold(whole, "abs_sums", [P, 3, 2 * TILES], F32)
        with ExitStack() as first:
            hold(first, "fac", [P, 13], F32)
            hold(first, "cos", [P, HD], F32)
            hold(first, "sin", [P, HD], F32)
            hold(first, "mask", [P, S], F32)
            hold(first, "w_hi", [P, GROUPS, KT, WC], F16)
            with ExitStack() as prep:
                hold(prep, "sc_parts", [P, 3, WC], BF16)
                hold(prep, "ident_b", [P, P], BF16)
                setup_block(nc, ins, keep)
                hold(prep, "w_lo", [P, GROUPS, KT, WC], F16)
                dequant_block(nc, ins, keep)
                attention_block(nc, ins, keep, x1_dram)
        hold(whole, "neg_half", [P, 1], F32)
        hold(whole, "ffn_q", [P, 3, TILES, 2 * D], BF16)
        hold(whole, "gate_s", [P, HID], F32)
        hold(whole, "up_s", [P, HID], F32)
        hold(whole, "down_s", [P, D], F32)
        with ExitStack() as second:
            hold(second, "xfac", [P, 7], F32)
            hold(second, "thr", [P, 6], F32)
            hold(second, "wqk_hi", [P, 2, XH * XD], F16)
            hold(second, "wqk_lo", [P, 2, XH * XD], F16)
            hold(second, "u", [XD, XH * XD], F32)
            hold(second, "bo", [P, 1], F32)
            hold(second, "g8", [P, 1], F32)
            hold(second, "half_of", [P, 2], F32)
            cross_setup_block(nc, ins, keep)
            cross_block(nc, ins, keep, x1_dram, x2_dram)
        ffn_block(nc, ins, keep, x2_dram, out)


def shape_constants():
    inv_freq = (1.0 / np.float32(10000.0) ** (np.arange(0, HD, 2, dtype=np.float32) / np.float32(HD)))
    freqs = np.arange(S, dtype=np.float32)[:, None] * inv_freq.astype(np.float32)
    emb = np.concatenate([freqs, freqs], axis=-1)
    sign = np.where(np.arange(HD) < HD // 2, -1.0, 1.0).astype(np.float32)
    cos, sin = np.cos(emb).astype(np.float32), np.sin(emb).astype(np.float32) * sign
    mask = np.where(np.tril(np.ones((S, S), bool)), 0.0, -3e38).astype(np.float32)
    half_of = np.repeat(np.eye(2, dtype=np.float32), XD, axis=0)
    two = lambda a: np.concatenate([a, a], axis=0)
    return {"cos": two(cos), "sin": two(sin), "mask": two(mask), "ident": np.eye(P, dtype=np.float32),
            "half_of": half_of}


def kernel(**inputs):
    import concourse.bacc as bacc
    from concourse.bass_utils import run_bass_kernel_spmd

    a = {k: np.asarray(v) for k, v in inputs.items()}

    def by_group(q, k, v, o, rows):
        return np.concatenate([q.reshape(KT, rows, GROUPS, QC).transpose(2, 0, 1, 3),
                               k.reshape(KT, rows, GROUPS, HD).transpose(2, 0, 1, 3),
                               v.reshape(KT, rows, GROUPS, HD).transpose(2, 0, 1, 3),
                               o.reshape(GROUPS, GH, rows, D)], axis=-1)

    def by_tile(w, tiles):
        flat = w.reshape(tiles, P, -1).transpose(1, 0, 2).reshape(P, TILES, -1)
        return flat.transpose(1, 0, 2)

    x = a["x"].reshape(TOK, D)
    c = a["ctx_4096"].reshape(TOK, D)
    columns = lambda m: m.reshape(TILES, P, KT, P).transpose(0, 3, 2, 1).reshape(TILES, P, KT * P)
    arrays = {
        "x_rows": x, "x_t": columns(x), "c_rows": c, "c_t": columns(c),
        "w_int": by_group(*(a["L0_attn_qw_" + n] for n in "qkvo"), P),
        "scales": by_group(*(a["L0_attn_scales_" + n] for n in "qkvo"), 1).reshape(GROUPS * KT, WC),
        "wq_t": a["L0_xattn_Wq"].T, "wk_t": a["L0_xattn_Wk"].T,
        "wv": a["L0_xattn_Wv"].reshape(XH, XD, XD).transpose(1, 0, 2).reshape(XD, XH * XD),
        "wo": a["L0_xattn_Wo"].reshape(XD, XH, XD).transpose(2, 1, 0).reshape(XD, XH * XD),
        "bo": a["L0_xattn_bo"].reshape(XD, 1), "g": a["L0_xattn_g"].reshape(XD, 1),
        "ffn_w": np.stack([by_tile(a["L0_ffn_gate_w"].T, KT), by_tile(a["L0_ffn_up_w"].T, KT),
                           by_tile(a["L0_ffn_down_w"].T, HT)]),
        "gate_s": a["L0_ffn_gate_scale"].reshape(1, HID), "up_s": a["L0_ffn_up_scale"].reshape(1, HID),
        "down_s": a["L0_ffn_down_scale"].reshape(1, D),
        **shape_constants(),
    }
    nc = bacc.Bacc("TRN2", target_bir_lowering=False, num_devices=1)
    feeds, ins = {}, {}
    for name, array in arrays.items():
        array = np.ascontiguousarray(array)
        feeds[f"in_{name}"] = array
        ins[name] = nc.dram_tensor(f"in_{name}", array.shape, mybir.dt.from_np(array.dtype), kind="ExternalInput").ap()
    out = nc.dram_tensor("out", (TOK, D), F32, kind="ExternalOutput").ap()
    decoder_layer(nc, ins, out)
    result = run_bass_kernel_spmd(nc, [feeds], core_ids=[0])
    return np.asarray(result.results[0]["out"]).reshape(B, S, D)
```

```python
from contextlib import ExitStack

import numpy as np
import concourse.bass as bass
from concourse import mybir

F32, F16, BF16, I32 = mybir.dt.float32, mybir.dt.float16, mybir.dt.bfloat16, mybir.dt.int32
ALU = mybir.AluOpType
ACT = mybir.ActivationFunctionType
AX = mybir.AxisListType
RMAX = bass.bass_isa.ReduceOp.absmax
RADD = bass.bass_isa.ReduceOp.add

P = 128
B, S, D = 16, 64, 512
TOK = B * S
TILES = TOK // P
KT = D // P
HD = 128
HEADS, KV = 32, 8
GROUPS = KV
GH = HEADS // KV
QC = GH * HD
QK = QC + HD
PC = QC + 2 * HD
WC = PC + D
STEPS = TILES * GROUPS
XH, XD = 8, 64
HID = 2048
HT = HID // P
FC = HID // D
EXP_BITS = 0x7F800000
TINY = 1e-30
EPS = 1e-5


def reached(eng, sem, count):
    if not isinstance(count, int) or count > 0:
        eng.wait_ge(sem, count)


def live(n, lag, steps):
    return not isinstance(n, int) or 0 <= n - lag < steps


def prepare_block(nc, ins, keep):
    w_int, weights, fac, xf = ins["w_int"], keep["weights"], keep["fac"], keep["xfac"]
    NW = KT
    NI = 2 * KT
    PAIRS = GROUPS // 2
    POOL_K = KT - 1
    UNITS = GROUPS * KT
    part_rows = [slice(k * UNITS, (k + 1) * UNITS) for k in range(3)]
    blocks = [(0, QC), (QC, QK), (QK, PC), (PC, WC)]
    with ExitStack() as ctx:
        sb = lambda name, shape, dt: ctx.enter_context(nc.sbuf_tensor(name, shape, dt))
        sem = lambda name: ctx.enter_context(nc.semaphore(name))
        w32 = sb("w32", [P, NW, WC], F32)
        sc = w32[:, NW - 1, :]
        parts = sb("parts", [P, WC], BF16)
        pick = sb("pick", [P, UNITS], BF16)
        wqk = sb("wqk", [P, 2, XH * XD], F32)
        wv = sb("wv", [XD, XH * XD], F32)
        wo = keep["u"]
        rows = sb("rows", [P, 2, D], F32)
        row_peaks = sb("row_peaks", [P, 2, TILES], F32)
        peak = sb("peak", [P, 8], F32)
        gpeak = sb("gpeak", [P, 8], F32)
        scale_ps = [ctx.enter_context(nc.psum_tensor(f"scale_ps{k}", [P, 1536], F32)) for k in range(2)]
        u_ps = ctx.enter_context(nc.psum_tensor("u_ps", [XD, XH * XD], F32))
        w_in = [sem(f"w_in{k}") for k in range(NI)]
        rows_in = [sem(f"rows_in{k}") for k in range(2)]
        sc_in, const_in, ident_in, wqk_in, small_in = (sem(s) for s in ("sc_in", "const_in", "ident_in", "wqk_in",
                                                                       "small_in"))
        cleared, sc_ready, spread, scaled, hi_done, lo_pool, lo_dve = (sem(s) for s in (
            "cleared", "sc_ready", "spread", "scaled", "hi_done", "lo_pool", "lo_dve"))
        peaked, all_peaked, step_done, row_peaked, folded = (sem(s) for s in (
            "peaked", "all_peaked", "step_done", "row_peaked", "folded"))
        block = ctx.enter_context(nc.Block())

        def landing(g, k):
            return weights[:, g, k].rearrange("p r c -> p (r c)").bitcast(I32)

        @block.sync
        def _(sp):
            def unit(q, half, k, first):
                g = 2 * q + half
                if not first:
                    sp.wait_ge(scaled, g * KT + k - NI + 1)
                sp.dma_start(landing(g, k), w_int[g, k]).then_inc(w_in[half * KT + k], 16)

            def row_loads(q, half, first):
                g = 2 * q + half
                for which, name in enumerate(("x_rows", "c_rows")):
                    if not (first and half == 0):
                        sp.wait_ge(row_peaked, 2 * g - 1 + which)
                    sp.dma_start(rows[:, which, :], ins[name].rearrange("(t p) d -> t p d", p=P)[g]
                                 ).then_inc(rows_in[which], 16)

            sp.wait_ge(cleared, 1)
            for rows_ in part_rows:
                sp.dma_start(sc[rows_, :], ins["scales"]).then_inc(sc_in, 16)
            for half in range(2):
                for k in range(KT):
                    unit(0, half, k, True)
            row_loads(0, 0, True)
            row_loads(0, 1, True)
            with sp.Fori(1, PAIRS) as q:
                for half in range(2):
                    for k in range(KT):
                        unit(q, half, k, False)
                    row_loads(q, half, False)

        @block.tensor
        def _(pe):
            def unit(g, k, first):
                if not first:
                    pe.wait_ge(scaled, g * KT + k - 1)
                column = pick[:, bass.ds(g * KT + k, 1)].to_broadcast([P, P])
                for a in range(0, WC, 512):
                    b = min(a + 512, WC)
                    last = nc.tensor.matmul(scale_ps[k % 2][:, a:b], column, parts[:, a:b], start=True, stop=True)
                last.then_inc(spread, 1)

            pe.wait_ge(sc_ready, 1)
            for k in range(KT):
                unit(0, k, k < 2)
            pe.wait_ge(small_in, 7 * 16)
            for h in range(XH):
                cols = slice(h * XD, (h + 1) * XD)
                last = nc.tensor.matmul(u_ps[:, cols], wv[:, cols], wo[:, cols], start=True, stop=True)
            last.then_inc(folded, 1)
            with pe.Fori(1, GROUPS) as g:
                for k in range(KT):
                    unit(g, k, False)

        @block.vector
        def _(dve):
            done = [0]

            def chain(ins_):
                done[0] += 1
                ins_.then_inc(step_done, 1)
                dve.wait_ge(step_done, done[0])

            def powers(cols, dst, inverse):
                chain(nc.vector.tensor_scalar(dst.bitcast(I32), gpeak[:, cols].bitcast(I32), EXP_BITS, None,
                                              ALU.bitwise_and))
                chain(nc.vector.reciprocal(inverse, dst))

            def unit(q, half, k, first):
                g = 2 * q + half
                dve.wait_ge(w_in[half * KT + k], q * 16 + 16)
                dve.wait_ge(spread, g * KT + k + 1)
                if not first:
                    dve.wait_ge(hi_done, g * KT + k - NW + 1)
                    if k < POOL_K:
                        dve.wait_ge(lo_pool, (g - 1) * POOL_K + k + 1)
                    else:
                        dve.wait_ge(lo_dve, g)
                nc.vector.scalar_tensor_tensor(out=w32[:, k, :], in0=landing(g, k), scalar=-8.0,
                                               in1=scale_ps[k % 2][:, 0:WC], op0=ALU.add,
                                               op1=ALU.mult).then_inc(scaled, 1)

            def low_part(q, half):
                g, k = 2 * q + half, POOL_K
                dve.wait_ge(hi_done, g * KT + k + 1)
                nc.vector.tensor_tensor(weights[:, g, k, 1, :], w32[:, k, :], weights[:, g, k, 0, :],
                                        ALU.subtract).then_inc(lo_dve, 1)

            def row_peak(q, half):
                g = 2 * q + half
                for which in range(2):
                    dve.wait_ge(rows_in[which], g * 16 + 16)
                    nc.vector.tensor_reduce(row_peaks[:, which, bass.ds(g, 1)], rows[:, which, :], AX.X, ALU.max,
                                            apply_absolute_value=True).then_inc(row_peaked, 1)

            nc.vector.memset(sc, 0.0).then_inc(cleared, 1)
            dve.wait_ge(sc_in, 48)
            for k, (a, b) in enumerate(blocks):
                chain(nc.vector.tensor_reduce(peak[:, k:k + 1], sc[:, a:b], AX.X, ALU.max, apply_absolute_value=True))
            nc.vector.tensor_scalar(peak[:, 0:4], peak[:, 0:4], TINY, None, ALU.max).then_inc(peaked, 1)
            dve.wait_ge(ident_in, 16)
            chain(nc.vector.tensor_reduce(pick[:], keep["ident"][:, 0:3 * UNITS].rearrange("p (k r) -> p r k", k=3),
                                          AX.X, ALU.max))
            dve.wait_ge(all_peaked, 1)
            powers(slice(0, 4), fac[:, 0:4], fac[:, 5:9])
            for k, (a, b) in enumerate(blocks):
                chain(nc.vector.tensor_scalar(sc[:, a:b], sc[:, a:b], fac[:, 5 + k:6 + k], None, ALU.mult))
            chain(nc.vector.tensor_copy(parts[:], sc))
            chain(nc.vector.tensor_tensor(sc, sc, parts[:], ALU.subtract))
            for k in range(1, 3):
                chain(nc.vector.tensor_copy(parts[part_rows[k], :], sc[part_rows[k], :]))
            third = part_rows[2]
            chain(nc.vector.tensor_tensor(sc[third, :], sc[third, :], parts[third, :], ALU.subtract))
            chain(nc.vector.tensor_copy(parts[third, :], sc[third, :]))
            nc.vector.memset(keep["neg_half"][:], -0.5).then_inc(sc_ready, 1)
            for k in range(KT):
                unit(0, 0, k, True)
            low_part(0, 0)
            row_peak(0, 0)
            dve.wait_ge(wqk_in, 64)
            for k in range(2):
                chain(nc.vector.tensor_reduce(peak[:, 4 + k:5 + k], wqk[:, k, :], AX.X, ALU.max,
                                              apply_absolute_value=True))
            nc.vector.tensor_scalar(peak[:, 4:6], peak[:, 4:6], TINY, None, ALU.max).then_inc(peaked, 1)
            for k in range(KT):
                unit(0, 1, k, False)
            low_part(0, 1)
            row_peak(0, 1)
            dve.wait_ge(all_peaked, 2)
            powers(slice(4, 6), xf[:, 0:2], xf[:, 3:5])
            for k in range(2):
                chain(nc.vector.tensor_scalar(wqk[:, k, :], wqk[:, k, :], xf[:, 3 + k:4 + k], None, ALU.mult))
                chain(nc.vector.tensor_copy(keep["wqk_hi"][:, k, :], wqk[:, k, :]))
                chain(nc.vector.tensor_tensor(keep["wqk_lo"][:, k, :], wqk[:, k, :], keep["wqk_hi"][:, k, :],
                                              ALU.subtract))
            dve.wait_ge(small_in, 7 * 16)
            chain(nc.vector.tensor_scalar(keep["g8"][:], keep["g8"][:], float(XD) ** 0.5, None, ALU.mult))
            dve.wait_ge(folded, 1)
            chain(nc.vector.tensor_scalar(keep["u"][:], u_ps[:], float(XD) ** -0.5, None, ALU.mult))
            with dve.Fori(1, PAIRS) as q:
                for half in range(2):
                    for k in range(KT):
                        unit(q, half, k, False)
                    low_part(q, half)
                    row_peak(q, half)
            dve.wait_ge(row_peaked, 2 * TILES)
            chain(nc.vector.tensor_reduce(peak[:, 6:8], row_peaks[:], AX.X, ALU.max))
            nc.vector.tensor_scalar(peak[:, 6:8], peak[:, 6:8], TINY, None, ALU.max).then_inc(peaked, 1)
            dve.wait_ge(all_peaked, 3)
            powers(slice(6, 7), fac[:, 4:5], fac[:, 9:10])
            powers(slice(7, 8), xf[:, 2:3], xf[:, 5:6])
            chain(nc.vector.tensor_tensor(fac[:, 10:11], fac[:, 0:1], fac[:, 1:2], ALU.mult))
            chain(nc.vector.tensor_tensor(fac[:, 10:11], fac[:, 10:11], fac[:, 4:5], ALU.mult))
            chain(nc.vector.tensor_tensor(fac[:, 10:11], fac[:, 10:11], fac[:, 4:5], ALU.mult))
            chain(nc.vector.tensor_scalar(fac[:, 10:11], fac[:, 10:11], float(HD) ** -0.5, None, ALU.mult))
            chain(nc.vector.tensor_tensor(fac[:, 11:12], fac[:, 2:3], fac[:, 3:4], ALU.mult))
            chain(nc.vector.tensor_tensor(fac[:, 11:12], fac[:, 11:12], fac[:, 4:5], ALU.mult))
            chain(nc.vector.tensor_tensor(xf[:, 6:7], xf[:, 1:2], xf[:, 2:3], ALU.mult))
            dve.wait_ge(lo_dve, GROUPS)

        @block.scalar
        def _(act):
            act.dma_start(keep["ident"][:], ins["ident"]).then_inc(ident_in, 16)
            for half in range(2):
                part = slice(half * XD, (half + 1) * XD)
                act.dma_start(wqk[part, 0, :], ins["wq_t"]).then_inc(wqk_in, 16)
                act.dma_start(wqk[part, 1, :], ins["wk_t"]).then_inc(wqk_in, 16)
                act.dma_start(keep["bo"][part, :], ins["bo"]).then_inc(small_in, 16)
                act.dma_start(keep["g8"][part, :], ins["g"]).then_inc(small_in, 16)
            act.dma_start(wv[:], ins["wv"]).then_inc(small_in, 16)
            act.dma_start(wo[:], ins["wo"]).then_inc(small_in, 16)
            act.dma_start(keep["half_of"][:], ins["half_of"]).then_inc(small_in, 16)
            act.dma_start(keep["cos"][:], ins["cos"]).then_inc(const_in, 16)
            act.dma_start(keep["sin"][:], ins["sin"]).then_inc(const_in, 16)
            act.dma_start(keep["mask"][:], ins["mask"]).then_inc(const_in, 16)

            def unit(g, k):
                act.wait_ge(scaled, g * KT + k + 1)
                nc.scalar.activation(weights[:, g, k, 0, :], w32[:, k, :], ACT.Copy).then_inc(hi_done, 1)

            for k in range(KT):
                unit(0, k)
            with act.Fori(1, GROUPS) as g:
                for k in range(KT):
                    unit(g, k)
            act.wait_ge(const_in, 48)

        @block.gpsimd
        def _(pool):
            def low_parts(g):
                for k in range(POOL_K):
                    pool.wait_ge(hi_done, g * KT + k + 1)
                    nc.gpsimd.tensor_tensor(weights[:, g, k, 1, :], w32[:, k, :], weights[:, g, k, 0, :],
                                            ALU.subtract).then_inc(lo_pool, 1)

            def all_peak(cols, count):
                pool.wait_ge(peaked, count)
                nc.gpsimd.partition_all_reduce(gpeak[:, cols], peak[:, cols], P, RMAX).then_inc(all_peaked, 1)

            all_peak(slice(0, 4), 1)
            low_parts(0)
            all_peak(slice(4, 6), 2)
            with pool.Fori(1, GROUPS) as g:
                low_parts(g)
            all_peak(slice(6, 8), 3)


def attention_block(nc, ins, keep, x1_dram, q_dram):
    fac = keep["fac"]
    w_hi, w_lo = (keep["weights"][:, :, :, part, :] for part in range(2))
    cos, sin, mask, ident = keep["cos"], keep["sin"], keep["mask"], keep["ident"]
    x_t, x_rows, ffn_w = ins["x_t"], ins["x_rows"], ins["ffn_w"]
    alpha, beta, x_inv = fac[:, 10:11], fac[:, 11:12], fac[:, 9:10]
    NV = 4
    HALF = HD // 2
    SUM_TILES = 3
    QUANT_FROM = TILES // 2
    ROW_TILES = TILES // (TILES - QUANT_FROM)
    QUANT_STEPS = 3 * ROW_TILES
    SUM_CHUNKS = SUM_TILES * GROUPS * 2

    def quant_unit(i, g):
        return (i - QUANT_FROM) * QUANT_STEPS + g

    with ExitStack() as ctx:
        sb = lambda name, shape, dt: ctx.enter_context(nc.sbuf_tensor(name, shape, dt))
        ps = lambda name, shape, dt: ctx.enter_context(nc.psum_tensor(name, shape, dt))
        sem = lambda name: ctx.enter_context(nc.semaphore(name))
        xt32 = sb("xt32", [P, KT * P], F32)
        xt_hi = sb("xt_hi", [P, KT * P], F16)
        xt_lo = sb("xt_lo", [P, KT * P], F16)
        x_res = sb("x_res", [P, D], F32)
        by_cos = sb("by_cos", [P, QK], F32)
        by_sin = sb("by_sin", [P, QK], F32)
        rot = sb("rot", [P, QK], F32)
        qk_t = sb("qk_t", [P, QK], F32)
        v_two = sb("v_two", [P, NV, 2, HD], F32)
        probs = sb("probs", [P, GH * S], F32)
        probs_t = sb("probs_t", [P, 2, P], F32)
        c_hi = sb("c_hi", [P, 2, GH * P], F16)
        c_lo = sb("c_lo", [P, 2, GH * P], F16)
        neg_max = sb("neg_max", [P, GH], F32)
        psum_row = sb("psum_row", [P, GH], F32)
        rcp = sb("rcp", [P, GH], F32)
        z = sb("z", [P, D], F32)
        y = sb("y", [P, D], F32)
        stats = sb("stats", [P, 6], F32)
        mv = sb("mv", [P, 2], F32)
        veps = sb("veps", [P, 1], F32)
        rstd = sb("rstd", [P, 1], F32)
        neg_half = sb("neg_half", [P, 1], F32)
        ffn_in = sb("ffn_in", [P, 2, D], F32)
        below = sb("below", [P, D], BF16)
        q_out = sb("q_out", [P, 2, D], BF16)
        abs_sums = sb("abs_sums", [P, 3, 2 * TILES], F32)
        asum = sb("asum", [P, 3], F32)
        gsum = sb("gsum", [P, 3], F32)
        thr = sb("thr", [P, 6], F32)
        pj = ps("pj", [P, 1024], F32)
        tr = ps("tr", [P, 1024], F32)
        sp_ = ps("scores_ps", [P, 512], F32)
        pv = ps("pv", [P, 2, 512], F32)
        oacc = ps("oacc", [P, 512], F32)

        xt_in, xr_in, ffn_sem = sem("xt_in"), sem("xr_in"), [sem("ffn_in0"), sem("ffn_in1")]
        xt_hi_done, xt_split = sem("xt_hi_done"), sem("xt_split")
        projected, turned, scored, p_turned, weighed, o_done = (sem(s) for s in (
            "projected", "turned", "scored", "p_turned", "weighed", "o_done"))
        roped, masked, maxed, inverted, c_lo_done, residual = (sem(s) for s in (
            "roped", "masked", "maxed", "inverted", "c_lo_done", "residual"))
        rotated, normed, rstd_done = sem("rotated"), sem("normed"), sem("rstd_done")
        v_copied, qk_copied, exped, pt_copied, c_hi_done = (sem(s) for s in (
            "v_copied", "qk_copied", "exped", "pt_copied", "c_hi_done"))
        ln_chain, y_done, stored, half_set = (sem(s) for s in ("ln_chain", "y_done", "stored", "half_set"))
        chunk_used, summed, all_summed, thr_done, below_done = (sem(s) for s in (
            "chunk_used", "summed", "all_summed", "thr_done", "below_done"))
        q_stored = [sem("q_stored0"), sem("q_stored1")]
        block = ctx.enter_context(nc.Block())

        def schedule(eng, step, loops):
            def tile(i, number):
                phase = ("sum" if number < SUM_TILES else "threshold" if number == SUM_TILES else
                         "wait" if number < QUANT_FROM else "quantise")
                for g in range(GROUPS):
                    step(i, g, i * GROUPS + g, phase)

            at = 0
            for a, b in loops:
                for i in range(at, a):
                    tile(i, i)
                with eng.Fori(a, b) as i:
                    tile(i, a)
                at = b
            for i in range(at, TILES):
                tile(i, i)
            for g in range(4):
                step(TILES, g, STEPS + g, "past")

        SUMMING, QUANTISING = (1, SUM_TILES), (QUANT_FROM + 1, TILES - 1)

        @block.sync
        def _(sp):
            def columns_in(i):
                reached(sp, xt_split, i)
                sp.dma_start(xt32[:], x_t[i]).then_inc(xt_in, 16)

            def rows(i, last):
                if not last:
                    columns_in(i + 1)
                reached(sp, residual, i)
                sp.dma_start(x_res[:], x_rows.rearrange("(t p) d -> t p d", p=P)[i]).then_inc(xr_in, 16)
                if isinstance(i, int) and i == 0:
                    return
                sp.wait_ge(y_done, i)
                sp.dma_start(x1_dram.rearrange("(t p) d -> t p d", p=P)[i - 1], y[:]).then_inc(stored, 16)

            def chunk_in(row_tile, half, before):
                reached(sp, chunk_used, before - 1)
                sp.dma_start(ffn_in[:, half, :], row_tile[:, half * D:(half + 1) * D]).then_inc(ffn_sem[half], 16)

            def sum_tile(i):
                for g in range(GROUPS):
                    for half in range(2):
                        chunk_in(ffn_w[i, g], half, (i * GROUPS + g) * 2 + half)
                    if g == GROUPS // 2:
                        rows(i, False)

            def quant_tile(i, last):
                for g in range(QUANT_STEPS):
                    unit, quarter = quant_unit(i, g), i - QUANT_FROM
                    of_step = lambda w: w.rearrange("m (q r) p c -> m q r p c", r=ROW_TILES)[
                        g // ROW_TILES, quarter, g % ROW_TILES]
                    for half in range(2):
                        chunk_in(of_step(ffn_w), half, unit * 2 + SUM_CHUNKS + half)
                    for half in range(2):
                        sp.wait_ge(chunk_used, unit * 2 + SUM_CHUNKS + half + 1)
                        sp.dma_start(of_step(q_dram)[:, half * D // 2:(half + 1) * D // 2], q_out[:, half, :].bitcast(I32)
                                     ).then_inc(q_stored[half], 16)
                    if g == QUANT_STEPS // 2:
                        rows(i, last)

            columns_in(0)
            sum_tile(0)
            with sp.Fori(*SUMMING) as i:
                sum_tile(i)
            for i in range(SUM_TILES, QUANT_FROM):
                rows(i, False)
            quant_tile(QUANT_FROM, False)
            with sp.Fori(*QUANTISING) as i:
                quant_tile(i, False)
            quant_tile(TILES - 1, True)
            sp.wait_ge(y_done, TILES)
            sp.dma_start(x1_dram.rearrange("(t p) d -> t p d", p=P)[TILES - 1], y[:]).then_inc(stored, 16)
            sp.wait_ge(stored, 16 * TILES)
            for half in range(2):
                sp.wait_ge(q_stored[half], 16 * 3 * TILES)

        @block.tensor
        def _(pe):
            def step(i, g, n, phase):
                if live(n, 1, STEPS):
                    pe.wait_ge(rotated, n)
                    reached(pe, qk_copied, n - 1)
                    for h in range(GH + 1):
                        last = nc.tensor.transpose(tr[:, h * P:(h + 1) * P], rot[:, h * P:(h + 1) * P], ident[:])
                    last.then_inc(turned, 1)
                if live(n, 0, STEPS):
                    if g == 0:
                        pe.wait_ge(xt_split, i + 1)
                    reached(pe, roped, n)
                    reached(pe, v_copied, n)
                    for k in range(KT):
                        for part, (xs, w) in enumerate(((xt_hi, w_hi), (xt_hi, w_lo), (xt_lo, w_hi))):
                            for a, b in ((0, QC), (QC, PC)):
                                last = nc.tensor.matmul(pj[:, a:b], xs[:, k * P:(k + 1) * P], w[:, g, k, a:b],
                                                        start=(k == 0 and part == 0), stop=(k == KT - 1 and part == 2))
                    last.then_inc(projected, 1)
                if live(n, 2, STEPS):
                    pe.wait_ge(normed, n - 1)
                    if live(n, 1, STEPS):
                        pe.wait_ge(qk_copied, n)
                    for c in range(2):
                        last = nc.tensor.transpose(tr[:, QK + c * P:QK + (c + 1) * P], probs[:, c * P:(c + 1) * P],
                                                   ident[:])
                    last.then_inc(p_turned, 1)
                if live(n, 1, STEPS):
                    pe.wait_ge(qk_copied, n)
                    for h in range(GH):
                        last = nc.tensor.matmul(sp_[:, h * P:(h + 1) * P], qk_t[:, h * P:(h + 1) * P],
                                                qk_t[:, QC:QK], start=True, stop=True)
                    last.then_inc(scored, 1)
                if live(n, 2, STEPS):
                    pe.wait_ge(pt_copied, n - 1)
                    reached(pe, c_lo_done, n - 2)
                    gv = (g - 2) % NV
                    for par in range(2):
                        rows = slice(par * S, par * S + S)
                        for b in range(2):
                            last = nc.tensor.matmul(
                                pv[:, par, 0:2 * P].rearrange("p (c b q) -> p c b q", c=2, b=2)[:, :, b, :],
                                v_two[rows, gv, b, :],
                                probs_t[rows, :, b * S:(b + 1) * S], start=(b == 0), stop=True,
                                skip_group_check=True)
                    last.then_inc(weighed, 1)
                if live(n, 3, STEPS):
                    go = (g - 3) % GROUPS
                    pe.wait_ge(c_lo_done, n - 2)
                    if go == 0:
                        reached(pe, residual, i)
                    for h in range(GH):
                        cols = slice(h * P, (h + 1) * P)
                        for part, (cs, w) in enumerate(((c_hi, w_hi), (c_hi, w_lo), (c_lo, w_hi))):
                            last = nc.tensor.matmul(oacc[:], cs[:, (g - 3) % 2, cols], w[:, go, h, PC:WC],
                                                    start=(go == 0 and h == 0 and part == 0),
                                                    stop=(go == GROUPS - 1 and h == GH - 1 and part == 2))
                    last.then_inc(o_done, 1)

            schedule(pe, step, [(1, TILES - 1)])

        @block.vector
        def _(dve):
            nc.vector.memset(neg_half[:], -0.5).then_inc(half_set, 1)

            def thresholds(g):
                if g == 0:
                    dve.wait_ge(chunk_used, SUM_CHUNKS)
                    nc.vector.tensor_reduce(asum[:], abs_sums[:], AX.X, ALU.add).then_inc(summed, 1)
                if g == 1:
                    dve.wait_ge(all_summed, 1)
                    nc.vector.tensor_scalar(thr[:, 0:3], gsum[:], 1.0 / (HID * D), 0.7, ALU.mult,
                                            ALU.mult).then_inc(thr_done, 1)
                    dve.wait_ge(thr_done, 1)
                    nc.vector.tensor_scalar(thr[:, 3:6], thr[:, 0:3], -1.0, None, ALU.mult).then_inc(thr_done, 1)

            def quantise(matrix, unit):
                for half in range(2):
                    w, chunk = ffn_in[:, half, :], unit * 2 + SUM_CHUNKS + half
                    dve.wait_ge(ffn_sem[half], (unit + SUM_TILES * GROUPS) * 16 + 16)
                    dve.wait_ge(thr_done, 2)
                    dve.wait_ge(chunk_used, chunk)
                    nc.vector.tensor_scalar(below[:], w, thr[:, 3 + matrix:4 + matrix], None, ALU.is_lt
                                            ).then_inc(below_done, 1)
                    dve.wait_ge(below_done, unit * 2 + half + 1)
                    if not isinstance(unit, int) or unit > 0:
                        dve.wait_ge(q_stored[half], unit * 16)
                    nc.vector.scalar_tensor_tensor(out=q_out[:, half, :], in0=w, scalar=thr[:, matrix:matrix + 1],
                                                   in1=below[:], op0=ALU.is_gt,
                                                   op1=ALU.subtract).then_inc(chunk_used, 1)

            def split_x(i):
                dve.wait_ge(xt_hi_done, i + 1)
                nc.vector.scalar_tensor_tensor(out=xt_lo[:], in0=xt32[:], scalar=x_inv, in1=xt_hi[:],
                                               op0=ALU.mult, op1=ALU.subtract).then_inc(xt_split, 1)

            def step(i, g, n, phase):
                if live(n, 0, STEPS):
                    dve.wait_ge(projected, n + 1)
                    reached(dve, rotated, n)
                    heads = GH + 1
                    src = pj[:, 0:QK].rearrange("p (h d) -> p h d", h=heads)
                    out = by_sin[:].rearrange("p (h d) -> p h d", h=heads)
                    nc.vector.tensor_tensor(by_cos[:].rearrange("p (h d) -> p h d", h=heads), src,
                                            cos[:, None, :].to_broadcast([P, heads, HD]), ALU.mult)
                    for a, b in ((0, HALF), (HALF, 0)):
                        last = nc.vector.tensor_tensor(out[:, :, a:a + HALF], src[:, :, b:b + HALF],
                                                       sin[:, None, a:a + HALF].to_broadcast([P, heads, HALF]),
                                                       ALU.mult)
                    last.then_inc(roped, 1)
                if live(n, 1, STEPS):
                    dve.wait_ge(scored, n)
                    reached(dve, p_turned, n - 1)
                    for b in range(2):
                        rows = slice(b * S, (b + 1) * S)
                        last = nc.vector.scalar_tensor_tensor(
                            out=probs[rows, :].rearrange("p (h k) -> p h k", h=GH),
                            in0=sp_[rows, :].rearrange("p (h k) -> p h k", h=GH)[:, :, b * S:(b + 1) * S],
                            scalar=alpha[rows, :], in1=mask[rows, None, :].to_broadcast([S, GH, S]),
                            op0=ALU.mult, op1=ALU.add)
                    last.then_inc(masked, 1)
                    dve.wait_ge(masked, n)
                    reached(dve, exped, n - 1)
                    nc.vector.tensor_reduce(neg_max[:], probs[:].rearrange("p (h k) -> p h k", h=GH), AX.X,
                                            ALU.max, negate=True).then_inc(maxed, 1)
                if live(n, 2, STEPS):
                    dve.wait_ge(c_hi_done, n - 1)
                    reached(dve, o_done, n - 3)
                    nc.vector.tensor_tensor(
                        c_lo[:, g % 2, :].rearrange("p (c r q) -> p r c q", c=2, r=2),
                        pv[:, :, 0:2 * P].rearrange("p r (c q) -> p r c q", c=2),
                        c_hi[:, g % 2, :].rearrange("p (c r q) -> p r c q", c=2, r=2),
                        ALU.subtract).then_inc(c_lo_done, 1)
                if live(n, 1, STEPS):
                    dve.wait_ge(exped, n)
                    reached(dve, normed, n - 1)
                    nc.vector.reciprocal(rcp[:], psum_row[:]).then_inc(inverted, 1)
                if phase == "sum":
                    for half in range(2):
                        dve.wait_ge(ffn_sem[half], (i * GROUPS + g) * 16 + 16)
                        nc.vector.tensor_reduce(
                            abs_sums[:, bass.ds(i, 1), 2 * g + half:2 * g + half + 1].rearrange("p m c -> p (m c)"),
                            ffn_in[:, half, :], AX.X, ALU.add, apply_absolute_value=True).then_inc(chunk_used, 1)
                if phase == "threshold":
                    thresholds(g)
                if phase == "quantise" and g < QUANT_STEPS:
                    quantise(g // ROW_TILES, quant_unit(i, g))
                if g == GROUPS - 1 and live(n, 0, STEPS - 1):
                    split_x(i + 1)
                if g == 2 and live(n, GROUPS, STEPS):
                    dve.wait_ge(o_done, i * GROUPS)
                    dve.wait_ge(xr_in, i * 16)
                    reached(dve, y_done, i - 1)
                    nc.vector.scalar_tensor_tensor(out=z[:], in0=oacc[:], scalar=beta, in1=x_res[:],
                                                   op0=ALU.mult, op1=ALU.add).then_inc(residual, 1)
                    dve.wait_ge(residual, i)
                    nc.vector.bn_stats(stats[:], z[:]).then_inc(ln_chain, 1)
                    dve.wait_ge(ln_chain, i * 3 - 2)
                    nc.vector.memset(veps[:], EPS)
                    nc.vector.bn_aggr(mv[:], stats[:]).then_inc(ln_chain, 1)
                    dve.wait_ge(ln_chain, i * 3 - 1)
                    nc.vector.tensor_tensor(veps[:], veps[:], mv[:, 1:2], ALU.add).then_inc(ln_chain, 1)
                if g == 3 and live(n, GROUPS, STEPS):
                    dve.wait_ge(rstd_done, i)
                    reached(dve, stored, (i - 1) * 16)
                    nc.vector.tensor_scalar(y[:], z[:], mv[:, 0:1], rstd[:], ALU.subtract,
                                            ALU.mult).then_inc(y_done, 1)

            split_x(0)
            schedule(dve, step, [SUMMING, QUANTISING])

        @block.scalar
        def _(act):
            def split_x(i):
                act.wait_ge(xt_in, i * 16 + 16)
                reached(act, projected, i * GROUPS)
                nc.scalar.activation(xt_hi[:], xt32[:], ACT.Copy, scale=x_inv).then_inc(xt_hi_done, 1)

            def step(i, g, n, phase):
                if live(n, 1, STEPS):
                    act.wait_ge(turned, n)
                    reached(act, scored, n - 1)
                    nc.scalar.activation(qk_t[:], tr[:, 0:QK], ACT.Copy).then_inc(qk_copied, 1)
                if live(n, 2, STEPS):
                    act.wait_ge(p_turned, n - 1)
                    reached(act, weighed, n - 2)
                    nc.scalar.activation(probs_t[:].rearrange("p c q -> p (c q)"), tr[:, QK:QK + 2 * P],
                                         ACT.Copy).then_inc(pt_copied, 1)
                if live(n, 2, STEPS):
                    act.wait_ge(weighed, n - 1)
                    reached(act, o_done, n - 3)
                    nc.scalar.activation(
                        c_hi[:, g % 2, :].rearrange("p (c r q) -> p r c q", c=2, r=2),
                        pv[:, :, 0:2 * P].rearrange("p r (c q) -> p r c q", c=2), ACT.Copy).then_inc(c_hi_done, 1)
                if live(n, 0, STEPS):
                    act.wait_ge(roped, n + 1)
                    reached(act, weighed, n - NV + 1)
                    for b in range(2):
                        for half in range(2):
                            last = nc.scalar.activation(v_two[half * S:(half + 1) * S, g % NV, b, :],
                                                        pj[b * S:(b + 1) * S, QK:PC], ACT.Copy)
                    last.then_inc(v_copied, 1)
                if live(n, 1, STEPS):
                    act.wait_ge(maxed, n)
                    reached(act, inverted, n - 1)
                    for h in range(GH):
                        cols = slice(h * S, (h + 1) * S)
                        last = nc.scalar.activation(probs[:, cols], probs[:, cols], ACT.Exp,
                                                    bias=neg_max[:, h:h + 1], accum_out=psum_row[:, h:h + 1])
                    last.then_inc(exped, 1)
                if g == GROUPS - 1 and live(n, 0, STEPS - 1):
                    split_x(i + 1)

            split_x(0)
            schedule(act, step, [(1, TILES - 1)])

        @block.gpsimd
        def _(pool):
            pool.wait_ge(half_set, 1)

            def step(i, g, n, phase):
                if live(n, 0, STEPS):
                    pool.wait_ge(roped, n + 1)
                    reached(pool, turned, n)
                    nc.gpsimd.tensor_tensor(rot[:], by_cos[:], by_sin[:], ALU.add).then_inc(rotated, 1)
                if live(n, 1, STEPS):
                    pool.wait_ge(inverted, n)
                    nc.gpsimd.tensor_tensor(probs[:].rearrange("p (h k) -> p h k", h=GH),
                                            probs[:].rearrange("p (h k) -> p h k", h=GH),
                                            rcp[:, :, None].to_broadcast([P, GH, S]), ALU.mult).then_inc(normed, 1)
                if phase == "threshold" and g == 0:
                    pool.wait_ge(summed, 1)
                    nc.gpsimd.partition_all_reduce(gsum[:], asum[:], P, RADD).then_inc(all_summed, 1)
                if g == 2 and live(n, GROUPS, STEPS):
                    pool.wait_ge(ln_chain, i * 3)
                    reached(pool, y_done, i - 1)
                    nc.gpsimd.tensor_tensor(rstd[:], veps[:], neg_half[:], ALU.pow).then_inc(rstd_done, 1)

            schedule(pool, step, [SUMMING, (SUM_TILES + 1, TILES - 1)])


def cross_block(nc, ins, keep, x1_dram, q_dram, x2_dram):
    ident, wqk_hi, wqk_lo, xf = (keep[k] for k in ("ident", "wqk_hi", "wqk_lo", "xfac"))
    ffn_q, u, half_of = keep["ffn_q"], keep["u"], keep["half_of"]
    wq_scale, k_scale, c_inv = xf[:, 0:1], xf[:, 6:7], xf[:, 5:6]
    NT = D // P
    SLOTS = 2 * NT
    ALL = SLOTS * TILES
    NQ = 4
    with ExitStack() as ctx:
        sb = lambda name, shape, dt: ctx.enter_context(nc.sbuf_tensor(name, shape, dt))
        ps = lambda name, shape, dt: ctx.enter_context(nc.psum_tensor(name, shape, dt))
        sem = lambda name: ctx.enter_context(nc.semaphore(name))
        x_raw = sb("x_raw", [P, D], F32)
        c_raw = sb("c_raw", [P, D], F32)
        x_res = sb("x_res2", [P, D], F32)
        c_t = sb("c_t", [P, NT * P], F32)
        xs = sb("xs", [P, 2, D], F16)
        cs = sb("cs", [P, 2, D], F16)
        e_k = sb("e_k", [P, 2, D], F32)
        p_q = sb("p_q", [P, NQ, D], F32)
        e_t = sb("e_t", [P, 2, NT, D], F32)
        p_t = sb("p_t", [P, 2, NT, D], F32)
        k_neg = sb("k_neg", [P, 1], F32)
        k_bias = sb("k_bias", [P, 1], F32)
        z_k = sb("z_k", [P, 2, NT], F32)
        r_k = sb("r_k", [P, NT], F32)
        q_max = sb("q_max", [P, XH], F32)
        q_sum = sb("q_sum", [P, XH], F32)
        q_rcp = sb("q_rcp", [P, XH], F32)
        g_t = sb("g_t", [XD, XH * XD], F32)
        m_sb = sb("m_sb", [P, NT, XD], F32)
        o_sb = sb("o_sb", [P, D], F32)
        sq = sb("sq", [P, D], F32)
        ss = sb("ss", [P, SLOTS], F32)
        rn = sb("rn", [P, SLOTS], F32)
        half8 = sb("half8", [P, SLOTS], F32)
        rn_wide = sb("rn_wide", [P, NT, P], F32)
        y1 = sb("y1", [P, D], F32)
        z = sb("z2", [P, D], F32)
        y = sb("y2", [P, D], F32)
        stats = sb("stats2", [P, 6], F32)
        mv = sb("mv2", [P, 2], F32)
        veps = sb("veps2", [P, 1], F32)
        rstd = sb("rstd2", [P, 1], F32)
        kl = ps("kl", [P, D], F32)
        ql = ps("ql", [P, 2, D], F32)
        trk = ps("trk", [P, D], F32)
        trp = ps("trp", [P, D], F32)
        gm = ps("gm", [P, D], F32)
        ob = ps("ob", [P, D], F32)
        nb = ps("nb", [P, D], F32)

        names = ("x_in", "c_in", "xr_in", "ct_in", "x_split", "c_split", "x_hi_done", "c_hi_done",
                 "k_logits", "q_logits", "k_turned", "q_turned", "g_done", "m_done", "o_done", "ss_done", "rb_done",
                 "k_maxed", "k_biased", "q_maxed", "q_shifted", "q_summed", "q_inverted", "m_scaled", "r_k_done",
                 "k_exped", "q_exped", "kt_copied", "qt_copied", "g_copied", "squared", "q_normed", "ss_copied",
                 "rn_done", "attended", "residual", "chain", "rstd_done", "y_done", "stored", "half8_set",
                 "rn_raw", "tables_in", "ternary_in")
        m = {name: sem("x_" + name) for name in names}
        block = ctx.enter_context(nc.Block())
        rows_of = lambda a: a.rearrange("(t p) d -> t p d", p=P)

        def schedule(eng, slot):
            for s in range(SLOTS):
                slot(0, s, s)
            with eng.Fori(1, TILES - 1) as i:
                for s in range(SLOTS):
                    slot(i, s, i * SLOTS + s)
            for s in range(SLOTS):
                slot(TILES - 1, s, ALL - SLOTS + s)
            for s in range(SLOTS):
                slot(TILES, s, ALL + s)

        @block.sync
        def _(sp):
            def rows_in(i):
                reached(sp, m["x_split"], 2 * i)
                sp.dma_start(x_raw[:], rows_of(x1_dram)[i]).then_inc(m["x_in"], 16)
                reached(sp, m["c_split"], 2 * i)
                sp.dma_start(c_raw[:], rows_of(ins["c_rows"])[i]).then_inc(m["c_in"], 16)

            def tile(i, first, last):
                reached(sp, m["g_done"], 2 * i)
                sp.dma_start(c_t[:], ins["c_t"][i]).then_inc(m["ct_in"], 16)
                if not last:
                    rows_in(i + 1)
                for matrix in range(3):
                    sp.dma_start(ffn_q[:, matrix, i, :].bitcast(I32), q_dram[matrix, i]).then_inc(m["ternary_in"], 16)
                reached(sp, m["residual"], i)
                sp.dma_start(x_res[:], rows_of(x1_dram)[i]).then_inc(m["xr_in"], 16)
                if not first:
                    sp.wait_ge(m["y_done"], i)
                    sp.dma_start(rows_of(x2_dram)[i - 1], y[:]).then_inc(m["stored"], 16)

            rows_in(0)
            sp.dma_start(keep["gate_s"][:], ins["gate_s"].to_broadcast([P, HID])).then_inc(m["tables_in"], 16)
            sp.dma_start(keep["up_s"][:], ins["up_s"].to_broadcast([P, HID])).then_inc(m["tables_in"], 16)
            sp.dma_start(keep["down_s"][:], ins["down_s"].to_broadcast([P, D])).then_inc(m["tables_in"], 16)
            tile(0, True, False)
            with sp.Fori(1, TILES - 1) as i:
                tile(i, False, False)
            tile(TILES - 1, False, True)
            sp.wait_ge(m["y_done"], TILES)
            sp.dma_start(rows_of(x2_dram)[TILES - 1], y[:]).then_inc(m["stored"], 16)
            sp.wait_ge(m["stored"], 16 * TILES)
            sp.wait_ge(m["tables_in"], 48)
            sp.wait_ge(m["ternary_in"], 16 * 3 * TILES)

        @block.tensor
        def _(pe):
            def slot(i, s, n):
                b, t = s // NT, s % NT
                bp = 1 - b
                seq = 2 * i + b
                if live(n, 0, ALL):
                    pe.wait_ge(m["c_split"], 2 * i + b + 1)
                    reached(pe, m["k_exped"], n)
                    for part, w in enumerate((wqk_hi, wqk_lo)):
                        last = nc.tensor.matmul(kl[:], w[:, 1, t * P:(t + 1) * P], cs[:, b, :],
                                                start=(part == 0), stop=(part == 1))
                    last.then_inc(m["k_logits"], 1)
                    pe.wait_ge(m["x_split"], 2 * i + b + 1)
                    reached(pe, m["q_shifted"], n - 1)
                    for part, w in enumerate((wqk_hi, wqk_lo)):
                        last = nc.tensor.matmul(ql[:, s % 2, :], xs[:, b, t * P:(t + 1) * P], w[:, 0, :],
                                                start=(part == 0), stop=(part == 1))
                    last.then_inc(m["q_logits"], 1)
                if live(n, 2, ALL):
                    bk, tk = ((s - 2) % SLOTS) // NT, (s - 2) % NT
                    pe.wait_ge(m["kt_copied"], n - 1)
                    if s == 0:
                        pe.wait_ge(m["ct_in"], 16 * i)
                    elif s == 2:
                        pe.wait_ge(m["ct_in"], 16 * i + 16)
                    if tk == 0:
                        reached(pe, m["m_scaled"], seq)
                    for j in range(NT):
                        last = nc.tensor.matmul(gm[0:XD, tk * P:(tk + 1) * P],
                                                c_t[:, j * P + bk * XD:j * P + (bk + 1) * XD],
                                                e_t[:, bk, j, tk * P:(tk + 1) * P],
                                                start=(j == 0), stop=(j == NT - 1))
                    if tk == NT - 1:
                        last.then_inc(m["g_done"], 1)
                if live(n, 1, ALL):
                    pe.wait_ge(m["k_exped"], n)
                    reached(pe, m["kt_copied"], n - 1)
                    for j in range(NT):
                        last = nc.tensor.transpose(trk[:, j * P:(j + 1) * P],
                                                   e_k[:, (s - 1) % 2, j * P:(j + 1) * P], ident[:])
                    last.then_inc(m["k_turned"], 1)
                if live(n, 2, ALL):
                    pe.wait_ge(m["q_normed"], n - 1)
                    reached(pe, m["qt_copied"], n - 2)
                    for j in range(NT):
                        last = nc.tensor.transpose(trp[:, j * P:(j + 1) * P],
                                                   p_q[:, (s - 2) % NQ, j * P:(j + 1) * P], ident[:])
                    last.then_inc(m["q_turned"], 1)
                if t == 1 and live(n, NT, ALL):
                    pe.wait_ge(m["g_copied"], seq)
                    for c in range(NT):
                        last = nc.tensor.matmul(gm[:, c * P:(c + 1) * P], g_t[:, c * P:(c + 1) * P],
                                                u[:, c * P:(c + 1) * P], start=True, stop=True)
                    last.then_inc(m["m_done"], 1)
                if t >= 2 and live(n, NT, ALL):
                    cols = slice((t - 2) * (D // 2), (t - 1) * (D // 2))
                    pe.wait_ge(m["m_scaled"], seq)
                    if t == 2:
                        pe.wait_ge(m["qt_copied"], n - 2)
                    if t == 2 and bp == 0:
                        reached(pe, m["squared"], i)
                    for c in range(NT):
                        last = nc.tensor.matmul(ob[bp * XD:(bp + 1) * XD, cols], m_sb[:, c, :],
                                                p_t[:, bp, c, cols], start=(c == 0), stop=(c == NT - 1))
                    if t == 3:
                        last.then_inc(m["o_done"], 1)
                if s == 4 and live(n, SLOTS, ALL):
                    pe.wait_ge(m["squared"], i)
                    reached(pe, m["attended"], i - 1)
                    for j in range(NT):
                        last = nc.tensor.matmul(nb[:, 2 * j:2 * j + 2], sq[:, j * P:(j + 1) * P], half_of[:],
                                                start=True, stop=True)
                    last.then_inc(m["ss_done"], 1)
                if s == 6 and live(n, SLOTS, ALL):
                    pe.wait_ge(m["rn_done"], i)
                    for j in range(NT):
                        last = nc.tensor.matmul(nb[:, j * P:(j + 1) * P],
                                                rn_wide[:, j, :], ident[:],
                                                start=True, stop=True)
                    last.then_inc(m["rb_done"], 1)

            schedule(pe, slot)

        @block.vector
        def _(dve):
            nc.vector.memset(half8[:], -0.5).then_inc(m["half8_set"], 1)

            def split(i, b):
                rows, other = slice(b * XD, (b + 1) * XD), slice((1 - b) * XD, (2 - b) * XD)
                dve.wait_ge(m["c_hi_done"], 2 * i + b + 1)
                nc.vector.scalar_tensor_tensor(out=cs[other, b, :], in0=c_raw[rows, :], scalar=c_inv[rows, :],
                                               in1=cs[rows, b, :], op0=ALU.mult,
                                               op1=ALU.subtract).then_inc(m["c_split"], 1)

            def slot(i, s, n):
                b, t = s // NT, s % NT
                if s == 0 and live(n, 0, ALL):
                    split(i, 1)
                if live(n, 0, ALL):
                    dve.wait_ge(m["k_logits"], n + 1)
                    reached(dve, m["k_biased"], n)
                    nc.vector.tensor_reduce(k_neg[:], kl[:], AX.X, ALU.max, negate=True).then_inc(m["k_maxed"], 1)
                if live(n, 1, ALL):
                    dve.wait_ge(m["q_exped"], n)
                    reached(dve, m["q_inverted"], n - 1)
                    nc.vector.tensor_reduce(q_sum[:], p_q[:, (s - 1) % NQ, :].rearrange("p (h d) -> p h d", h=XH),
                                            AX.X, ALU.add).then_inc(m["q_summed"], 1)
                if live(n, 0, ALL):
                    dve.wait_ge(m["k_maxed"], n + 1)
                    reached(dve, m["k_exped"], n)
                    nc.vector.tensor_scalar(k_bias[:], k_neg[:], k_scale, None, ALU.mult).then_inc(m["k_biased"], 1)
                    dve.wait_ge(m["q_logits"], n + 1)
                    q3 = ql[:, s % 2, :].rearrange("p (h d) -> p h d", h=XH)
                    reached(dve, m["q_shifted"], n)
                    nc.vector.tensor_reduce(q_max[:], q3, AX.X, ALU.max).then_inc(m["q_maxed"], 1)
                if live(n, 1, ALL):
                    dve.wait_ge(m["q_summed"], n)
                    reached(dve, m["q_normed"], n - 1)
                    nc.vector.reciprocal(q_rcp[:], q_sum[:]).then_inc(m["q_inverted"], 1)
                if live(n, 0, ALL):
                    dve.wait_ge(m["q_maxed"], n + 1)
                    reached(dve, m["q_turned"], n - NQ + 1)
                    nc.vector.tensor_tensor(p_q[:, s % NQ, :].rearrange("p (h d) -> p h d", h=XH), q3,
                                            q_max[:, :, None].to_broadcast([P, XH, XD]),
                                            ALU.subtract).then_inc(m["q_shifted"], 1)
                if t == 1 and live(n, NT, ALL):
                    dve.wait_ge(m["k_exped"], n - 1)
                    reached(dve, m["m_scaled"], 2 * i + b - 1)
                    nc.vector.reciprocal(r_k[:], z_k[:, 1 - b, :]).then_inc(m["r_k_done"], 1)
                if t == 1 and live(n, NT, ALL):
                    seq = 2 * i + b
                    dve.wait_ge(m["m_done"], seq)
                    dve.wait_ge(m["r_k_done"], seq)
                    reached(dve, m["o_done"], seq - 1)
                    for h in range(2):
                        rows = slice(h * XD, (h + 1) * XD)
                        last = nc.vector.tensor_tensor(
                            m_sb[rows, :, :],
                            gm[rows, :].rearrange("p (c o) -> p c o", c=NT)[:, :, h * XD:(h + 1) * XD],
                            r_k[rows, :, None].to_broadcast([XD, NT, XD]), ALU.mult)
                    last.then_inc(m["m_scaled"], 1)
                if s == 4 and live(n, SLOTS, ALL):
                    dve.wait_ge(m["ss_done"], i)
                    reached(dve, m["rn_raw"], i - 1)
                    nc.vector.tensor_scalar(ss[:], nb[:, 0:SLOTS], 1e-24, None, ALU.max).then_inc(m["ss_copied"], 1)
                if s == 5 and live(n, SLOTS, ALL):
                    dve.wait_ge(m["rn_raw"], i)
                    reached(dve, m["rb_done"], i - 1)
                    nc.vector.tensor_copy(rn_wide[:].rearrange("p j (b o) -> p (j b) o", b=2),
                                          rn[:, :, None].to_broadcast([P, SLOTS, XD])).then_inc(m["rn_done"], 1)
                if s == 4 and live(n, 0, ALL - SLOTS):
                    split(i + 1, 0)
                if s == 6 and live(n, SLOTS, ALL):
                    dve.wait_ge(m["rb_done"], i)
                    reached(dve, m["residual"], i - 1)
                    nc.vector.scalar_tensor_tensor(out=y1[:], in0=o_sb[:], scalar=keep["g8"][:], in1=nb[:],
                                                   op0=ALU.mult, op1=ALU.mult).then_inc(m["attended"], 1)
                    dve.wait_ge(m["attended"], i)
                    dve.wait_ge(m["xr_in"], 16 * i)
                    reached(dve, m["y_done"], i - 1)
                    nc.vector.tensor_tensor(z[:], y1[:], x_res[:], ALU.add).then_inc(m["residual"], 1)
                    dve.wait_ge(m["residual"], i)
                    nc.vector.bn_stats(stats[:], z[:]).then_inc(m["chain"], 1)
                    dve.wait_ge(m["chain"], 3 * i - 2)
                    nc.vector.memset(veps[:], EPS)
                    nc.vector.bn_aggr(mv[:], stats[:]).then_inc(m["chain"], 1)
                    dve.wait_ge(m["chain"], 3 * i - 1)
                    nc.vector.tensor_tensor(veps[:], veps[:], mv[:, 1:2], ALU.add).then_inc(m["chain"], 1)
                if s == 7 and live(n, SLOTS, ALL):
                    dve.wait_ge(m["rstd_done"], i)
                    reached(dve, m["stored"], 16 * (i - 1))
                    nc.vector.tensor_scalar(y[:], z[:], mv[:, 0:1], rstd[:], ALU.subtract,
                                            ALU.mult).then_inc(m["y_done"], 1)

            split(0, 0)
            schedule(dve, slot)

        @block.scalar
        def _(act):
            def split(i, b):
                rows = slice(b * XD, (b + 1) * XD)
                act.wait_ge(m["c_in"], 16 * i + 16)
                reached(act, m["k_logits"], i * SLOTS - (NT if b == 0 else 0))
                nc.scalar.activation(cs[rows, b, :], c_raw[rows, :], ACT.Copy,
                                     scale=c_inv[rows, :]).then_inc(m["c_hi_done"], 1)
                act.wait_ge(m["x_in"], 16 * i + 16)
                reached(act, m["q_logits"], i * SLOTS - (NT if b == 0 else 0))
                nc.scalar.activation(xs[rows, b, :], x_raw[rows, :], ACT.Copy).then_inc(m["x_hi_done"], 1)

            def slot(i, s, n):
                b, t = s // NT, s % NT
                if s == 0 and live(n, 0, ALL):
                    split(i, 1)
                if live(n, 0, ALL):
                    act.wait_ge(m["k_biased"], n + 1)
                    reached(act, m["k_turned"], n - 1)
                    if t == 0:
                        reached(act, m["r_k_done"], 2 * i + b - 1)
                    nc.scalar.activation(e_k[:, s % 2, :], kl[:], ACT.Exp, bias=k_bias[:], scale=k_scale,
                                         accum_out=z_k[:, b, t:t + 1]).then_inc(m["k_exped"], 1)
                if t == 1 and live(n, NT, ALL):
                    seq = 2 * i + b
                    act.wait_ge(m["g_done"], seq)
                    reached(act, m["m_done"], seq - 1)
                    nc.scalar.activation(g_t[:], gm[0:XD, :], ACT.Copy).then_inc(m["g_copied"], 1)
                if live(n, 1, ALL):
                    bk, tk = ((s - 1) % SLOTS) // NT, (s - 1) % NT
                    act.wait_ge(m["k_turned"], n)
                    if tk == 0:
                        reached(act, m["g_done"], 2 * i + b - 1)
                    nc.scalar.activation(e_t[:, bk, :, tk * P:(tk + 1) * P],
                                         trk[:].rearrange("p (j r) -> p j r", j=NT),
                                         ACT.Copy).then_inc(m["kt_copied"], 1)
                if live(n, 0, ALL):
                    act.wait_ge(m["q_shifted"], n + 1)
                    nc.scalar.activation(p_q[:, s % NQ, :], p_q[:, s % NQ, :], ACT.Exp,
                                         scale=wq_scale).then_inc(m["q_exped"], 1)
                if live(n, 2, ALL):
                    bq, tq = ((s - 2) % SLOTS) // NT, (s - 2) % NT
                    act.wait_ge(m["q_turned"], n - 1)
                    if tq == 0:
                        reached(act, m["o_done"], 2 * i + b - 1)
                    nc.scalar.activation(p_t[:, bq, :, tq * P:(tq + 1) * P],
                                         trp[:].rearrange("p (c q) -> p c q", c=NT),
                                         ACT.Copy).then_inc(m["qt_copied"], 1)
                if s == 3 and live(n, SLOTS - 1, ALL):
                    act.wait_ge(m["o_done"], 2 * i)
                    reached(act, m["attended"], i - 1)
                    reached(act, m["ss_done"], i - 1)
                    nc.scalar.activation(o_sb[:], ob[:], ACT.Identity, bias=keep["bo"][:])
                    nc.scalar.activation(sq[:], ob[:], ACT.Square, bias=keep["bo"][:]).then_inc(m["squared"], 1)
                if s == 4 and live(n, 0, ALL - SLOTS):
                    split(i + 1, 0)

            split(0, 0)
            schedule(act, slot)

        @block.gpsimd
        def _(pool):
            pool.wait_ge(m["half8_set"], 1)

            def split(i, b, normed):
                rows, other = slice(b * XD, (b + 1) * XD), slice((1 - b) * XD, (2 - b) * XD)
                pool.wait_ge(m["x_hi_done"], 2 * i + b + 1)
                reached(pool, m["q_normed"], normed)
                nc.gpsimd.tensor_tensor(xs[other, b, :], x_raw[rows, :], xs[rows, b, :],
                                        ALU.subtract).then_inc(m["x_split"], 1)
                pool.wait_ge(m["x_split"], 2 * i + b + 1)

            def slot(i, s, n):
                if s == 0 and live(n, 0, ALL):
                    split(i, 1, n - 1)
                if live(n, 1, ALL):
                    pool.wait_ge(m["q_inverted"], n)
                    p3 = p_q[:, (s - 1) % NQ, :].rearrange("p (h d) -> p h d", h=XH)
                    nc.gpsimd.tensor_tensor(p3, p3, q_rcp[:, :, None].to_broadcast([P, XH, XD]),
                                            ALU.mult).then_inc(m["q_normed"], 1)
                if s == 4 and live(n, 0, ALL - SLOTS):
                    split(i + 1, 0, n)
                if s == 4 and live(n, SLOTS, ALL):
                    pool.wait_ge(m["ss_copied"], i)
                    nc.gpsimd.tensor_tensor(rn[:], ss[:], half8[:], ALU.pow).then_inc(m["rn_raw"], 1)
                if s == 6 and live(n, SLOTS, ALL):
                    pool.wait_ge(m["chain"], 3 * i)
                    reached(pool, m["y_done"], i - 1)
                    nc.gpsimd.tensor_tensor(rstd[:], veps[:], keep["neg_half"][:], ALU.pow
                                            ).then_inc(m["rstd_done"], 1)

            split(0, 0, 0)
            schedule(pool, slot)


def ffn_block(nc, ins, keep, x2_dram, out):
    ident, ffn_q = keep["ident"], keep["ffn_q"]
    gate_s, up_s, down_s = keep["gate_s"], keep["up_s"], keep["down_s"]
    w_gate = ffn_q[:, 0].rearrange("p t c -> p (t c)").rearrange("p (k o) -> p k o", k=KT)
    w_up = ffn_q[:, 1].rearrange("p t c -> p (t c)").rearrange("p (k o) -> p k o", k=KT)
    w_down = ffn_q[:, 2].rearrange("p t c -> p (t c)").rearrange("p (k o) -> p k o", k=HT)
    with ExitStack() as ctx:
        sb = lambda name, shape, dt: ctx.enter_context(nc.sbuf_tensor(name, shape, dt))
        ps = lambda name, shape, dt: ctx.enter_context(nc.psum_tensor(name, shape, dt))
        x_in_sb = sb("fx", [P, D], F32)
        x_res = sb("fx_res", [P, D], F32)
        xt_hi = sb("fxt_hi", [P, D], F16)
        xt_lo = sb("fxt_lo", [P, D], F16)
        gate = sb("gate", [P, 2, D], F32)
        up = sb("up", [P, 2, D], F32)
        silu = sb("silu", [P, 2, D], F32)
        h = sb("h", [P, HID], F32)
        hs = sb("hs", [P, HID], F32)
        ht_hi = sb("ht_hi", [P, 2, D], F16)
        ht_lo = sb("ht_lo", [P, 2, D], F16)
        peaks = sb("peaks", [P, FC], F32)
        peak = sb("fpeak", [P, 1], F32)
        power = sb("power", [P, 1], F32)
        inverse = sb("inverse", [P, 1], F32)
        powered = sb("powered", [P, 1], F32)
        d_sb = sb("d_sb", [P, D], F32)
        z = sb("fz", [P, D], F32)
        y = sb("fy", [P, D], F32)
        stats = sb("fstats", [P, 6], F32)
        mv = sb("fmv", [P, 2], F32)
        veps = sb("fveps", [P, 1], F32)
        rstd = sb("frstd", [P, 1], F32)
        tx = ps("tx", [P, D], F32)
        gp = ps("gp", [P, 2, D], F32)
        up_ps = ps("up_ps", [P, 2, D], F32)
        th = ps("th", [P, 2, D], F32)
        dn = ps("dn", [P, D], F32)
        names = ("x_in", "xr_in", "x_turned", "x_hi", "x_split", "gate_up", "gated", "upped", "silu_done", "h_done",
                 "maxed", "peaked", "clamped", "powered", "inverted", "h_scaled", "h_turned", "ht_hi", "ht_split",
                 "down", "unscaled", "residual", "chain", "rstd_done", "y_done", "stored")
        m = {name: ctx.enter_context(nc.semaphore("f_" + name)) for name in names}
        block = ctx.enter_context(nc.Block())
        rows_of = lambda a: a.rearrange("(t p) d -> t p d", p=P)

        def schedule(eng, tile):
            tile(0, True, False, False)
            tile(1, False, False, False)
            with eng.Fori(2, TILES - 1) as i:
                tile(i, False, False, False)
            tile(TILES - 1, False, True, False)
            tile(TILES, False, True, True)

        @block.sync
        def _(sp):
            def store(i):
                sp.wait_ge(m["y_done"], i + 1)
                sp.dma_start(rows_of(out)[i], y[:]).then_inc(m["stored"], 16)

            def residual_rows(i):
                reached(sp, m["residual"], i)
                sp.dma_start(x_res[:], rows_of(x2_dram)[i]).then_inc(m["xr_in"], 16)

            def next_rows(i):
                reached(sp, m["x_turned"], i)
                sp.dma_start(x_in_sb[:], rows_of(x2_dram)[i]).then_inc(m["x_in"], 16)

            next_rows(0)
            next_rows(1)
            residual_rows(0)
            with sp.Fori(2, TILES) as i:
                next_rows(i)
                residual_rows(i - 1)
                store(i - 2)
            residual_rows(TILES - 1)
            store(TILES - 2)
            store(TILES - 1)
            sp.wait_ge(m["stored"], 16 * TILES)

        @block.tensor
        def _(pe):
            def turn_rows(i):
                pe.wait_ge(m["x_in"], 16 * i + 16)
                reached(pe, m["x_split"], i)
                for k in range(KT):
                    last = nc.tensor.transpose(tx[:, k * P:(k + 1) * P], x_in_sb[:, k * P:(k + 1) * P], ident[:])
                last.then_inc(m["x_turned"], 1)

            def tile(i, first, last_tile, past):
                def gate_and_up(c):
                    n = i * FC + c
                    if not (first and c < 2):
                        pe.wait_ge(m["upped"], n - 1)
                    for w, o in ((w_gate, gp), (w_up, up_ps)):
                        for k in range(KT):
                            for part, xs in enumerate((xt_hi, xt_lo)):
                                last = nc.tensor.matmul(o[:, c % 2, :], xs[:, k * P:(k + 1) * P],
                                                        w[:, k, c * D:(c + 1) * D],
                                                        start=(k == 0 and part == 0), stop=(k == KT - 1 and part == 1))
                    last.then_inc(m["gate_up"], 1)

                def turn_hidden(c):
                    n = (i - 1) * FC + c
                    if c == 0:
                        pe.wait_ge(m["h_scaled"], i)
                    reached(pe, m["ht_split"], n - 1)
                    for k in range(4):
                        last = nc.tensor.transpose(th[:, c % 2, k * P:(k + 1) * P],
                                                   hs[:, (c * 4 + k) * P:(c * 4 + k + 1) * P], ident[:])
                    last.then_inc(m["h_turned"], 1)

                def down(c):
                    n = (i - 1) * FC + c
                    pe.wait_ge(m["ht_split"], n + 1)
                    if c == 0:
                        reached(pe, m["unscaled"], i - 1)
                    for k in range(4):
                        for part, hx in enumerate((ht_hi, ht_lo)):
                            last = nc.tensor.matmul(dn[:], hx[:, c % 2, k * P:(k + 1) * P], w_down[:, c * 4 + k, :],
                                                    start=(c == 0 and k == 0 and part == 0),
                                                    stop=(c == FC - 1 and k == 3 and part == 1))
                    last.then_inc(m["down"], 1)

                if not past:
                    pe.wait_ge(m["x_split"], i + 1)
                    gate_and_up(0)
                    gate_and_up(1)
                if not first:
                    turn_hidden(0)
                    turn_hidden(1)
                    down(0)
                    turn_hidden(2)
                    down(1)
                    turn_hidden(3)
                if not past:
                    gate_and_up(2)
                    gate_and_up(3)
                if not last_tile:
                    turn_rows(i + 1)
                if not first:
                    down(2)
                    down(3)

            turn_rows(0)
            schedule(pe, tile)

        @block.vector
        def _(dve):
            def split_low(i):
                dve.wait_ge(m["x_hi"], i + 1)
                nc.vector.tensor_tensor(xt_lo[:], tx[:], xt_hi[:], ALU.subtract).then_inc(m["x_split"], 1)

            def tile(i, first, last_tile, past):
                def scale_chunk(c):
                    n = i * FC + c
                    dve.wait_ge(m["gate_up"], n + 1)
                    if not (first and c < 2):
                        dve.wait_ge(m["h_done"], n - 1)
                    nc.vector.tensor_tensor(gate[:, c % 2, :], gp[:, c % 2, :], gate_s[:, c * D:(c + 1) * D],
                                            ALU.mult).then_inc(m["gated"], 1)
                    nc.vector.tensor_tensor(up[:, c % 2, :], up_ps[:, c % 2, :], up_s[:, c * D:(c + 1) * D],
                                            ALU.mult).then_inc(m["upped"], 1)

                def chunk_peak(c):
                    dve.wait_ge(m["h_done"], i * FC + c + 1)
                    if c == 0:
                        reached(dve, m["peaked"], i)
                    nc.vector.tensor_reduce(peaks[:, c:c + 1], h[:, c * D:(c + 1) * D], AX.X, ALU.max,
                                            apply_absolute_value=True).then_inc(m["maxed"], 1)

                def hidden_low(c):
                    n = (i - 1) * FC + c
                    dve.wait_ge(m["ht_hi"], n + 1)
                    nc.vector.tensor_tensor(ht_lo[:, c % 2, :], th[:, c % 2, :], ht_hi[:, c % 2, :],
                                            ALU.subtract).then_inc(m["ht_split"], 1)

                if not past:
                    scale_chunk(0)
                    scale_chunk(1)
                    chunk_peak(0)
                if not first:
                    for c in range(FC):
                        hidden_low(c)
                if not past:
                    chunk_peak(1)
                    scale_chunk(2)
                    chunk_peak(2)
                    scale_chunk(3)
                if not last_tile:
                    split_low(i + 1)
                if not first:
                    dve.wait_ge(m["down"], i * FC)
                    nc.vector.scalar_tensor_tensor(out=d_sb[:], in0=dn[:], scalar=powered[:], in1=down_s[:],
                                                   op0=ALU.mult, op1=ALU.mult).then_inc(m["unscaled"], 1)
                if not past:
                    chunk_peak(3)
                    dve.wait_ge(m["maxed"], i * FC + FC)
                    nc.vector.tensor_reduce(peak[:], peaks[:], AX.X, ALU.max).then_inc(m["peaked"], 1)
                    dve.wait_ge(m["peaked"], i + 1)
                    nc.vector.tensor_scalar(power[:], peak[:], TINY, None, ALU.max).then_inc(m["clamped"], 1)
                    dve.wait_ge(m["clamped"], i + 1)
                    nc.vector.tensor_scalar(powered[:].bitcast(I32), power[:].bitcast(I32), EXP_BITS, None,
                                            ALU.bitwise_and).then_inc(m["powered"], 1)
                    dve.wait_ge(m["powered"], i + 1)
                    nc.vector.reciprocal(inverse[:], powered[:]).then_inc(m["inverted"], 1)
                if not first:
                    dve.wait_ge(m["unscaled"], i)
                    dve.wait_ge(m["xr_in"], 16 * i)
                    reached(dve, m["y_done"], i - 1)
                    nc.vector.tensor_tensor(z[:], d_sb[:], x_res[:], ALU.add).then_inc(m["residual"], 1)
                    dve.wait_ge(m["residual"], i)
                    nc.vector.bn_stats(stats[:], z[:]).then_inc(m["chain"], 1)
                    dve.wait_ge(m["chain"], 3 * i - 2)
                    nc.vector.memset(veps[:], EPS)
                    nc.vector.bn_aggr(mv[:], stats[:]).then_inc(m["chain"], 1)
                    dve.wait_ge(m["chain"], 3 * i - 1)
                    nc.vector.tensor_tensor(veps[:], veps[:], mv[:, 1:2], ALU.add).then_inc(m["chain"], 1)
                    dve.wait_ge(m["rstd_done"], i)
                    reached(dve, m["stored"], 16 * (i - 1))
                    nc.vector.tensor_scalar(y[:], z[:], mv[:, 0:1], rstd[:], ALU.subtract,
                                            ALU.mult).then_inc(m["y_done"], 1)

            split_low(0)
            schedule(dve, tile)

        @block.scalar
        def _(act):
            def split_high(i):
                act.wait_ge(m["x_turned"], i + 1)
                reached(act, m["gate_up"], i * FC)
                nc.scalar.activation(xt_hi[:], tx[:], ACT.Copy).then_inc(m["x_hi"], 1)

            def tile(i, first, last_tile, past):
                def silu_chunk(c):
                    n = i * FC + c
                    act.wait_ge(m["gated"], n + 1)
                    nc.scalar.activation(silu[:, c % 2, :], gate[:, c % 2, :], ACT.Silu).then_inc(m["silu_done"], 1)

                if not past:
                    silu_chunk(0)
                    silu_chunk(1)
                if not first:
                    for c in range(FC):
                        n = (i - 1) * FC + c
                        act.wait_ge(m["h_turned"], n + 1)
                        reached(act, m["down"], n - 1)
                        nc.scalar.activation(ht_hi[:, c % 2, :], th[:, c % 2, :], ACT.Copy).then_inc(m["ht_hi"], 1)
                if not past:
                    silu_chunk(2)
                if not last_tile:
                    split_high(i + 1)
                if not past:
                    silu_chunk(3)
                    act.wait_ge(m["inverted"], i + 1)
                    reached(act, m["h_turned"], i * FC)
                    nc.scalar.activation(hs[:], h[:], ACT.Copy, scale=inverse[:]).then_inc(m["h_scaled"], 1)

            split_high(0)
            schedule(act, tile)

        @block.gpsimd
        def _(pool):
            def tile(i, first, last_tile, past):
                def hidden(c):
                    n = i * FC + c
                    pool.wait_ge(m["silu_done"], n + 1)
                    pool.wait_ge(m["upped"], n + 1)
                    if c == 0:
                        reached(pool, m["h_scaled"], i)
                    nc.gpsimd.tensor_tensor(h[:, c * D:(c + 1) * D], silu[:, c % 2, :], up[:, c % 2, :],
                                            ALU.mult).then_inc(m["h_done"], 1)

                if not past:
                    hidden(0)
                    hidden(1)
                if not past:
                    hidden(2)
                    hidden(3)
                if not first:
                    pool.wait_ge(m["chain"], 3 * i)
                    reached(pool, m["y_done"], i - 1)
                    nc.gpsimd.tensor_tensor(rstd[:], veps[:], keep["neg_half"][:], ALU.pow
                                            ).then_inc(m["rstd_done"], 1)

            schedule(pool, tile)


def decoder_layer(nc, ins, out):
    x1_dram = nc.dram_tensor("x1_scratch", [TOK, D], F32, kind="Internal").ap()
    q_dram = nc.dram_tensor("ternary_scratch", [3, TILES, P, D], I32, kind="Internal").ap()
    x2_dram = nc.dram_tensor("x2_scratch", [TOK, D], F32, kind="Internal").ap()
    with ExitStack() as whole:
        keep = {}

        def hold(stack, name, shape, dt):
            keep[name] = stack.enter_context(nc.sbuf_tensor("keep_" + name, shape, dt))

        hold(whole, "ident", [P, P], F32)
        hold(whole, "neg_half", [P, 1], F32)
        hold(whole, "xfac", [P, 7], F32)
        hold(whole, "wqk_hi", [P, 2, XH * XD], F16)
        hold(whole, "wqk_lo", [P, 2, XH * XD], F16)
        hold(whole, "u", [XD, XH * XD], F32)
        hold(whole, "bo", [P, 1], F32)
        hold(whole, "g8", [P, 1], F32)
        hold(whole, "half_of", [P, 2], F32)
        with ExitStack() as first:
            hold(first, "fac", [P, 12], F32)
            hold(first, "cos", [P, HD], F32)
            hold(first, "sin", [P, HD], F32)
            hold(first, "mask", [P, S], F32)
            hold(first, "weights", [P, GROUPS, KT, 2, WC], F16)
            prepare_block(nc, ins, keep)
            attention_block(nc, ins, keep, x1_dram, q_dram)
        hold(whole, "ffn_q", [P, 3, TILES, 2 * D], BF16)
        hold(whole, "gate_s", [P, HID], F32)
        hold(whole, "up_s", [P, HID], F32)
        hold(whole, "down_s", [P, D], F32)
        cross_block(nc, ins, keep, x1_dram, q_dram, x2_dram)
        ffn_block(nc, ins, keep, x2_dram, out)


def shape_constants():
    inv_freq = (1.0 / np.float32(10000.0) ** (np.arange(0, HD, 2, dtype=np.float32) / np.float32(HD)))
    freqs = np.arange(S, dtype=np.float32)[:, None] * inv_freq.astype(np.float32)
    emb = np.concatenate([freqs, freqs], axis=-1)
    sign = np.where(np.arange(HD) < HD // 2, -1.0, 1.0).astype(np.float32)
    cos, sin = np.cos(emb).astype(np.float32), np.sin(emb).astype(np.float32) * sign
    mask = np.where(np.tril(np.ones((S, S), bool)), 0.0, -3e38).astype(np.float32)
    half_of = np.repeat(np.eye(2, dtype=np.float32), XD, axis=0)
    two = lambda a: np.concatenate([a, a], axis=0)
    return {"cos": two(cos), "sin": two(sin), "mask": two(mask), "ident": np.eye(P, dtype=np.float32),
            "half_of": half_of}


def kernel(**inputs):
    import concourse.bacc as bacc
    from concourse.bass_utils import run_bass_kernel_spmd

    a = {k: np.asarray(v) for k, v in inputs.items()}

    def by_group(q, k, v, o, rows):
        return np.concatenate([q.reshape(KT, rows, GROUPS, QC).transpose(2, 0, 1, 3),
                               k.reshape(KT, rows, GROUPS, HD).transpose(2, 0, 1, 3),
                               v.reshape(KT, rows, GROUPS, HD).transpose(2, 0, 1, 3),
                               o.reshape(GROUPS, GH, rows, D)], axis=-1)

    def by_tile(w, tiles):
        flat = w.reshape(tiles, P, -1).transpose(1, 0, 2).reshape(P, TILES, -1)
        return flat.transpose(1, 0, 2)

    x = a["x"].reshape(TOK, D)
    c = a["ctx_4096"].reshape(TOK, D)
    columns = lambda m: m.reshape(TILES, P, KT, P).transpose(0, 3, 2, 1).reshape(TILES, P, KT * P)
    arrays = {
        "x_rows": x, "x_t": columns(x), "c_rows": c, "c_t": columns(c),
        "w_int": by_group(*(a["L0_attn_qw_" + n] for n in "qkvo"), P),
        "scales": by_group(*(a["L0_attn_scales_" + n] for n in "qkvo"), 1).reshape(GROUPS * KT, WC),
        "wq_t": a["L0_xattn_Wq"].T, "wk_t": a["L0_xattn_Wk"].T,
        "wv": a["L0_xattn_Wv"].reshape(XH, XD, XD).transpose(1, 0, 2).reshape(XD, XH * XD),
        "wo": a["L0_xattn_Wo"].reshape(XD, XH, XD).transpose(2, 1, 0).reshape(XD, XH * XD),
        "bo": a["L0_xattn_bo"].reshape(XD, 1), "g": a["L0_xattn_g"].reshape(XD, 1),
        "ffn_w": np.stack([by_tile(a["L0_ffn_gate_w"].T, KT), by_tile(a["L0_ffn_up_w"].T, KT),
                           by_tile(a["L0_ffn_down_w"].T, HT)]),
        "gate_s": a["L0_ffn_gate_scale"].reshape(1, HID), "up_s": a["L0_ffn_up_scale"].reshape(1, HID),
        "down_s": a["L0_ffn_down_scale"].reshape(1, D),
        **shape_constants(),
    }
    nc = bacc.Bacc("TRN2", target_bir_lowering=False, num_devices=1)
    feeds, ins = {}, {}
    for name, array in arrays.items():
        array = np.ascontiguousarray(array)
        feeds[f"in_{name}"] = array
        ins[name] = nc.dram_tensor(f"in_{name}", array.shape, mybir.dt.from_np(array.dtype), kind="ExternalInput").ap()
    out = nc.dram_tensor("out", (TOK, D), F32, kind="ExternalOutput").ap()
    decoder_layer(nc, ins, out)
    result = run_bass_kernel_spmd(nc, [feeds], core_ids=[0])
    return np.asarray(result.results[0]["out"]).reshape(B, S, D)
```

```python
from contextlib import ExitStack

import numpy as np
import concourse.bass as bass
from concourse import mybir

F32, F16, BF16, I32 = mybir.dt.float32, mybir.dt.float16, mybir.dt.bfloat16, mybir.dt.int32
ALU = mybir.AluOpType
ACT = mybir.ActivationFunctionType
AX = mybir.AxisListType
RMAX = bass.bass_isa.ReduceOp.absmax
RADD = bass.bass_isa.ReduceOp.add

P = 128
B, S, D = 16, 64, 512
TOK = B * S
TILES = TOK // P
KT = D // P
HD = 128
HEADS, KV = 32, 8
GROUPS = KV
GH = HEADS // KV
QC = GH * HD
QK = QC + HD
PC = QC + 2 * HD
WC = PC + D
STEPS = TILES * GROUPS
XH, XD = 8, 64
HID = 2048
HT = HID // P
FC = HID // D
EXP_BITS = 0x7F800000
TINY = 1e-30
EPS = 1e-5


def reached(eng, sem, count):
    if not isinstance(count, int) or count > 0:
        eng.wait_ge(sem, count)


def live(n, lag, steps):
    return not isinstance(n, int) or 0 <= n - lag < steps


def prepare_block(nc, ins, keep):
    w_int, weights, fac, xf = ins["w_int"], keep["weights"], keep["fac"], keep["xfac"]
    NW = KT
    NI = 2 * KT
    PAIRS = GROUPS // 2
    POOL_K = KT - 1
    UNITS = GROUPS * KT
    part_rows = [slice(k * UNITS, (k + 1) * UNITS) for k in range(3)]
    blocks = [(0, QC), (QC, QK), (QK, PC), (PC, WC)]
    with ExitStack() as ctx:
        sb = lambda name, shape, dt: ctx.enter_context(nc.sbuf_tensor(name, shape, dt))
        sem = lambda name: ctx.enter_context(nc.semaphore(name))
        w32 = sb("w32", [P, NW, WC], F32)
        sc = w32[:, NW - 1, :]
        parts = sb("parts", [P, WC], BF16)
        pick = sb("pick", [P, UNITS], BF16)
        wqk = sb("wqk", [P, 2, XH * XD], F32)
        wv = sb("wv", [XD, XH * XD], F32)
        wo = keep["u"]
        rows = [keep["x_raw"], keep["c_raw"]]
        row_peaks = sb("row_peaks", [P, TILES], F32)
        peak = sb("peak", [P, 8], F32)
        gpeak = sb("gpeak", [P, 8], F32)
        scale_ps = [ctx.enter_context(nc.psum_tensor(f"scale_ps{k}", [P, 1536], F32)) for k in range(2)]
        u_ps = ctx.enter_context(nc.psum_tensor("u_ps", [XD, XH * XD], F32))
        w_in = [sem(f"w_in{k}") for k in range(NI)]
        rows_in = [sem(f"rows_in{k}") for k in range(2)]
        sc_in, const_in, ident_in, wqk_in, small_in = (sem(s) for s in ("sc_in", "const_in", "ident_in", "wqk_in",
                                                                       "small_in"))
        cleared, sc_ready, spread, scaled, hi_done, lo_pool, lo_dve = (sem(s) for s in (
            "cleared", "sc_ready", "spread", "scaled", "hi_done", "lo_pool", "lo_dve"))
        peaked, all_peaked, step_done, row_peaked, folded, x_scaled, xt_hi_done = (sem(s) for s in (
            "peaked", "all_peaked", "step_done", "row_peaked", "folded", "x_scaled", "first_xt_hi_done"))
        block = ctx.enter_context(nc.Block())

        def landing(g, k):
            return weights[:, g, k].rearrange("p r c -> p (r c)").bitcast(I32)

        @block.sync
        def _(sp):
            def unit(q, half, k, first):
                g = 2 * q + half
                if not first:
                    sp.wait_ge(scaled, g * KT + k - NI + 1)
                sp.dma_start(landing(g, k), w_int[g, k]).then_inc(w_in[half * KT + k], 16)

            def row_loads(q, half, first):
                g = 2 * q + half
                if not first:
                    sp.wait_ge(row_peaked, g - 1)
                sp.dma_start(rows[half][:], ins["x_rows"].rearrange("(t p) d -> t p d", p=P)[g]
                             ).then_inc(rows_in[half], 16)

            for rows_ in part_rows:
                sp.dma_start(sc[rows_, :], ins["scales"]).then_inc(sc_in, 16)
            unit(0, 0, 0, True)
            row_loads(0, 0, True)
            for k in range(1, KT):
                unit(0, 0, k, True)
            row_loads(0, 1, True)
            for k in range(KT):
                unit(0, 1, k, True)
            with sp.Fori(1, PAIRS) as q:
                for half in range(2):
                    row_loads(q, half, False)
                    for k in range(KT):
                        unit(q, half, k, False)

        @block.tensor
        def _(pe):
            def unit(g, k, first):
                if not first:
                    pe.wait_ge(scaled, g * KT + k - 1)
                column = pick[:, bass.ds(g * KT + k, 1)].to_broadcast([P, P])
                for a in range(0, WC, 512):
                    b = min(a + 512, WC)
                    last = nc.tensor.matmul(scale_ps[k % 2][:, a:b], column, parts[:, a:b], start=True, stop=True)
                last.then_inc(spread, 1)

            pe.wait_ge(sc_ready, 1)
            for k in range(KT):
                unit(0, k, k < 2)
            pe.wait_ge(small_in, 7 * 16)
            for h in range(XH):
                cols = slice(h * XD, (h + 1) * XD)
                last = nc.tensor.matmul(u_ps[:, cols], wv[:, cols], wo[:, cols], start=True, stop=True)
            last.then_inc(folded, 1)
            with pe.Fori(1, GROUPS) as g:
                for k in range(KT):
                    unit(g, k, False)

        @block.vector
        def _(dve):
            done = [0]

            def chain(ins_):
                done[0] += 1
                ins_.then_inc(step_done, 1)
                dve.wait_ge(step_done, done[0])

            def powers(cols, dst, inverse):
                chain(nc.vector.tensor_scalar(dst.bitcast(I32), gpeak[:, cols].bitcast(I32), EXP_BITS, None,
                                              ALU.bitwise_and))
                chain(nc.vector.reciprocal(inverse, dst))

            def unit(q, half, k, first):
                g = 2 * q + half
                dve.wait_ge(w_in[half * KT + k], q * 16 + 16)
                dve.wait_ge(spread, g * KT + k + 1)
                if not first:
                    dve.wait_ge(hi_done, g * KT + k - NW + 1)
                    if k < POOL_K:
                        dve.wait_ge(lo_pool, (g - 1) * POOL_K + k + 1)
                    else:
                        dve.wait_ge(lo_dve, g)
                nc.vector.scalar_tensor_tensor(out=w32[:, k, :], in0=landing(g, k), scalar=-8.0,
                                               in1=scale_ps[k % 2][:, 0:WC], op0=ALU.add,
                                               op1=ALU.mult).then_inc(scaled, 1)

            def low_part(g):
                k = POOL_K
                dve.wait_ge(hi_done, g * KT + k + 1)
                nc.vector.tensor_tensor(weights[:, g, k, 1, :], w32[:, k, :], weights[:, g, k, 0, :],
                                        ALU.subtract).then_inc(lo_dve, 1)

            def row_peak(q, half):
                g = 2 * q + half
                dve.wait_ge(rows_in[half], q * 16 + 16)
                nc.vector.tensor_reduce(row_peaks[:, bass.ds(g, 1)], rows[half][:], AX.X, ALU.max,
                                        apply_absolute_value=True).then_inc(row_peaked, 1)

            def group(q, half):
                unit(q, half, 0, False)
                low_part(2 * q + half - 1)
                row_peak(q, half)
                for k in range(1, KT):
                    unit(q, half, k, False)

            free = slice(3 * UNITS, P)
            nc.vector.memset(sc[free, :], 0.0).then_inc(cleared, 1)
            dve.wait_ge(cleared, 1)
            dve.wait_ge(sc_in, 48)
            for k, (a, b) in enumerate(blocks):
                chain(nc.vector.tensor_reduce(peak[:, k:k + 1], sc[:, a:b], AX.X, ALU.max, apply_absolute_value=True))
            nc.vector.tensor_scalar(peak[:, 0:4], peak[:, 0:4], TINY, None, ALU.max).then_inc(peaked, 1)
            dve.wait_ge(ident_in, 16)
            chain(nc.vector.tensor_reduce(pick[:], keep["ident"][:, 0:3 * UNITS].rearrange("p (k r) -> p r k", k=3),
                                          AX.X, ALU.max))
            dve.wait_ge(all_peaked, 1)
            powers(slice(0, 4), fac[:, 0:4], fac[:, 5:9])
            for k, (a, b) in enumerate(blocks):
                chain(nc.vector.tensor_scalar(sc[:, a:b], sc[:, a:b], fac[:, 5 + k:6 + k], None, ALU.mult))
            chain(nc.vector.tensor_copy(parts[:], sc))
            chain(nc.vector.tensor_tensor(sc, sc, parts[:], ALU.subtract))
            for k in range(1, 3):
                chain(nc.vector.tensor_copy(parts[part_rows[k], :], sc[part_rows[k], :]))
            third = part_rows[2]
            chain(nc.vector.tensor_tensor(sc[third, :], sc[third, :], parts[third, :], ALU.subtract))
            chain(nc.vector.tensor_copy(parts[third, :], sc[third, :]))
            nc.vector.memset(keep["neg_half"][:], -0.5).then_inc(sc_ready, 1)
            row_peak(0, 0)
            for k in range(KT):
                unit(0, 0, k, True)
            dve.wait_ge(wqk_in, 64)
            for k in range(2):
                chain(nc.vector.tensor_reduce(peak[:, 4 + k:5 + k], wqk[:, k, :], AX.X, ALU.max,
                                              apply_absolute_value=True))
            nc.vector.tensor_scalar(peak[:, 4:6], peak[:, 4:6], TINY, None, ALU.max).then_inc(peaked, 1)
            group(0, 1)
            dve.wait_ge(all_peaked, 2)
            powers(slice(4, 6), xf[:, 0:2], xf[:, 3:5])
            for k in range(2):
                chain(nc.vector.tensor_scalar(wqk[:, k, :], wqk[:, k, :], xf[:, 3 + k:4 + k], None, ALU.mult))
                chain(nc.vector.tensor_copy(keep["wqk_hi"][:, k, :], wqk[:, k, :]))
                chain(nc.vector.tensor_tensor(keep["wqk_lo"][:, k, :], wqk[:, k, :], keep["wqk_hi"][:, k, :],
                                              ALU.subtract))
            dve.wait_ge(small_in, 7 * 16)
            chain(nc.vector.tensor_scalar(keep["g8"][:], keep["g8"][:], float(XD) ** 0.5, None, ALU.mult))
            dve.wait_ge(folded, 1)
            chain(nc.vector.tensor_scalar(keep["u"][:], u_ps[:], float(XD) ** -0.5, None, ALU.mult))
            with dve.Fori(1, PAIRS) as q:
                for half in range(2):
                    group(q, half)
            dve.wait_ge(row_peaked, TILES)
            chain(nc.vector.tensor_reduce(peak[:, 6:7], row_peaks[:], AX.X, ALU.max))
            nc.vector.tensor_scalar(peak[:, 6:7], peak[:, 6:7], TINY, None, ALU.max).then_inc(peaked, 1)
            low_part(GROUPS - 1)
            dve.wait_ge(all_peaked, 3)
            chain(nc.vector.tensor_scalar(fac[:, 4:5].bitcast(I32), gpeak[:, 6:7].bitcast(I32), EXP_BITS, None,
                                          ALU.bitwise_and))
            nc.vector.reciprocal(fac[:, 9:10], fac[:, 4:5]).then_inc(x_scaled, 1)
            chain(nc.vector.tensor_tensor(fac[:, 10:11], fac[:, 0:1], fac[:, 1:2], ALU.mult))
            chain(nc.vector.tensor_tensor(fac[:, 10:11], fac[:, 10:11], fac[:, 4:5], ALU.mult))
            chain(nc.vector.tensor_tensor(fac[:, 10:11], fac[:, 10:11], fac[:, 4:5], ALU.mult))
            chain(nc.vector.tensor_scalar(fac[:, 10:11], fac[:, 10:11], float(HD) ** -0.5, None, ALU.mult))
            chain(nc.vector.tensor_tensor(fac[:, 11:12], fac[:, 2:3], fac[:, 3:4], ALU.mult))
            chain(nc.vector.tensor_tensor(fac[:, 11:12], fac[:, 11:12], fac[:, 4:5], ALU.mult))
            dve.wait_ge(xt_hi_done, 1)
            chain(nc.vector.scalar_tensor_tensor(out=keep["xt_lo"][:], in0=keep["xt32"][:], scalar=fac[:, 9:10],
                                                 in1=keep["xt_hi"][:], op0=ALU.mult, op1=ALU.subtract))
            dve.wait_ge(lo_dve, GROUPS)

        @block.scalar
        def _(act):
            act.dma_start(keep["ident"][:], ins["ident"]).then_inc(ident_in, 16)
            for half in range(2):
                part = slice(half * XD, (half + 1) * XD)
                act.dma_start(wqk[part, 0, :], ins["wq_t"]).then_inc(wqk_in, 16)
                act.dma_start(wqk[part, 1, :], ins["wk_t"]).then_inc(wqk_in, 16)
                act.dma_start(keep["bo"][part, :], ins["bo"]).then_inc(small_in, 16)
                act.dma_start(keep["g8"][part, :], ins["g"]).then_inc(small_in, 16)
            act.dma_start(wv[:], ins["wv"]).then_inc(small_in, 16)
            act.dma_start(wo[:], ins["wo"]).then_inc(small_in, 16)
            act.dma_start(keep["half_of"][:], ins["half_of"]).then_inc(small_in, 16)
            act.dma_start(keep["cos"][:], ins["cos"]).then_inc(const_in, 16)
            act.dma_start(keep["sin"][:], ins["sin"]).then_inc(const_in, 16)
            act.dma_start(keep["mask"][:], ins["mask"]).then_inc(const_in, 16)
            act.dma_start(keep["xt32"][:], ins["x_t"][0]).then_inc(const_in, 16)

            def unit(g, k):
                act.wait_ge(scaled, g * KT + k + 1)
                nc.scalar.activation(weights[:, g, k, 0, :], w32[:, k, :], ACT.Copy).then_inc(hi_done, 1)

            for k in range(KT):
                unit(0, k)
            with act.Fori(1, GROUPS) as g:
                for k in range(KT):
                    unit(g, k)
            act.wait_ge(const_in, 64)
            act.wait_ge(x_scaled, 1)
            nc.scalar.activation(keep["xt_hi"][:], keep["xt32"][:], ACT.Copy, scale=fac[:, 9:10]
                                 ).then_inc(xt_hi_done, 1)

        @block.gpsimd
        def _(pool):
            def low_parts(g):
                for k in range(POOL_K):
                    pool.wait_ge(hi_done, g * KT + k + 1)
                    nc.gpsimd.tensor_tensor(weights[:, g, k, 1, :], w32[:, k, :], weights[:, g, k, 0, :],
                                            ALU.subtract).then_inc(lo_pool, 1)

            def all_peak(cols, count):
                pool.wait_ge(peaked, count)
                nc.gpsimd.partition_all_reduce(gpeak[:, cols], peak[:, cols], P, RMAX).then_inc(all_peaked, 1)

            all_peak(slice(0, 4), 1)
            low_parts(0)
            all_peak(slice(4, 6), 2)
            with pool.Fori(1, GROUPS) as g:
                low_parts(g)
            all_peak(slice(6, 7), 3)


def attention_block(nc, ins, keep, x1_dram, q_dram):
    fac, xf = keep["fac"], keep["xfac"]
    w_hi, w_lo = (keep["weights"][:, :, :, part, :] for part in range(2))
    cos, sin, mask, ident = keep["cos"], keep["sin"], keep["mask"], keep["ident"]
    x_t, x_rows, ffn_w = ins["x_t"], ins["x_rows"], ins["ffn_w"]
    alpha, beta, x_inv = fac[:, 10:11], fac[:, 11:12], fac[:, 9:10]
    NV = 4
    HALF = HD // 2
    SUM_TILES = 3
    QUANT_FROM = TILES // 2
    ROW_TILES = TILES // (TILES - QUANT_FROM)
    QUANT_STEPS = 3 * ROW_TILES
    SUM_CHUNKS = SUM_TILES * GROUPS * 2
    BEFORE = SUM_CHUNKS + TILES

    def quant_unit(i, g):
        return (i - QUANT_FROM) * QUANT_STEPS + g

    with ExitStack() as ctx:
        sb = lambda name, shape, dt: ctx.enter_context(nc.sbuf_tensor(name, shape, dt))
        ps = lambda name, shape, dt: ctx.enter_context(nc.psum_tensor(name, shape, dt))
        sem = lambda name: ctx.enter_context(nc.semaphore(name))
        xt32, xt_hi, xt_lo = (keep[k] for k in ("xt32", "xt_hi", "xt_lo"))
        x_res = sb("x_res", [P, D], F32)
        by_cos = sb("by_cos", [P, QK], F32)
        by_sin = sb("by_sin", [P, QK], F32)
        rot = sb("rot", [P, QK], F32)
        qk_hi = sb("qk_hi", [P, QK], F16)
        qk_lo = sb("qk_lo", [P, QK], F16)
        v_two = sb("v_two", [P, NV, 2, HD], F32)
        probs = sb("probs", [P, GH * S], F32)
        probs_t = sb("probs_t", [P, 2, P], F32)
        c_hi = sb("c_hi", [P, 2, GH * P], F16)
        c_lo = sb("c_lo", [P, 2, GH * P], F16)
        neg_max = sb("neg_max", [P, GH], F32)
        psum_row = sb("psum_row", [P, GH], F32)
        rcp = sb("rcp", [P, GH], F32)
        z, stored = keep["x1_out"], keep["x1_stored"]
        stats = sb("stats", [P, 6], F32)
        mv = sb("mv", [P, 2], F32)
        veps = sb("veps", [P, 1], F32)
        rstd = sb("rstd", [P, 1], F32)
        ffn_in = sb("ffn_in", [P, 2, D], F32)
        below = sb("below", [P, D], BF16)
        q_out = sb("q_out", [P, 2, D], BF16)
        abs_sums = sb("abs_sums", [P, 3, 2 * TILES], F32)
        asum = sb("asum", [P, 3], F32)
        gsum = sb("gsum", [P, 3], F32)
        thr = sb("thr", [P, 6], F32)
        c_peaks = sb("c_peaks", [P, TILES], F32)
        c_peak = sb("c_peak", [P, 1], F32)
        c_gpeak = sb("c_gpeak", [P, 1], F32)
        pj = ps("pj", [P, 1024], F32)
        tr = ps("tr", [P, 2 * P], F32)
        sp_ = ps("scores_ps", [P, 512], F32)
        pv = ps("pv", [P, 2, 512], F32)
        oacc = ps("oacc", [P, 512], F32)

        xt_in, xr_in, ffn_sem = sem("xt_in"), sem("xr_in"), [sem("ffn_in0"), sem("ffn_in1")]
        xt_hi_done, xt_split = sem("xt_hi_done"), sem("xt_split")
        projected, scored, p_turned, weighed, o_done = (sem(s) for s in (
            "projected", "scored", "p_turned", "weighed", "o_done"))
        roped, masked, maxed, inverted, c_lo_done, residual = (sem(s) for s in (
            "roped", "masked", "maxed", "inverted", "c_lo_done", "residual"))
        rotated, normed, rstd_done = sem("rotated"), sem("normed"), sem("rstd_done")
        v_copied, qk_hi_done, qk_split, exped, pt_copied, c_hi_done = (sem(s) for s in (
            "v_copied", "qk_hi_done", "qk_split", "exped", "pt_copied", "c_hi_done"))
        ln_chain, y_done = sem("ln_chain"), sem("y_done")
        chunk_used, summed, all_summed, thr_done, below_done, c_chain, c_peaked, c_all_peaked = (sem(s) for s in (
            "chunk_used", "summed", "all_summed", "thr_done", "below_done", "c_chain", "c_peaked", "c_all_peaked"))
        q_stored, cross_in = [sem("q_stored0"), sem("q_stored1")], sem("cross_in")
        block = ctx.enter_context(nc.Block())

        def schedule(eng, step, loops):
            def tile(i, number):
                phase = ("sum" if number < SUM_TILES else "threshold" if number == SUM_TILES else
                         "wait" if number < QUANT_FROM else "quantise")
                for g in range(GROUPS):
                    step(i, g, i * GROUPS + g, phase)

            at = 0
            for a, b in loops:
                for i in range(at, a):
                    tile(i, i)
                with eng.Fori(a, b) as i:
                    tile(i, a)
                at = b
            for i in range(at, TILES):
                tile(i, i)
            for g in range(4):
                step(TILES, g, STEPS + g, "past")

        SUMMING, QUANTISING = (1, SUM_TILES), (QUANT_FROM + 1, TILES - 1)

        @block.sync
        def _(sp):
            def columns_in(i):
                reached(sp, xt_split, i - 1)
                sp.dma_start(xt32[:], x_t[i]).then_inc(xt_in, 16)

            def rows(i, last):
                if not last:
                    columns_in(i + 1)
                reached(sp, residual, i)
                sp.dma_start(x_res[:], x_rows.rearrange("(t p) d -> t p d", p=P)[i]).then_inc(xr_in, 16)

            def store(i):
                sp.wait_ge(y_done, i + 1)
                sp.dma_start(x1_dram.rearrange("(t p) d -> t p d", p=P)[i], z[:]).then_inc(stored, 16)

            def chunk_in(columns, half, before):
                reached(sp, chunk_used, before - 1)
                sp.dma_start(ffn_in[:, half, :], columns).then_inc(ffn_sem[half], 16)

            def sum_tile(i):
                for g in range(GROUPS):
                    for half in range(2):
                        chunk_in(ffn_w[i, g, :, half * D:(half + 1) * D], half, (i * GROUPS + g) * 2 + half)
                    if g == GROUPS // 2:
                        rows(i, False)

            def quant_tile(i, last):
                for g in range(QUANT_STEPS):
                    unit, quarter = quant_unit(i, g), i - QUANT_FROM
                    of_step = lambda w: w.rearrange("m (q r) p c -> m q r p c", r=ROW_TILES)[
                        g // ROW_TILES, quarter, g % ROW_TILES]
                    for half in range(2):
                        chunk_in(of_step(ffn_w)[:, half * D:(half + 1) * D], half, unit * 2 + BEFORE + half)
                    for half in range(2):
                        sp.wait_ge(chunk_used, unit * 2 + BEFORE + half + 1)
                        sp.dma_start(of_step(q_dram)[:, half * D // 2:(half + 1) * D // 2],
                                     q_out[:, half, :].bitcast(I32)).then_inc(q_stored[half], 16)
                    if g == QUANT_STEPS // 2:
                        rows(i, last)

            sum_tile(0)
            with sp.Fori(*SUMMING) as i:
                sum_tile(i)
                store(i - 1)
            for t in range(TILES):
                chunk_in(ins["c_rows"].rearrange("(t p) d -> t p d", p=P)[t], t % 2, SUM_CHUNKS + t)
            for i in range(SUM_TILES, QUANT_FROM):
                rows(i, False)
                store(i - 1)
            quant_tile(QUANT_FROM, False)
            store(QUANT_FROM - 1)
            with sp.Fori(*QUANTISING) as i:
                quant_tile(i, False)
                store(i - 1)
            quant_tile(TILES - 1, True)
            store(TILES - 2)
            sp.wait_ge(stored, 16 * (TILES - 1))
            sp.dma_start(keep["x_raw"][:], x1_dram.rearrange("(t p) d -> t p d", p=P)[0]).then_inc(cross_in, 16)
            sp.dma_start(keep["c_raw"][:], ins["c_rows"].rearrange("(t p) d -> t p d", p=P)[0]).then_inc(cross_in, 16)
            store(TILES - 1)
            sp.wait_ge(cross_in, 32)
            for half in range(2):
                sp.wait_ge(q_stored[half], 16 * 3 * TILES)

        @block.tensor
        def _(pe):
            def step(i, g, n, phase):
                if live(n, 0, STEPS):
                    if g == 0:
                        reached(pe, xt_split, i)
                    reached(pe, roped, n)
                    reached(pe, v_copied, n)
                    for h in range(GH + 1):
                        cols = slice(h * HD, (h + 1) * HD)
                        for k in range(KT):
                            for part, (xs, w) in enumerate(((xt_hi, w_hi), (xt_hi, w_lo), (xt_lo, w_hi))):
                                nc.tensor.matmul(pj[:, cols], w[:, g, k, cols], xs[:, k * P:(k + 1) * P],
                                                 start=(k == 0 and part == 0), stop=(k == KT - 1 and part == 2))
                    for k in range(KT):
                        for part, (xs, w) in enumerate(((xt_hi, w_hi), (xt_hi, w_lo), (xt_lo, w_hi))):
                            last = nc.tensor.matmul(pj[:, QK:PC], xs[:, k * P:(k + 1) * P], w[:, g, k, QK:PC],
                                                    start=(k == 0 and part == 0), stop=(k == KT - 1 and part == 2))
                    last.then_inc(projected, 1)
                if live(n, 2, STEPS):
                    pe.wait_ge(normed, n - 1)
                    reached(pe, pt_copied, n - 2)
                    for c in range(2):
                        last = nc.tensor.transpose(tr[:, c * P:(c + 1) * P], probs[:, c * P:(c + 1) * P], ident[:])
                    last.then_inc(p_turned, 1)
                if live(n, 1, STEPS):
                    pe.wait_ge(qk_split, n)
                    for h in range(GH):
                        for part, (queries, key) in enumerate(((qk_hi, qk_hi), (qk_hi, qk_lo), (qk_lo, qk_hi))):
                            last = nc.tensor.matmul(sp_[:, h * P:(h + 1) * P], queries[:, h * P:(h + 1) * P],
                                                    key[:, QC:QK], start=(part == 0), stop=(part == 2))
                    last.then_inc(scored, 1)
                if live(n, 2, STEPS):
                    pe.wait_ge(pt_copied, n - 1)
                    reached(pe, c_lo_done, n - 2)
                    gv = (g - 2) % NV
                    for par in range(2):
                        rows = slice(par * S, par * S + S)
                        for b in range(2):
                            last = nc.tensor.matmul(
                                pv[:, par, 0:2 * P].rearrange("p (c b q) -> p c b q", c=2, b=2)[:, :, b, :],
                                v_two[rows, gv, b, :],
                                probs_t[rows, :, b * S:(b + 1) * S], start=(b == 0), stop=True,
                                skip_group_check=True)
                    last.then_inc(weighed, 1)
                if live(n, 3, STEPS):
                    go = (g - 3) % GROUPS
                    pe.wait_ge(c_lo_done, n - 2)
                    if go == 0:
                        reached(pe, residual, i)
                    for h in range(GH):
                        cols = slice(h * P, (h + 1) * P)
                        for part, (cs, w) in enumerate(((c_hi, w_hi), (c_hi, w_lo), (c_lo, w_hi))):
                            last = nc.tensor.matmul(oacc[:], cs[:, (g - 3) % 2, cols], w[:, go, h, PC:WC],
                                                    start=(go == 0 and h == 0 and part == 0),
                                                    stop=(go == GROUPS - 1 and h == GH - 1 and part == 2))
                    last.then_inc(o_done, 1)

            schedule(pe, step, [(1, TILES - 1)])

        @block.vector
        def _(dve):
            def thresholds(g):
                def chain(ins_, count):
                    ins_.then_inc(c_chain, 1)
                    dve.wait_ge(c_chain, count)

                if g < TILES // 2:
                    for half in range(2):
                        dve.wait_ge(ffn_sem[half], (SUM_TILES * GROUPS + g) * 16 + 16)
                        nc.vector.tensor_reduce(c_peaks[:, 2 * g + half:2 * g + half + 1], ffn_in[:, half, :], AX.X,
                                                ALU.max, apply_absolute_value=True).then_inc(chunk_used, 1)
                if g == TILES // 2:
                    dve.wait_ge(chunk_used, BEFORE)
                    chain(nc.vector.tensor_reduce(c_peak[:], c_peaks[:], AX.X, ALU.max), 1)
                    nc.vector.tensor_scalar(c_peak[:], c_peak[:], TINY, None, ALU.max).then_inc(c_peaked, 1)
                if g == TILES // 2 + 1:
                    power, inverse, key_scale = xf[:, 2:3], xf[:, 5:6], xf[:, 6:7]
                    dve.wait_ge(c_all_peaked, 1)
                    chain(nc.vector.tensor_scalar(power.bitcast(I32), c_gpeak[:].bitcast(I32), EXP_BITS, None,
                                                  ALU.bitwise_and), 2)
                    chain(nc.vector.reciprocal(inverse, power), 3)
                    chain(nc.vector.tensor_tensor(key_scale, xf[:, 1:2], power, ALU.mult), 4)
                if g == 0:
                    dve.wait_ge(chunk_used, SUM_CHUNKS)
                    nc.vector.tensor_reduce(asum[:], abs_sums[:], AX.X, ALU.add).then_inc(summed, 1)
                if g == 1:
                    dve.wait_ge(all_summed, 1)
                    nc.vector.tensor_scalar(thr[:, 0:3], gsum[:], 1.0 / (HID * D), 0.7, ALU.mult,
                                            ALU.mult).then_inc(thr_done, 1)
                    dve.wait_ge(thr_done, 1)
                    nc.vector.tensor_scalar(thr[:, 3:6], thr[:, 0:3], -1.0, None, ALU.mult).then_inc(thr_done, 1)

            def quantise(matrix, unit, half):
                w, chunk = ffn_in[:, half, :], unit * 2 + BEFORE + half
                dve.wait_ge(ffn_sem[half], (unit + BEFORE // 2) * 16 + 16)
                dve.wait_ge(thr_done, 2)
                dve.wait_ge(chunk_used, chunk)
                nc.vector.tensor_scalar(below[:], w, thr[:, 3 + matrix:4 + matrix], None, ALU.is_lt
                                        ).then_inc(below_done, 1)
                dve.wait_ge(below_done, unit * 2 + half + 1)
                if not isinstance(unit, int) or unit > 0:
                    dve.wait_ge(q_stored[half], unit * 16)
                nc.vector.scalar_tensor_tensor(out=q_out[:, half, :], in0=w, scalar=thr[:, matrix:matrix + 1],
                                               in1=below[:], op0=ALU.is_gt,
                                               op1=ALU.subtract).then_inc(chunk_used, 1)

            def split_x(i):
                dve.wait_ge(xt_hi_done, i)
                nc.vector.scalar_tensor_tensor(out=xt_lo[:], in0=xt32[:], scalar=x_inv, in1=xt_hi[:],
                                               op0=ALU.mult, op1=ALU.subtract).then_inc(xt_split, 1)

            def qk_low(n):
                dve.wait_ge(qk_hi_done, n + 1)
                reached(dve, scored, n)
                nc.vector.tensor_tensor(qk_lo[:], rot[:], qk_hi[:], ALU.subtract).then_inc(qk_split, 1)

            def step(i, g, n, phase):
                if live(n, 0, STEPS):
                    dve.wait_ge(projected, n + 1)
                    reached(dve, rotated, n)
                    heads = GH + 1
                    src = pj[:, 0:QK].rearrange("p (h t) -> p h t", h=heads)
                    out = by_sin[:].rearrange("p (h t) -> p h t", h=heads)
                    nc.vector.tensor_tensor(by_cos[:].rearrange("p (h t) -> p h t", h=heads), src,
                                            cos[:, None, :].to_broadcast([P, heads, P]), ALU.mult)
                    for a, b in ((0, HALF), (HALF, 0)):
                        last = nc.vector.tensor_tensor(out[a:a + HALF], src[b:b + HALF],
                                                       sin[b:b + HALF, None, :].to_broadcast([HALF, heads, P]),
                                                       ALU.mult)
                    last.then_inc(roped, 1)
                if live(n, 1, STEPS):
                    dve.wait_ge(scored, n)
                    reached(dve, p_turned, n - 1)
                    for b in range(2):
                        rows = slice(b * S, (b + 1) * S)
                        last = nc.vector.scalar_tensor_tensor(
                            out=probs[rows, :].rearrange("p (h k) -> p h k", h=GH),
                            in0=sp_[rows, :].rearrange("p (h k) -> p h k", h=GH)[:, :, b * S:(b + 1) * S],
                            scalar=alpha[rows, :], in1=mask[rows, None, :].to_broadcast([S, GH, S]),
                            op0=ALU.mult, op1=ALU.add)
                    last.then_inc(masked, 1)
                    dve.wait_ge(masked, n)
                    reached(dve, exped, n - 1)
                    nc.vector.tensor_reduce(neg_max[:], probs[:].rearrange("p (h k) -> p h k", h=GH), AX.X,
                                            ALU.max, negate=True).then_inc(maxed, 1)
                if live(n, 2, STEPS):
                    dve.wait_ge(c_hi_done, n - 1)
                    reached(dve, o_done, n - 3)
                    nc.vector.tensor_tensor(
                        c_lo[:, g % 2, :].rearrange("p (c r q) -> p r c q", c=2, r=2),
                        pv[:, :, 0:2 * P].rearrange("p r (c q) -> p r c q", c=2),
                        c_hi[:, g % 2, :].rearrange("p (c r q) -> p r c q", c=2, r=2),
                        ALU.subtract).then_inc(c_lo_done, 1)
                if g == GROUPS - 1 and live(n, 0, STEPS - 1):
                    split_x(i + 1)
                if live(n, 1, STEPS):
                    dve.wait_ge(exped, n)
                    reached(dve, normed, n - 1)
                    nc.vector.reciprocal(rcp[:], psum_row[:]).then_inc(inverted, 1)
                if phase == "sum":
                    for half in range(2):
                        dve.wait_ge(ffn_sem[half], (i * GROUPS + g) * 16 + 16)
                        nc.vector.tensor_reduce(
                            abs_sums[:, bass.ds(i, 1), 2 * g + half:2 * g + half + 1].rearrange("p m c -> p (m c)"),
                            ffn_in[:, half, :], AX.X, ALU.add, apply_absolute_value=True).then_inc(chunk_used, 1)
                        if half == 0:
                            qk_low(n)
                quantising = phase == "quantise" and g < QUANT_STEPS
                if quantising:
                    quantise(g // ROW_TILES, quant_unit(i, g), 0)
                if live(n, 0, STEPS) and phase != "sum":
                    qk_low(n)
                if quantising:
                    quantise(g // ROW_TILES, quant_unit(i, g), 1)
                if phase == "threshold":
                    thresholds(g)
                if g == 2 and live(n, GROUPS, STEPS):
                    dve.wait_ge(o_done, i * GROUPS)
                    dve.wait_ge(xr_in, i * 16)
                    reached(dve, stored, (i - 1) * 16)
                    nc.vector.scalar_tensor_tensor(out=z[:], in0=oacc[:], scalar=beta, in1=x_res[:],
                                                   op0=ALU.mult, op1=ALU.add).then_inc(residual, 1)
                stats_step = GROUPS - 2 if live(n, 0, STEPS) else 2
                if g == stats_step and live(n, GROUPS, STEPS):
                    dve.wait_ge(residual, i)
                    nc.vector.bn_stats(stats[:], z[:]).then_inc(ln_chain, 1)
                    dve.wait_ge(ln_chain, i * 3 - 2)
                    nc.vector.memset(veps[:], EPS)
                    nc.vector.bn_aggr(mv[:], stats[:]).then_inc(ln_chain, 1)
                    dve.wait_ge(ln_chain, i * 3 - 1)
                    nc.vector.tensor_tensor(veps[:], veps[:], mv[:, 1:2], ALU.add).then_inc(ln_chain, 1)
                if g == stats_step + 1 and live(n, GROUPS, STEPS):
                    dve.wait_ge(rstd_done, i)
                    nc.vector.tensor_scalar(z[:], z[:], mv[:, 0:1], rstd[:], ALU.subtract,
                                            ALU.mult).then_inc(y_done, 1)

            schedule(dve, step, [SUMMING, QUANTISING])

        @block.scalar
        def _(act):
            def split_x(i):
                act.wait_ge(xt_in, i * 16)
                act.wait_ge(projected, i * GROUPS)
                nc.scalar.activation(xt_hi[:], xt32[:], ACT.Copy, scale=x_inv).then_inc(xt_hi_done, 1)

            def step(i, g, n, phase):
                if live(n, 1, STEPS):
                    act.wait_ge(rotated, n)
                    reached(act, scored, n - 1)
                    nc.scalar.activation(qk_hi[:], rot[:], ACT.Copy).then_inc(qk_hi_done, 1)
                if live(n, 2, STEPS):
                    act.wait_ge(p_turned, n - 1)
                    reached(act, weighed, n - 2)
                    nc.scalar.activation(probs_t[:].rearrange("p c q -> p (c q)"), tr[:],
                                         ACT.Copy).then_inc(pt_copied, 1)
                if live(n, 2, STEPS):
                    act.wait_ge(weighed, n - 1)
                    reached(act, o_done, n - 3)
                    nc.scalar.activation(
                        c_hi[:, g % 2, :].rearrange("p (c r q) -> p r c q", c=2, r=2),
                        pv[:, :, 0:2 * P].rearrange("p r (c q) -> p r c q", c=2), ACT.Copy).then_inc(c_hi_done, 1)
                if live(n, 0, STEPS):
                    act.wait_ge(roped, n + 1)
                    reached(act, weighed, n - NV + 1)
                    for b in range(2):
                        for half in range(2):
                            last = nc.scalar.activation(v_two[half * S:(half + 1) * S, g % NV, b, :],
                                                        pj[b * S:(b + 1) * S, QK:PC], ACT.Copy)
                    last.then_inc(v_copied, 1)
                if g == GROUPS - 1 and live(n, 0, STEPS - 1):
                    split_x(i + 1)
                if live(n, 1, STEPS):
                    act.wait_ge(maxed, n)
                    reached(act, inverted, n - 1)
                    for h in range(GH):
                        cols = slice(h * S, (h + 1) * S)
                        last = nc.scalar.activation(probs[:, cols], probs[:, cols], ACT.Exp,
                                                    bias=neg_max[:, h:h + 1], accum_out=psum_row[:, h:h + 1])
                    last.then_inc(exped, 1)

            schedule(act, step, [(1, TILES - 1)])

        @block.gpsimd
        def _(pool):
            def step(i, g, n, phase):
                if live(n, 0, STEPS):
                    pool.wait_ge(roped, n + 1)
                    reached(pool, qk_split, n)
                    nc.gpsimd.tensor_tensor(rot[:], by_cos[:], by_sin[:], ALU.add).then_inc(rotated, 1)
                if live(n, 1, STEPS):
                    pool.wait_ge(inverted, n)
                    nc.gpsimd.tensor_tensor(probs[:].rearrange("p (h k) -> p h k", h=GH),
                                            probs[:].rearrange("p (h k) -> p h k", h=GH),
                                            rcp[:, :, None].to_broadcast([P, GH, S]), ALU.mult).then_inc(normed, 1)
                if phase == "threshold" and g == 0:
                    pool.wait_ge(summed, 1)
                    nc.gpsimd.partition_all_reduce(gsum[:], asum[:], P, RADD).then_inc(all_summed, 1)
                if phase == "threshold" and g == TILES // 2:
                    pool.wait_ge(c_peaked, 1)
                    nc.gpsimd.partition_all_reduce(c_gpeak[:], c_peak[:], P, RMAX).then_inc(c_all_peaked, 1)
                stats_step = GROUPS - 2 if live(n, 0, STEPS) else 2
                if g == stats_step and live(n, GROUPS, STEPS):
                    pool.wait_ge(ln_chain, i * 3)
                    reached(pool, y_done, i - 1)
                    nc.gpsimd.tensor_tensor(rstd[:], veps[:], keep["neg_half"][:], ALU.pow
                                            ).then_inc(rstd_done, 1)

            schedule(pool, step, [SUMMING, (SUM_TILES + 1, TILES - 1)])


def cross_block(nc, ins, keep, x1_dram, q_dram, x2_dram):
    ident, wqk_hi, wqk_lo, xf = (keep[k] for k in ("ident", "wqk_hi", "wqk_lo", "xfac"))
    ffn_q, u, half_of = keep["ffn_q"], keep["u"], keep["half_of"]
    wq_scale, k_scale, c_inv = xf[:, 0:1], xf[:, 6:7], xf[:, 5:6]
    NT = D // P
    SLOTS = 2 * NT
    ALL = SLOTS * TILES
    NQ = SLOTS
    with ExitStack() as ctx:
        sb = lambda name, shape, dt: ctx.enter_context(nc.sbuf_tensor(name, shape, dt))
        ps = lambda name, shape, dt: ctx.enter_context(nc.psum_tensor(name, shape, dt))
        sem = lambda name: ctx.enter_context(nc.semaphore(name))
        x_raw, c_raw = keep["x_raw"], keep["c_raw"]
        x_res = sb("x_res2", [P, D], F32)
        c_t = sb("c_t", [P, 2, NT * XD], F32)
        xs = sb("xs", [P, 2, D], F16)
        cs = sb("cs", [P, 2, D], F16)
        e_k = sb("e_k", [P, 2, D], F32)
        p_q = sb("p_q", [P, NQ, D], F32)
        e_t = sb("e_t", [P, 2, NT, D], F32)
        p_t = sb("p_t", [P, 2, NT, D], F32)
        k_neg = sb("k_neg", [P, 1], F32)
        k_bias = sb("k_bias", [P, 1], F32)
        z_k = sb("z_k", [P, 2, NT], F32)
        r_k = sb("r_k", [P, NT], F32)
        q_max = sb("q_max", [P, XH], F32)
        q_sum = sb("q_sum", [P, XH], F32)
        q_rcp = sb("q_rcp", [P, XH], F32)
        g_t = sb("g_t", [XD, XH * XD], F32)
        m_sb = sb("m_sb", [P, NT, XD], F32)
        o_sb = sb("o_sb", [P, D], F32)
        sq = sb("sq", [P, D], F32)
        ss = sb("ss", [P, SLOTS], F32)
        rn = sb("rn", [P, SLOTS], F32)
        half8 = sb("half8", [P, SLOTS], F32)
        rn_wide = sb("rn_wide", [P, NT, P], F32)
        y1 = sb("y1", [P, D], F32)
        z = sb("z2", [P, D], F32)
        y = keep["x2_out"]
        stats = sb("stats2", [P, 6], F32)
        mv = sb("mv2", [P, 2], F32)
        veps = sb("veps2", [P, 1], F32)
        rstd = sb("rstd2", [P, 1], F32)
        kl = ps("kl", [P, D], F32)
        ql = ps("ql", [P, 2, D], F32)
        trk = ps("trk", [P, D], F32)
        trp = ps("trp", [P, D], F32)
        gm = ps("gm", [XD, D], F32)
        ob = ps("ob", [P, D], F32)
        nb = ps("nb", [P, D], F32)

        names = ("x_in", "c_in", "xr_in", "x_split", "c_split", "x_hi_done", "c_hi_done",
                 "k_logits", "q_logits", "k_turned", "q_turned", "g_done", "m_done", "o_done", "ss_done", "rb_done",
                 "k_maxed", "k_biased", "q_maxed", "q_shifted", "q_summed", "q_inverted", "m_scaled", "r_k_done",
                 "k_exped", "q_exped", "kt_copied", "qt_copied", "g_copied", "squared", "q_normed", "ss_copied",
                 "rn_done", "attended", "residual", "chain", "rstd_done", "y_done", "half8_set", "c_scaled",
                 "rn_raw", "first_in", "tables_in", "ternary_in")
        m = {name: sem("x_" + name) for name in names}
        m["stored"] = keep["x2_stored"]
        m["ct_in"] = [sem("x_ct_in0"), sem("x_ct_in1")]
        block = ctx.enter_context(nc.Block())
        rows_of = lambda a: a.rearrange("(t p) d -> t p d", p=P)

        def schedule(eng, slot):
            def tile(i, slots):
                for s in range(slots):
                    slot(i, s, i * SLOTS + s)

            tile(0, SLOTS)
            tile(1, SLOTS)
            with eng.Fori(2, TILES - 1) as i:
                tile(i, SLOTS)
            tile(TILES - 1, SLOTS)
            tile(TILES, SLOTS)
            tile(TILES + 1, SLOTS)

        @block.sync
        def _(sp):
            def rows_in(i):
                sp.wait_ge(m["x_split"], 2 * i)
                sp.dma_start(x_raw[:], rows_of(x1_dram)[i]).then_inc(m["x_in"], 16)
                sp.wait_ge(m["c_split"], 2 * i)
                sp.dma_start(c_raw[:], rows_of(ins["c_rows"])[i]).then_inc(m["c_in"], 16)

            def context_columns(i, b):
                reached(sp, m["g_done"], 2 * i + b - 1)
                sp.dma_start(c_t[:, b, :], ins["c_t"][i, :, b, :]).then_inc(m["ct_in"][b], 16)

            def residual_rows(i):
                reached(sp, m["residual"], i)
                sp.dma_start(x_res[:], rows_of(x1_dram)[i]).then_inc(m["xr_in"], 16)

            def store(i):
                sp.wait_ge(m["y_done"], i + 1)
                sp.dma_start(rows_of(x2_dram)[i], y[:]).then_inc(m["stored"], 16)

            def tile(i, first, second, last):
                if not first:
                    residual_rows(i - 1)
                context_columns(i, 1)
                if not last:
                    rows_in(i + 1)
                for matrix in range(3):
                    sp.dma_start(ffn_q[:, matrix, i, :].bitcast(I32), q_dram[matrix, i]).then_inc(m["ternary_in"], 16)
                if not (first or second):
                    store(i - 2)
                if not last:
                    context_columns(i + 1, 0)

            context_columns(0, 0)
            sp.wait_ge(keep["x1_stored"], 16 * TILES)
            sp.dma_start(keep["gate_s"][:], ins["gate_s"].to_broadcast([P, HID])).then_inc(m["tables_in"], 16)
            sp.dma_start(keep["up_s"][:], ins["up_s"].to_broadcast([P, HID])).then_inc(m["tables_in"], 16)
            sp.dma_start(keep["down_s"][:], ins["down_s"].to_broadcast([P, D])).then_inc(m["tables_in"], 16)
            tile(0, True, False, False)
            tile(1, False, True, False)
            with sp.Fori(2, TILES - 1) as i:
                tile(i, False, False, False)
            tile(TILES - 1, False, False, True)
            residual_rows(TILES - 1)
            store(TILES - 2)
            sp.wait_ge(m["stored"], 16 * (TILES - 1))
            sp.dma_start(keep["f_rows"][:], rows_of(x2_dram)[0]).then_inc(m["first_in"], 16)
            store(TILES - 1)
            sp.wait_ge(m["first_in"], 16)
            sp.wait_ge(m["tables_in"], 48)
            sp.wait_ge(m["ternary_in"], 16 * 3 * TILES)

        @block.tensor
        def _(pe):
            def attend(b, positions):
                for c in range(NT):
                    last = nc.tensor.matmul(ob[b * XD:(b + 1) * XD, positions], m_sb[:, c, :],
                                            p_t[:, b, c, positions], start=(c == 0), stop=(c == NT - 1))
                return last

            def slot(i, s, n):
                b, t = s // NT, s % NT
                bp = 1 - b
                seq = 2 * i + b
                if live(n, 0, ALL):
                    pe.wait_ge(m["c_split"], 2 * i + b + 1)
                    reached(pe, m["k_exped"], n)
                    for part, w in enumerate((wqk_hi, wqk_lo)):
                        last = nc.tensor.matmul(kl[:], w[:, 1, t * P:(t + 1) * P], cs[:, b, :],
                                                start=(part == 0), stop=(part == 1))
                    last.then_inc(m["k_logits"], 1)
                    pe.wait_ge(m["x_split"], 2 * i + b + 1)
                    reached(pe, m["q_shifted"], n - 1)
                    for part, w in enumerate((wqk_hi, wqk_lo)):
                        last = nc.tensor.matmul(ql[:, s % 2, :], xs[:, b, t * P:(t + 1) * P], w[:, 0, :],
                                                start=(part == 0), stop=(part == 1))
                    last.then_inc(m["q_logits"], 1)
                if live(n, 2, ALL):
                    bk, tk = ((s - 2) % SLOTS) // NT, (s - 2) % NT
                    pe.wait_ge(m["kt_copied"], n - 1)
                    if s == 2:
                        pe.wait_ge(m["ct_in"][0], 16 * i + 16)
                    elif s == 6:
                        pe.wait_ge(m["ct_in"][1], 16 * i + 16)
                    if tk == 0:
                        reached(pe, m["g_copied"], seq)
                    for j in range(NT):
                        last = nc.tensor.matmul(gm[:, tk * P:(tk + 1) * P], c_t[:, bk, j * XD:(j + 1) * XD],
                                                e_t[:, bk, j, tk * P:(tk + 1) * P],
                                                start=(j == 0), stop=(j == NT - 1))
                    if tk == NT - 1:
                        last.then_inc(m["g_done"], 1)
                if live(n, 1, ALL):
                    pe.wait_ge(m["k_exped"], n)
                    reached(pe, m["kt_copied"], n - 1)
                    for j in range(NT):
                        last = nc.tensor.transpose(trk[:, j * P:(j + 1) * P],
                                                   e_k[:, (s - 1) % 2, j * P:(j + 1) * P], ident[:])
                    last.then_inc(m["k_turned"], 1)
                if live(n, 3, ALL):
                    pe.wait_ge(m["q_normed"], n - 2)
                    reached(pe, m["qt_copied"], n - 3)
                    for j in range(NT):
                        last = nc.tensor.transpose(trp[:, j * P:(j + 1) * P],
                                                   p_q[:, (s - 3) % NQ, j * P:(j + 1) * P], ident[:])
                    last.then_inc(m["q_turned"], 1)
                if t == 2 and live(n, NT, ALL):
                    pe.wait_ge(m["g_copied"], seq)
                    if s == 2:
                        reached(pe, m["attended"], i - 1)
                    else:
                        reached(pe, m["ss_copied"], i)
                    for c in range(NT):
                        last = nc.tensor.matmul(nb[:, c * P:(c + 1) * P], g_t[:, c * P:(c + 1) * P],
                                                u[:, c * P:(c + 1) * P], start=True, stop=True)
                    last.then_inc(m["m_done"], 1)
                if t == 3 and live(n, NT, ALL):
                    pe.wait_ge(m["m_scaled"], seq)
                    pe.wait_ge(m["qt_copied"], n - NT + 1)
                    if bp == 0:
                        reached(pe, m["squared"], i)
                        attend(0, slice(0, D // 2))
                    else:
                        attend(1, slice(0, D)).then_inc(m["o_done"], 1)
                if s == 1 and live(n, SLOTS, ALL):
                    attend(0, slice(D // 2, D)).then_inc(m["o_done"], 1)
                if s == 5 and live(n, SLOTS, ALL):
                    pe.wait_ge(m["squared"], i)
                    pe.wait_ge(m["m_scaled"], 2 * i)
                    for j in range(NT):
                        last = nc.tensor.matmul(nb[:, 2 * j:2 * j + 2], sq[:, j * P:(j + 1) * P], half_of[:],
                                                start=True, stop=True)
                    last.then_inc(m["ss_done"], 1)
                if s == 0 and live(n, 2 * SLOTS, ALL):
                    pe.wait_ge(m["rn_done"], i - 1)
                    if live(n, SLOTS, ALL):
                        pe.wait_ge(m["m_scaled"], seq - 1)
                    for j in range(NT):
                        last = nc.tensor.matmul(nb[:, j * P:(j + 1) * P], rn_wide[:, j, :], ident[:],
                                                start=True, stop=True)
                    last.then_inc(m["rb_done"], 1)

            schedule(pe, slot)

        @block.vector
        def _(dve):
            nc.vector.memset(half8[:], -0.5).then_inc(m["half8_set"], 1)

            def slot(i, s, n):
                b, t = s // NT, s % NT
                if live(n, 0, ALL):
                    dve.wait_ge(m["k_logits"], n + 1)
                    reached(dve, m["k_biased"], n)
                    nc.vector.tensor_reduce(k_neg[:], kl[:], AX.X, ALU.max, negate=True).then_inc(m["k_maxed"], 1)
                if live(n, 2, ALL):
                    dve.wait_ge(m["q_summed"], n - 1)
                    reached(dve, m["q_normed"], n - 2)
                    nc.vector.reciprocal(q_rcp[:], q_sum[:]).then_inc(m["q_inverted"], 1)
                if live(n, 0, ALL):
                    dve.wait_ge(m["k_maxed"], n + 1)
                    reached(dve, m["k_exped"], n)
                    nc.vector.tensor_scalar(k_bias[:], k_neg[:], k_scale, None, ALU.mult).then_inc(m["k_biased"], 1)
                    dve.wait_ge(m["q_logits"], n + 1)
                    q3 = ql[:, s % 2, :].rearrange("p (h d) -> p h d", h=XH)
                    reached(dve, m["q_shifted"], n)
                    nc.vector.tensor_reduce(q_max[:], q3, AX.X, ALU.max).then_inc(m["q_maxed"], 1)
                    dve.wait_ge(m["q_maxed"], n + 1)
                    reached(dve, m["q_turned"], n - NQ + 1)
                    nc.vector.tensor_tensor(p_q[:, s % NQ, :].rearrange("p (h d) -> p h d", h=XH), q3,
                                            q_max[:, :, None].to_broadcast([P, XH, XD]),
                                            ALU.subtract).then_inc(m["q_shifted"], 1)
                if live(n, 1, ALL):
                    dve.wait_ge(m["q_exped"], n)
                    reached(dve, m["q_inverted"], n - 1)
                    nc.vector.tensor_reduce(q_sum[:], p_q[:, (s - 1) % NQ, :].rearrange("p (h d) -> p h d", h=XH),
                                            AX.X, ALU.add).then_inc(m["q_summed"], 1)
                if t == 2 and live(n, NT, ALL):
                    seq = 2 * i + b
                    reached(dve, m["m_scaled"], seq - 1)
                    nc.vector.reciprocal(r_k[:], z_k[:, 1 - b, :]).then_inc(m["r_k_done"], 1)
                    dve.wait_ge(m["m_done"], seq)
                    dve.wait_ge(m["r_k_done"], seq)
                    reached(dve, m["o_done"], seq - 1)
                    for h in range(2):
                        rows = slice(h * XD, (h + 1) * XD)
                        last = nc.vector.tensor_tensor(
                            m_sb[rows, :, :],
                            nb[rows, :].rearrange("p (c o) -> p c o", c=NT)[:, :, h * XD:(h + 1) * XD],
                            r_k[rows, :, None].to_broadcast([XD, NT, XD]), ALU.mult)
                    last.then_inc(m["m_scaled"], 1)
                if s == 5 and live(n, SLOTS, ALL):
                    dve.wait_ge(m["ss_done"], i)
                    reached(dve, m["rn_raw"], i - 1)
                    nc.vector.tensor_scalar(ss[:], nb[:, 0:SLOTS], 1e-24, None, ALU.max).then_inc(m["ss_copied"], 1)
                if s == 7 and live(n, SLOTS, ALL):
                    dve.wait_ge(m["rn_raw"], i)
                    reached(dve, m["rb_done"], i - 1)
                    nc.vector.tensor_copy(rn_wide[:].rearrange("p j (b o) -> p (j b) o", b=2),
                                          rn[:, :, None].to_broadcast([P, SLOTS, XD])).then_inc(m["rn_done"], 1)
                if s == 1 and live(n, 2 * SLOTS, ALL):
                    dve.wait_ge(m["rb_done"], i - 1)
                    reached(dve, m["residual"], i - 2)
                    nc.vector.scalar_tensor_tensor(out=y1[:], in0=o_sb[:], scalar=keep["g8"][:], in1=nb[:],
                                                   op0=ALU.mult, op1=ALU.mult).then_inc(m["attended"], 1)
                if s == 4 and live(n, 2 * SLOTS, ALL):
                    dve.wait_ge(m["residual"], i - 1)
                    nc.vector.bn_stats(stats[:], z[:]).then_inc(m["chain"], 1)
                if s == 5 and live(n, 2 * SLOTS, ALL):
                    dve.wait_ge(m["chain"], 3 * (i - 1) - 2)
                    nc.vector.memset(veps[:], EPS)
                    nc.vector.bn_aggr(mv[:], stats[:]).then_inc(m["chain"], 1)
                    dve.wait_ge(m["chain"], 3 * (i - 1) - 1)
                    nc.vector.tensor_tensor(veps[:], veps[:], mv[:, 1:2], ALU.add).then_inc(m["chain"], 1)
                if s == 7 and live(n, 2 * SLOTS, ALL):
                    dve.wait_ge(m["rstd_done"], i - 1)
                    reached(dve, m["stored"], 16 * (i - 2))
                    nc.vector.tensor_scalar(y[:], z[:], mv[:, 0:1], rstd[:], ALU.subtract,
                                            ALU.mult).then_inc(m["y_done"], 1)

            schedule(dve, slot)

        @block.scalar
        def _(act):
            def scale_context(i):
                reached(act, m["c_in"], 16 * i)
                nc.scalar.activation(c_raw[:], c_raw[:], ACT.Copy, scale=c_inv).then_inc(m["c_scaled"], 1)

            def split(i, b):
                rows = slice(b * XD, (b + 1) * XD)
                act.wait_ge(m["c_scaled"], i + 1)
                reached(act, m["k_logits"], i * SLOTS - (NT if b == 0 else 0))
                nc.scalar.activation(cs[rows, b, :], c_raw[rows, :], ACT.Copy).then_inc(m["c_hi_done"], 1)
                reached(act, m["x_in"], 16 * i)
                reached(act, m["q_logits"], i * SLOTS - (NT if b == 0 else 0))
                nc.scalar.activation(xs[rows, b, :], x_raw[rows, :], ACT.Copy).then_inc(m["x_hi_done"], 1)

            def slot(i, s, n):
                b, t = s // NT, s % NT
                if live(n, 4, ALL):
                    bq, tq = ((s - 4) % SLOTS) // NT, (s - 4) % NT
                    act.wait_ge(m["q_turned"], n - 3)
                    if tq == 0:
                        reached(act, m["o_done"], 2 * i + b - 2)
                    nc.scalar.activation(p_t[:, bq, :, tq * P:(tq + 1) * P],
                                         trp[:].rearrange("p (c q) -> p c q", c=NT),
                                         ACT.Copy).then_inc(m["qt_copied"], 1)
                if live(n, 0, ALL):
                    act.wait_ge(m["k_biased"], n + 1)
                    reached(act, m["k_turned"], n - 1)
                    if t == 0:
                        reached(act, m["r_k_done"], 2 * i + b - 1)
                    nc.scalar.activation(e_k[:, s % 2, :], kl[:], ACT.Exp, bias=k_bias[:], scale=k_scale,
                                         accum_out=z_k[:, b, t:t + 1]).then_inc(m["k_exped"], 1)
                if t == 1 and live(n, NT, ALL):
                    seq = 2 * i + b
                    act.wait_ge(m["g_done"], seq)
                    reached(act, m["m_done"], seq - 1)
                    nc.scalar.activation(g_t[:], gm[:], ACT.Copy).then_inc(m["g_copied"], 1)
                if live(n, 1, ALL):
                    bk, tk = ((s - 1) % SLOTS) // NT, (s - 1) % NT
                    act.wait_ge(m["k_turned"], n)
                    if tk == 0:
                        reached(act, m["g_done"], 2 * i + b - 1)
                    nc.scalar.activation(e_t[:, bk, :, tk * P:(tk + 1) * P],
                                         trk[:].rearrange("p (j r) -> p j r", j=NT),
                                         ACT.Copy).then_inc(m["kt_copied"], 1)
                if live(n, 0, ALL):
                    act.wait_ge(m["q_shifted"], n + 1)
                    nc.scalar.activation(p_q[:, s % NQ, :], p_q[:, s % NQ, :], ACT.Exp,
                                         scale=wq_scale).then_inc(m["q_exped"], 1)
                if s == 0 and live(n, 0, ALL):
                    split(i, 1)
                if s == 4 and live(n, SLOTS, ALL):
                    act.wait_ge(m["o_done"], 2 * i)
                    reached(act, m["attended"], i - 1)
                    reached(act, m["ss_done"], i - 1)
                    nc.scalar.activation(o_sb[:], ob[:], ACT.Identity, bias=keep["bo"][:])
                    nc.scalar.activation(sq[:], ob[:], ACT.Square, bias=keep["bo"][:]).then_inc(m["squared"], 1)
                if s == 5 and live(n, 0, ALL - SLOTS):
                    scale_context(i + 1)
                if s == 6 and live(n, 0, ALL - SLOTS):
                    split(i + 1, 0)

            scale_context(0)
            split(0, 0)
            schedule(act, slot)

        @block.gpsimd
        def _(pool):
            pool.wait_ge(m["half8_set"], 1)

            def split(i, b, normed):
                rows, other = slice(b * XD, (b + 1) * XD), slice((1 - b) * XD, (2 - b) * XD)
                reached(pool, m["q_normed"], normed)
                pool.wait_ge(m["c_hi_done"], 2 * i + b + 1)
                nc.gpsimd.tensor_tensor(cs[other, b, :], c_raw[rows, :], cs[rows, b, :],
                                        ALU.subtract).then_inc(m["c_split"], 1)
                pool.wait_ge(m["c_split"], 2 * i + b + 1)
                pool.wait_ge(m["x_hi_done"], 2 * i + b + 1)
                nc.gpsimd.tensor_tensor(xs[other, b, :], x_raw[rows, :], xs[rows, b, :],
                                        ALU.subtract).then_inc(m["x_split"], 1)
                pool.wait_ge(m["x_split"], 2 * i + b + 1)

            def slot(i, s, n):
                if live(n, 2, ALL):
                    pool.wait_ge(m["q_inverted"], n - 1)
                    p3 = p_q[:, (s - 2) % NQ, :].rearrange("p (h d) -> p h d", h=XH)
                    nc.gpsimd.tensor_tensor(p3, p3, q_rcp[:, :, None].to_broadcast([P, XH, XD]),
                                            ALU.mult).then_inc(m["q_normed"], 1)
                if s == 1 and live(n, 0, ALL):
                    split(i, 1, n - 1)
                if s == 6 and live(n, 0, ALL - SLOTS):
                    split(i + 1, 0, n - 1)
                if s == 2 and live(n, 2 * SLOTS, ALL):
                    pool.wait_ge(m["attended"], i - 1)
                    pool.wait_ge(m["xr_in"], 16 * (i - 1))
                    reached(pool, m["y_done"], i - 2)
                    nc.gpsimd.tensor_tensor(z[:], y1[:], x_res[:], ALU.add).then_inc(m["residual"], 1)
                if s == 5 and live(n, SLOTS, ALL):
                    pool.wait_ge(m["ss_copied"], i)
                    nc.gpsimd.tensor_tensor(rn[:], ss[:], half8[:], ALU.pow).then_inc(m["rn_raw"], 1)
                if s == 5 and live(n, 2 * SLOTS, ALL):
                    pool.wait_ge(m["chain"], 3 * (i - 1))
                    reached(pool, m["y_done"], i - 2)
                    nc.gpsimd.tensor_tensor(rstd[:], veps[:], keep["neg_half"][:], ALU.pow
                                            ).then_inc(m["rstd_done"], 1)

            split(0, 0, 0)
            schedule(pool, slot)


def ffn_block(nc, ins, keep, x2_dram, out):
    ident, ffn_q = keep["ident"], keep["ffn_q"]
    gate_s, up_s, down_s = keep["gate_s"], keep["up_s"], keep["down_s"]
    w_gate = ffn_q[:, 0].rearrange("p t c -> p (t c)").rearrange("p (k o) -> p k o", k=KT)
    w_up = ffn_q[:, 1].rearrange("p t c -> p (t c)").rearrange("p (k o) -> p k o", k=KT)
    w_down = ffn_q[:, 2].rearrange("p t c -> p (t c)").rearrange("p (k o) -> p k o", k=HT)
    with ExitStack() as ctx:
        sb = lambda name, shape, dt: ctx.enter_context(nc.sbuf_tensor(name, shape, dt))
        ps = lambda name, shape, dt: ctx.enter_context(nc.psum_tensor(name, shape, dt))
        x_in_sb = keep["f_rows"]
        x_res = sb("fx_res", [P, D], F32)
        xt_hi = sb("fxt_hi", [P, D], F16)
        xt_lo = sb("fxt_lo", [P, D], F16)
        gate = sb("gate", [P, 2, D], F32)
        up = sb("up", [P, 2, D], F32)
        silu = sb("silu", [P, 2, D], F32)
        h = sb("h", [P, HID], F32)
        hs = sb("hs", [P, HID], F32)
        ht_hi = sb("ht_hi", [P, 2, D], F16)
        ht_lo = sb("ht_lo", [P, 2, D], F16)
        peaks = sb("peaks", [P, FC], F32)
        peak = sb("fpeak", [P, 1], F32)
        power = sb("power", [P, 1], F32)
        inverse = sb("inverse", [P, 1], F32)
        powered = sb("powered", [P, 1], F32)
        d_sb = sb("d_sb", [P, D], F32)
        z = sb("fz", [P, D], F32)
        y = sb("fy", [P, D], F32)
        stats = sb("fstats", [P, 6], F32)
        mv = sb("fmv", [P, 2], F32)
        veps = sb("fveps", [P, 1], F32)
        rstd = sb("frstd", [P, 1], F32)
        tx = ps("tx", [P, D], F32)
        gp = ps("gp", [P, 2, D], F32)
        up_ps = ps("up_ps", [P, 2, D], F32)
        th = ps("th", [P, 2, D], F32)
        dn = ps("dn", [P, D], F32)
        names = ("x_in", "xr_in", "x_turned", "x_hi", "x_split", "gate_up", "gated", "upped", "silu_done", "h_done",
                 "maxed", "peaked", "clamped", "powered", "inverted", "h_scaled", "h_turned", "ht_hi", "ht_split",
                 "down", "unscaled", "residual", "chain", "rstd_done", "y_done", "stored")
        m = {name: ctx.enter_context(nc.semaphore("f_" + name)) for name in names}
        block = ctx.enter_context(nc.Block())
        rows_of = lambda a: a.rearrange("(t p) d -> t p d", p=P)

        def schedule(eng, tile):
            tile(0, True, False, False)
            tile(1, False, False, False)
            with eng.Fori(2, TILES - 1) as i:
                tile(i, False, False, False)
            tile(TILES - 1, False, True, False)
            tile(TILES, False, True, True)

        @block.sync
        def _(sp):
            def store(i):
                sp.wait_ge(m["y_done"], i + 1)
                sp.dma_start(rows_of(out)[i], y[:]).then_inc(m["stored"], 16)

            def residual_rows(i):
                reached(sp, m["residual"], i)
                sp.dma_start(x_res[:], rows_of(x2_dram)[i]).then_inc(m["xr_in"], 16)

            def next_rows(i):
                sp.wait_ge(m["x_turned"], i)
                sp.dma_start(x_in_sb[:], rows_of(x2_dram)[i]).then_inc(m["x_in"], 16)

            sp.wait_ge(keep["x2_stored"], 16 * TILES)
            next_rows(1)
            residual_rows(0)
            with sp.Fori(2, TILES) as i:
                next_rows(i)
                residual_rows(i - 1)
                store(i - 2)
            residual_rows(TILES - 1)
            store(TILES - 2)
            store(TILES - 1)
            sp.wait_ge(m["stored"], 16 * TILES)

        @block.tensor
        def _(pe):
            def turn_rows(i):
                reached(pe, m["x_in"], 16 * i)
                reached(pe, m["x_split"], i)
                for k in range(KT):
                    last = nc.tensor.transpose(tx[:, k * P:(k + 1) * P], x_in_sb[:, k * P:(k + 1) * P], ident[:])
                last.then_inc(m["x_turned"], 1)

            def tile(i, first, last_tile, past):
                def gate_and_up(c):
                    n = i * FC + c
                    if not (first and c < 2):
                        pe.wait_ge(m["upped"], n - 1)
                    for w, o in ((w_gate, gp), (w_up, up_ps)):
                        for k in range(KT):
                            for part, xs in enumerate((xt_hi, xt_lo)):
                                last = nc.tensor.matmul(o[:, c % 2, :], xs[:, k * P:(k + 1) * P],
                                                        w[:, k, c * D:(c + 1) * D],
                                                        start=(k == 0 and part == 0), stop=(k == KT - 1 and part == 1))
                    last.then_inc(m["gate_up"], 1)

                def turn_hidden(c):
                    n = (i - 1) * FC + c
                    if c == 0:
                        pe.wait_ge(m["h_scaled"], i)
                    reached(pe, m["ht_split"], n - 1)
                    for k in range(4):
                        last = nc.tensor.transpose(th[:, c % 2, k * P:(k + 1) * P],
                                                   hs[:, (c * 4 + k) * P:(c * 4 + k + 1) * P], ident[:])
                    last.then_inc(m["h_turned"], 1)

                def down(c):
                    n = (i - 1) * FC + c
                    pe.wait_ge(m["ht_split"], n + 1)
                    if c == 0:
                        reached(pe, m["unscaled"], i - 1)
                    for k in range(4):
                        for part, hx in enumerate((ht_hi, ht_lo)):
                            last = nc.tensor.matmul(dn[:], hx[:, c % 2, k * P:(k + 1) * P], w_down[:, c * 4 + k, :],
                                                    start=(c == 0 and k == 0 and part == 0),
                                                    stop=(c == FC - 1 and k == 3 and part == 1))
                    last.then_inc(m["down"], 1)

                if not past:
                    pe.wait_ge(m["x_split"], i + 1)
                    gate_and_up(0)
                    gate_and_up(1)
                if not first:
                    turn_hidden(0)
                    turn_hidden(1)
                if not past:
                    gate_and_up(2)
                if not first:
                    down(0)
                    turn_hidden(2)
                    down(1)
                    turn_hidden(3)
                if not past:
                    gate_and_up(3)
                if not last_tile:
                    turn_rows(i + 1)
                if not first:
                    down(2)
                    down(3)

            turn_rows(0)
            schedule(pe, tile)

        @block.vector
        def _(dve):
            def split_low(i):
                dve.wait_ge(m["x_hi"], i + 1)
                nc.vector.tensor_tensor(xt_lo[:], tx[:], xt_hi[:], ALU.subtract).then_inc(m["x_split"], 1)

            def tile(i, first, last_tile, past):
                def scale_chunk(c):
                    n = i * FC + c
                    dve.wait_ge(m["gate_up"], n + 1)
                    if not (first and c < 2):
                        dve.wait_ge(m["h_done"], n - 1)
                    nc.vector.tensor_tensor(gate[:, c % 2, :], gp[:, c % 2, :], gate_s[:, c * D:(c + 1) * D],
                                            ALU.mult).then_inc(m["gated"], 1)
                    nc.vector.tensor_tensor(up[:, c % 2, :], up_ps[:, c % 2, :], up_s[:, c * D:(c + 1) * D],
                                            ALU.mult).then_inc(m["upped"], 1)

                def chunk_peak(c):
                    dve.wait_ge(m["h_done"], i * FC + c + 1)
                    if c == 0:
                        reached(dve, m["peaked"], i)
                    nc.vector.tensor_reduce(peaks[:, c:c + 1], h[:, c * D:(c + 1) * D], AX.X, ALU.max,
                                            apply_absolute_value=True).then_inc(m["maxed"], 1)

                def hidden_low(c):
                    n = (i - 1) * FC + c
                    dve.wait_ge(m["ht_hi"], n + 1)
                    nc.vector.tensor_tensor(ht_lo[:, c % 2, :], th[:, c % 2, :], ht_hi[:, c % 2, :],
                                            ALU.subtract).then_inc(m["ht_split"], 1)

                if not past:
                    scale_chunk(0)
                    scale_chunk(1)
                    chunk_peak(0)
                if not first:
                    hidden_low(0)
                    hidden_low(1)
                if not past:
                    chunk_peak(1)
                    scale_chunk(2)
                if not first:
                    hidden_low(2)
                if not past:
                    chunk_peak(2)
                if not first:
                    hidden_low(3)
                if not past:
                    scale_chunk(3)
                if not last_tile:
                    split_low(i + 1)
                if not first:
                    dve.wait_ge(m["down"], i * FC)
                    nc.vector.scalar_tensor_tensor(out=d_sb[:], in0=dn[:], scalar=powered[:], in1=down_s[:],
                                                   op0=ALU.mult, op1=ALU.mult).then_inc(m["unscaled"], 1)
                if not past:
                    chunk_peak(3)
                    dve.wait_ge(m["maxed"], i * FC + FC)
                    nc.vector.tensor_reduce(peak[:], peaks[:], AX.X, ALU.max).then_inc(m["peaked"], 1)
                    dve.wait_ge(m["peaked"], i + 1)
                    nc.vector.tensor_scalar(power[:], peak[:], TINY, None, ALU.max).then_inc(m["clamped"], 1)
                    dve.wait_ge(m["clamped"], i + 1)
                    nc.vector.tensor_scalar(powered[:].bitcast(I32), power[:].bitcast(I32), EXP_BITS, None,
                                            ALU.bitwise_and).then_inc(m["powered"], 1)
                    dve.wait_ge(m["powered"], i + 1)
                    nc.vector.reciprocal(inverse[:], powered[:]).then_inc(m["inverted"], 1)
                if not first:
                    dve.wait_ge(m["unscaled"], i)
                    dve.wait_ge(m["xr_in"], 16 * i)
                    reached(dve, m["y_done"], i - 1)
                    nc.vector.tensor_tensor(z[:], d_sb[:], x_res[:], ALU.add).then_inc(m["residual"], 1)
                    dve.wait_ge(m["residual"], i)
                    nc.vector.bn_stats(stats[:], z[:]).then_inc(m["chain"], 1)
                    dve.wait_ge(m["chain"], 3 * i - 2)
                    nc.vector.memset(veps[:], EPS)
                    nc.vector.bn_aggr(mv[:], stats[:]).then_inc(m["chain"], 1)
                    dve.wait_ge(m["chain"], 3 * i - 1)
                    nc.vector.tensor_tensor(veps[:], veps[:], mv[:, 1:2], ALU.add).then_inc(m["chain"], 1)
                    dve.wait_ge(m["rstd_done"], i)
                    reached(dve, m["stored"], 16 * (i - 1))
                    nc.vector.tensor_scalar(y[:], z[:], mv[:, 0:1], rstd[:], ALU.subtract,
                                            ALU.mult).then_inc(m["y_done"], 1)

            split_low(0)
            schedule(dve, tile)

        @block.scalar
        def _(act):
            def split_high(i):
                act.wait_ge(m["x_turned"], i + 1)
                reached(act, m["gate_up"], i * FC)
                nc.scalar.activation(xt_hi[:], tx[:], ACT.Copy).then_inc(m["x_hi"], 1)

            def tile(i, first, last_tile, past):
                def silu_chunk(c):
                    n = i * FC + c
                    act.wait_ge(m["gated"], n + 1)
                    nc.scalar.activation(silu[:, c % 2, :], gate[:, c % 2, :], ACT.Silu).then_inc(m["silu_done"], 1)

                def hidden_high(c):
                    n = (i - 1) * FC + c
                    act.wait_ge(m["h_turned"], n + 1)
                    reached(act, m["down"], n - 1)
                    nc.scalar.activation(ht_hi[:, c % 2, :], th[:, c % 2, :], ACT.Copy).then_inc(m["ht_hi"], 1)

                if not past:
                    silu_chunk(0)
                    silu_chunk(1)
                if not first:
                    hidden_high(0)
                    hidden_high(1)
                if not past:
                    silu_chunk(2)
                if not first:
                    hidden_high(2)
                    hidden_high(3)
                if not last_tile:
                    split_high(i + 1)
                if not past:
                    silu_chunk(3)
                    act.wait_ge(m["inverted"], i + 1)
                    reached(act, m["h_turned"], i * FC)
                    nc.scalar.activation(hs[:], h[:], ACT.Copy, scale=inverse[:]).then_inc(m["h_scaled"], 1)

            split_high(0)
            schedule(act, tile)

        @block.gpsimd
        def _(pool):
            def tile(i, first, last_tile, past):
                def hidden(c):
                    n = i * FC + c
                    pool.wait_ge(m["silu_done"], n + 1)
                    pool.wait_ge(m["upped"], n + 1)
                    if c == 0:
                        reached(pool, m["h_scaled"], i)
                    nc.gpsimd.tensor_tensor(h[:, c * D:(c + 1) * D], silu[:, c % 2, :], up[:, c % 2, :],
                                            ALU.mult).then_inc(m["h_done"], 1)

                if not past:
                    hidden(0)
                    hidden(1)
                if not past:
                    hidden(2)
                    hidden(3)
                if not first:
                    pool.wait_ge(m["chain"], 3 * i)
                    reached(pool, m["y_done"], i - 1)
                    nc.gpsimd.tensor_tensor(rstd[:], veps[:], keep["neg_half"][:], ALU.pow
                                            ).then_inc(m["rstd_done"], 1)

            schedule(pool, tile)


def decoder_layer(nc, ins, out):
    x1_dram = nc.dram_tensor("x1_scratch", [TOK, D], F32, kind="Internal").ap()
    q_dram = nc.dram_tensor("ternary_scratch", [3, TILES, P, D], I32, kind="Internal").ap()
    x2_dram = nc.dram_tensor("x2_scratch", [TOK, D], F32, kind="Internal").ap()
    with ExitStack() as whole:
        keep = {}

        def hold(stack, name, shape, dt):
            keep[name] = stack.enter_context(nc.sbuf_tensor("keep_" + name, shape, dt))

        hold(whole, "ident", [P, P], F32)
        hold(whole, "neg_half", [P, 1], F32)
        hold(whole, "xfac", [P, 7], F32)
        hold(whole, "wqk_hi", [P, 2, XH * XD], F16)
        hold(whole, "wqk_lo", [P, 2, XH * XD], F16)
        hold(whole, "u", [XD, XH * XD], F32)
        hold(whole, "bo", [P, 1], F32)
        hold(whole, "g8", [P, 1], F32)
        hold(whole, "half_of", [P, 2], F32)
        keep["x1_stored"], keep["x2_stored"] = (whole.enter_context(nc.semaphore(name)) for name in (
            "x1_stored", "x2_stored"))
        hold(whole, "x1_out", [P, D], F32)
        hold(whole, "x_raw", [P, D], F32)
        hold(whole, "c_raw", [P, D], F32)
        with ExitStack() as first:
            hold(first, "fac", [P, 12], F32)
            hold(first, "cos", [P, HD], F32)
            hold(first, "sin", [P, HD], F32)
            hold(first, "mask", [P, S], F32)
            hold(first, "xt32", [P, KT * P], F32)
            hold(first, "xt_hi", [P, KT * P], F16)
            hold(first, "xt_lo", [P, KT * P], F16)
            hold(first, "weights", [P, GROUPS, KT, 2, WC], F16)
            prepare_block(nc, ins, keep)
            attention_block(nc, ins, keep, x1_dram, q_dram)
        hold(whole, "x2_out", [P, D], F32)
        hold(whole, "f_rows", [P, D], F32)
        hold(whole, "ffn_q", [P, 3, TILES, 2 * D], BF16)
        hold(whole, "gate_s", [P, HID], F32)
        hold(whole, "up_s", [P, HID], F32)
        hold(whole, "down_s", [P, D], F32)
        cross_block(nc, ins, keep, x1_dram, q_dram, x2_dram)
        ffn_block(nc, ins, keep, x2_dram, out)


def shape_constants():
    inv_freq = (1.0 / np.float32(10000.0) ** (np.arange(0, HD, 2, dtype=np.float32) / np.float32(HD)))
    freqs = np.arange(S, dtype=np.float32)[:, None] * inv_freq.astype(np.float32)
    emb = np.concatenate([freqs, freqs], axis=-1)
    sign = np.where(np.arange(HD) < HD // 2, 1.0, -1.0).astype(np.float32)
    cos, sin = np.cos(emb).astype(np.float32), np.sin(emb).astype(np.float32) * sign
    mask = np.where(np.tril(np.ones((S, S), bool)), 0.0, -3e38).astype(np.float32)
    half_of = np.repeat(np.eye(2, dtype=np.float32), XD, axis=0)
    two = lambda a: np.concatenate([a, a], axis=0)
    return {"cos": two(cos).T, "sin": two(sin).T, "mask": two(mask), "ident": np.eye(P, dtype=np.float32),
            "half_of": half_of}


def kernel(**inputs):
    import concourse.bacc as bacc
    from concourse.bass_utils import run_bass_kernel_spmd

    a = {k: np.asarray(v) for k, v in inputs.items()}

    def by_group(q, k, v, o, rows):
        return np.concatenate([q.reshape(KT, rows, GROUPS, QC).transpose(2, 0, 1, 3),
                               k.reshape(KT, rows, GROUPS, HD).transpose(2, 0, 1, 3),
                               v.reshape(KT, rows, GROUPS, HD).transpose(2, 0, 1, 3),
                               o.reshape(GROUPS, GH, rows, D)], axis=-1)

    def by_tile(w, tiles):
        flat = w.reshape(tiles, P, -1).transpose(1, 0, 2).reshape(P, TILES, -1)
        return flat.transpose(1, 0, 2)

    x = a["x"].reshape(TOK, D)
    c = a["ctx_4096"].reshape(TOK, D)
    columns = lambda m: m.reshape(TILES, P, KT, P).transpose(0, 3, 2, 1).reshape(TILES, P, KT * P)
    arrays = {
        "x_rows": x, "x_t": columns(x), "c_rows": c,
        "c_t": c.reshape(TILES, 2, S, KT, P).transpose(0, 4, 1, 3, 2).reshape(TILES, P, 2, KT * S),
        "w_int": by_group(*(a["L0_attn_qw_" + n] for n in "qkvo"), P),
        "scales": by_group(*(a["L0_attn_scales_" + n] for n in "qkvo"), 1).reshape(GROUPS * KT, WC),
        "wq_t": a["L0_xattn_Wq"].T, "wk_t": a["L0_xattn_Wk"].T,
        "wv": a["L0_xattn_Wv"].reshape(XH, XD, XD).transpose(1, 0, 2).reshape(XD, XH * XD),
        "wo": a["L0_xattn_Wo"].reshape(XD, XH, XD).transpose(2, 1, 0).reshape(XD, XH * XD),
        "bo": a["L0_xattn_bo"].reshape(XD, 1), "g": a["L0_xattn_g"].reshape(XD, 1),
        "ffn_w": np.stack([by_tile(a["L0_ffn_gate_w"].T, KT), by_tile(a["L0_ffn_up_w"].T, KT),
                           by_tile(a["L0_ffn_down_w"].T, HT)]),
        "gate_s": a["L0_ffn_gate_scale"].reshape(1, HID), "up_s": a["L0_ffn_up_scale"].reshape(1, HID),
        "down_s": a["L0_ffn_down_scale"].reshape(1, D),
        **shape_constants(),
    }
    nc = bacc.Bacc("TRN2", target_bir_lowering=False, num_devices=1)
    feeds, ins = {}, {}
    for name, array in arrays.items():
        array = np.ascontiguousarray(array)
        feeds[f"in_{name}"] = array
        ins[name] = nc.dram_tensor(f"in_{name}", array.shape, mybir.dt.from_np(array.dtype), kind="ExternalInput").ap()
    out = nc.dram_tensor("out", (TOK, D), F32, kind="ExternalOutput").ap()
    decoder_layer(nc, ins, out)
    result = run_bass_kernel_spmd(nc, [feeds], core_ids=[0])
    return np.asarray(result.results[0]["out"]).reshape(B, S, D)
```
